# Optimizing a Trainium2 kernel written in Bass

```python
import numpy as np
import jax
import jax.numpy as jnp

def _softmax(x, axis=-1):
    return jax.nn.softmax(x, axis=axis)

def _gelu(x):
    return jax.nn.gelu(x, approximate=True)

def _silu(x):
    return jax.nn.silu(x)

def _sigmoid(x):
    return jax.nn.sigmoid(x)

def _layernorm(x, axis=-1, eps=1e-05):
    m = jnp.mean(x, axis=axis, keepdims=True)
    v = jnp.var(x, axis=axis, keepdims=True)
    return (x - m) / jnp.sqrt(v + eps)

def _scatter_add(tgt, idx, src, axis=0):
    return tgt.at[idx].add(src)

def _segment_sum(src, seg, n):
    return jax.ops.segment_sum(src, seg, n)
kernel_name = 'mk_gnn_resnorm_d2_gnn_r32_086d25'

def setup_inputs(seed: int=0):
    np.random.seed(seed)
    _w = jnp.asarray

    def _rec_inputs():
        import jax
        import jax.numpy as jnp
        _gk = jax.random.key(seed)
        x = -0.0001126 + 1 * jax.random.normal(jax.random.fold_in(_gk, 1), (3125, 256), jnp.float32)
        _s = jax.random.randint(jax.random.fold_in(_gk, 2), (25000,), 0, 3125, jnp.int32)
        _d = jax.random.randint(jax.random.fold_in(_gk, 3), (25000,), 0, 3125, jnp.int32)
        _loop = jnp.arange(3125, dtype=jnp.int32)
        src = jnp.concatenate([_s, _d, _loop])
        dst = jnp.concatenate([_d, _s, _loop])
        _o = jnp.argsort(dst, stable=True)
        src = src[_o]
        dst = dst[_o]
        edge_attr_32 = jax.random.uniform(jax.random.fold_in(_gk, 11), (53125, 32), jnp.float32, 0.0, 1)
        edge_type_3 = jax.random.randint(jax.random.fold_in(_gk, 13), (53125,), 0, 3, jnp.int32)
        return (x, src, dst, edge_attr_32, edge_type_3)
    x, src, dst, edge_attr_32, edge_type_3 = _rec_inputs()

    def _L0_gnn_setup():
        import jax, jax.numpy as jnp
        import numpy as np
        import math
        N = 30000
        E = 18750
        IN_DIM = 256
        HID = 64
        EMB = 64
        HEADS = 4
        EPS = 1e-05

        def _glorot(key, shape):
            fan_in, fan_out = (shape[0], shape[1])
            lim = math.sqrt(6.0 / (fan_in + fan_out))
            return jax.random.uniform(key, shape, jnp.float32, -lim, lim)

        def transformer_conv(x, edge_index, wq, bq, wk, bk, wv, bv, ws, bs, heads, out_ch):
            n = x.shape[0]
            q = (x @ wq + bq).reshape(n, heads, out_ch)
            k = (x @ wk + bk).reshape(n, heads, out_ch)
            v = (x @ wv + bv).reshape(n, heads, out_ch)
            src, dst = (edge_index[0], edge_index[1])
            qi, kj, vj = (q[dst], k[src], v[src])
            alpha = jnp.sum(qi * kj, axis=-1) / math.sqrt(out_ch)
            amax = jax.lax.stop_gradient(jax.ops.segment_max(alpha, dst, num_segments=n))
            ex = jnp.exp(alpha - amax[dst])
            denom = jax.ops.segment_sum(ex, dst, num_segments=n)
            alpha = ex / denom[dst]
            out = jax.ops.segment_sum(vj * alpha[..., None], dst, num_segments=n)
            out = out.reshape(n, heads * out_ch)
            return out + x @ ws + bs

        def batch_norm(x, gamma, beta):
            mean = jnp.mean(x, axis=0)
            var = jnp.mean(jnp.square(x - mean), axis=0)
            return (x - mean) * jax.lax.rsqrt(var + EPS) * gamma + beta

        def leaky_relu(x):
            return jnp.where(x >= 0, x, 0.1 * x)
        key = jax.random.key(seed)
        ks = jax.random.split(key, 24)
        inp = {'x': jax.random.normal(ks[0], (N, IN_DIM), jnp.float32), 'edge_index': jax.random.randint(ks[1], (2, E), 0, N, jnp.int64)}
        w1 = HID * HEADS
        inp.update({'w1q': _glorot(ks[2], (IN_DIM, w1)), 'b1q': jnp.zeros((w1,), jnp.float32), 'w1k': _glorot(ks[3], (IN_DIM, w1)), 'b1k': jnp.zeros((w1,), jnp.float32), 'w1v': _glorot(ks[4], (IN_DIM, w1)), 'b1v': jnp.zeros((w1,), jnp.float32), 'w1s': _glorot(ks[5], (IN_DIM, w1)), 'b1s': jnp.zeros((w1,), jnp.float32), 'g1': jnp.ones((w1,), jnp.float32), 'be1': jnp.zeros((w1,), jnp.float32)})
        w2 = EMB * HEADS
        inp.update({'w2q': _glorot(ks[6], (w1, w2)), 'b2q': jnp.zeros((w2,), jnp.float32), 'w2k': _glorot(ks[7], (w1, w2)), 'b2k': jnp.zeros((w2,), jnp.float32), 'w2v': _glorot(ks[8], (w1, w2)), 'b2v': jnp.zeros((w2,), jnp.float32), 'w2s': _glorot(ks[9], (w1, w2)), 'b2s': jnp.zeros((w2,), jnp.float32), 'g2': jnp.ones((w2,), jnp.float32), 'be2': jnp.zeros((w2,), jnp.float32)})
        return inp
    _L0_gnn_all = _L0_gnn_setup()
    _L0_gnn_in = {k: v for k, v in _L0_gnn_all.items() if k in ('w1q', 'b1q', 'w1k', 'b1k', 'w1v', 'b1v', 'w1s', 'b1s', 'g1', 'be1', 'w2q', 'b2q', 'w2k', 'b2k', 'w2v', 'b2v', 'w2s', 'b2s', 'g2', 'be2')}
    del _L0_gnn_all

    def _L1_gnn_setup():
        import jax, jax.numpy as jnp
        import numpy as np
        N_NODES = 50000
        N_EDGES = 25000
        D = 256
        N_REL = 3
        N_LAYERS = 3
        N_DISTS = 32

        def _rgcn_layer(x, src, dst, edge_type, edge_attr, W, root, bias, nn_w, nn_b):
            n = x.shape[0]
            edge_w = edge_attr @ nn_w.T + nn_b
            msg = jax.nn.relu(x[src] * edge_w)
            out = x @ root + bias
            for r in range(N_REL):
                mask = edge_type == r
                m = jnp.where(mask[:, None], msg, 0.0)
                s = jax.ops.segment_sum(m, dst, num_segments=n)
                cnt = jax.ops.segment_sum(mask.astype(x.dtype), dst, num_segments=n)
                mean = s / jnp.maximum(cnt, 1.0)[:, None]
                out = out + mean @ W[r]
            return out
        key = jax.random.key(seed)
        ks = jax.random.split(key, 10)
        x = jax.random.normal(ks[0], (N_NODES, D), dtype=jnp.float32)
        edge_index = jax.random.randint(ks[1], (2, N_EDGES), 0, N_NODES)
        edge_type = jax.random.randint(ks[2], (N_EDGES,), 0, N_REL)
        edge_attr = jax.random.uniform(ks[3], (N_EDGES, N_DISTS), dtype=jnp.float32)
        W = jax.random.normal(ks[4], (N_LAYERS, N_REL, D, D), dtype=jnp.float32) * (1.0 / np.sqrt(D))
        root = jax.random.normal(ks[5], (N_LAYERS, D, D), dtype=jnp.float32) * (1.0 / np.sqrt(D))
        bias = jnp.zeros((N_LAYERS, D), dtype=jnp.float32)
        nn_w = jax.random.normal(ks[6], (D, N_DISTS), dtype=jnp.float32) * (1.0 / np.sqrt(N_DISTS))
        nn_b = jnp.zeros((D,), dtype=jnp.float32)
        return {'x': x, 'edge_index': edge_index, 'edge_type': edge_type, 'edge_attr': edge_attr, 'W': W, 'root': root, 'bias': bias, 'nn_w': nn_w, 'nn_b': nn_b}
    _L1_gnn_all = _L1_gnn_setup()
    _L1_gnn_in = {k: v for k, v in _L1_gnn_all.items() if k in ('W', 'root', 'bias', 'nn_w', 'nn_b')}
    del _L1_gnn_all
    return {'x': x, 'src': src, 'dst': dst, 'edge_attr_32': edge_attr_32, 'edge_type_3': edge_type_3, 'L0_gnn_w1q': _L0_gnn_in['w1q'], 'L0_gnn_b1q': _L0_gnn_in['b1q'], 'L0_gnn_w1k': _L0_gnn_in['w1k'], 'L0_gnn_b1k': _L0_gnn_in['b1k'], 'L0_gnn_w1v': _L0_gnn_in['w1v'], 'L0_gnn_b1v': _L0_gnn_in['b1v'], 'L0_gnn_w1s': _L0_gnn_in['w1s'], 'L0_gnn_b1s': _L0_gnn_in['b1s'], 'L0_gnn_g1': _L0_gnn_in['g1'], 'L0_gnn_be1': _L0_gnn_in['be1'], 'L0_gnn_w2q': _L0_gnn_in['w2q'], 'L0_gnn_b2q': _L0_gnn_in['b2q'], 'L0_gnn_w2k': _L0_gnn_in['w2k'], 'L0_gnn_b2k': _L0_gnn_in['b2k'], 'L0_gnn_w2v': _L0_gnn_in['w2v'], 'L0_gnn_b2v': _L0_gnn_in['b2v'], 'L0_gnn_w2s': _L0_gnn_in['w2s'], 'L0_gnn_b2s': _L0_gnn_in['b2s'], 'L0_gnn_g2': _L0_gnn_in['g2'], 'L0_gnn_be2': _L0_gnn_in['be2'], 'L1_gnn_W': _L1_gnn_in['W'], 'L1_gnn_root': _L1_gnn_in['root'], 'L1_gnn_bias': _L1_gnn_in['bias'], 'L1_gnn_nn_w': _L1_gnn_in['nn_w'], 'L1_gnn_nn_b': _L1_gnn_in['nn_b']}

def reference(x, src, dst, edge_attr_32, edge_type_3, L0_gnn_w1q, L0_gnn_b1q, L0_gnn_w1k, L0_gnn_b1k, L0_gnn_w1v, L0_gnn_b1v, L0_gnn_w1s, L0_gnn_b1s, L0_gnn_g1, L0_gnn_be1, L0_gnn_w2q, L0_gnn_b2q, L0_gnn_w2k, L0_gnn_b2k, L0_gnn_w2v, L0_gnn_b2v, L0_gnn_w2s, L0_gnn_b2s, L0_gnn_g2, L0_gnn_be2, L1_gnn_W, L1_gnn_root, L1_gnn_bias, L1_gnn_nn_w, L1_gnn_nn_b):
    import jax
    import jax.numpy as jnp

    def _L0_gnn_ref(x, edge_index, w1q, b1q, w1k, b1k, w1v, b1v, w1s, b1s, g1, be1, w2q, b2q, w2k, b2k, w2v, b2v, w2s, b2s, g2, be2):
        import jax, jax.numpy as jnp
        import numpy as np
        import math
        N = 30000
        E = 18750
        IN_DIM = 256
        HID = 64
        EMB = 64
        HEADS = 4
        EPS = 1e-05

        def _glorot(key, shape):
            fan_in, fan_out = (shape[0], shape[1])
            lim = math.sqrt(6.0 / (fan_in + fan_out))
            return jax.random.uniform(key, shape, jnp.float32, -lim, lim)

        def transformer_conv(x, edge_index, wq, bq, wk, bk, wv, bv, ws, bs, heads, out_ch):
            n = x.shape[0]
            q = (x @ wq + bq).reshape(n, heads, out_ch)
            k = (x @ wk + bk).reshape(n, heads, out_ch)
            v = (x @ wv + bv).reshape(n, heads, out_ch)
            src, dst = (edge_index[0], edge_index[1])
            qi, kj, vj = (q[dst], k[src], v[src])
            alpha = jnp.sum(qi * kj, axis=-1) / math.sqrt(out_ch)
            amax = jax.lax.stop_gradient(jax.ops.segment_max(alpha, dst, num_segments=n))
            ex = jnp.exp(alpha - amax[dst])
            denom = jax.ops.segment_sum(ex, dst, num_segments=n)
            alpha = ex / denom[dst]
            out = jax.ops.segment_sum(vj * alpha[..., None], dst, num_segments=n)
            out = out.reshape(n, heads * out_ch)
            return out + x @ ws + bs

        def batch_norm(x, gamma, beta):
            mean = jnp.mean(x, axis=0)
            var = jnp.mean(jnp.square(x - mean), axis=0)
            return (x - mean) * jax.lax.rsqrt(var + EPS) * gamma + beta

        def leaky_relu(x):
            return jnp.where(x >= 0, x, 0.1 * x)
        h = transformer_conv(x, edge_index, w1q, b1q, w1k, b1k, w1v, b1v, w1s, b1s, HEADS, HID)
        h = leaky_relu(batch_norm(h, g1, be1))
        h = transformer_conv(h, edge_index, w2q, b2q, w2k, b2k, w2v, b2v, w2s, b2s, HEADS, EMB)
        h = leaky_relu(batch_norm(h, g2, be2))
        return h

    def _L1_gnn_ref(x, edge_index, edge_type, edge_attr, W, root, bias, nn_w, nn_b):
        import jax, jax.numpy as jnp
        import numpy as np
        N_NODES = 50000
        N_EDGES = 25000
        D = 256
        N_REL = 3
        N_LAYERS = 3
        N_DISTS = 32

        def _rgcn_layer(x, src, dst, edge_type, edge_attr, W, root, bias, nn_w, nn_b):
            n = x.shape[0]
            edge_w = edge_attr @ nn_w.T + nn_b
            msg = jax.nn.relu(x[src] * edge_w)
            out = x @ root + bias
            for r in range(N_REL):
                mask = edge_type == r
                m = jnp.where(mask[:, None], msg, 0.0)
                s = jax.ops.segment_sum(m, dst, num_segments=n)
                cnt = jax.ops.segment_sum(mask.astype(x.dtype), dst, num_segments=n)
                mean = s / jnp.maximum(cnt, 1.0)[:, None]
                out = out + mean @ W[r]
            return out
        src, dst = (edge_index[0], edge_index[1])
        h = x
        for l in range(N_LAYERS):
            h = _rgcn_layer(h, src, dst, edge_type, edge_attr, W[l], root[l], bias[l], nn_w, nn_b)
        return h
    edge_index = jnp.stack([src, dst])
    x = _layernorm(x + _L0_gnn_ref(x, edge_index, L0_gnn_w1q, L0_gnn_b1q, L0_gnn_w1k, L0_gnn_b1k, L0_gnn_w1v, L0_gnn_b1v, L0_gnn_w1s, L0_gnn_b1s, L0_gnn_g1, L0_gnn_be1, L0_gnn_w2q, L0_gnn_b2q, L0_gnn_w2k, L0_gnn_b2k, L0_gnn_w2v, L0_gnn_b2v, L0_gnn_w2s, L0_gnn_b2s, L0_gnn_g2, L0_gnn_be2), axis=-1)
    x = _layernorm(x + _L1_gnn_ref(x, edge_index, edge_type_3, edge_attr_32, L1_gnn_W, L1_gnn_root, L1_gnn_bias, L1_gnn_nn_w, L1_gnn_nn_b), axis=-1)
    return x

_drawn_inputs = setup_inputs


def setup_inputs(seed=0):
    import zlib

    import numpy as np

    out = dict(_drawn_inputs(seed))
    spreads = {'L0_gnn_b1q': (0.0, 0.471),
     'L0_gnn_b1k': (0.0, 0.8),
     'L0_gnn_b1v': (0.0, 0.8),
     'L0_gnn_b1s': (0.0, 0.8),
     'L0_gnn_g1': (1.0, 0.2),
     'L0_gnn_be1': (0.0, 0.1),
     'L0_gnn_b2q': (0.0, 0.8),
     'L0_gnn_b2k': (0.0, 0.8),
     'L0_gnn_b2v': (0.0, 0.8),
     'L0_gnn_b2s': (0.0, 0.8),
     'L0_gnn_g2': (1.0, 0.2),
     'L0_gnn_be2': (0.0, 0.1),
     'L1_gnn_bias': (0.0, 0.1),
     'L1_gnn_nn_b': (0.0, 0.1)}
    factors = {}
    for name, (base, spread) in spreads.items():
        noise = np.random.default_rng([zlib.crc32(name.encode()), seed]).standard_normal(out[name].shape)
        drawn = base * np.exp(spread * noise) if base else spread * noise
        out[name] = jnp.asarray(drawn.astype(out[name].dtype))
    for name, factor in factors.items():
        out[name] = (out[name] * factor).astype(out[name].dtype)
    return out
```

```python
from contextlib import ExitStack

import concourse.bass as bass
from concourse import mybir

ALU = mybir.AluOpType
ACT = mybir.ActivationFunctionType
AX = mybir.AxisListType
F32 = mybir.dt.float32
BF16 = mybir.dt.bfloat16
I32 = mybir.dt.int32

P = 128
N, D = 3125, 256
E = 53125
HEADS, HD = 4, 64
VW = HD + 1
ND = 32
NREL = 3
W = 32
NW = -(-N // W)
NT = -(-N // P)
WPT = P // W
NWP = NT * WPT
NP = NT * P
NTAIL = N - (NT - 1) * P
T = (E + NW * (P - 1)) // P
U = 8
HALF = U // 2
TRIPS = T // U
EP, EJ = 125, 425
CG = 5
G = EJ // CG
GU = 5
GTRIPS = G // GU
REC = 36
C_SRC, C_DL, C_SEG = ND, ND + 1, ND + 2
SEG = NREL * W
KVW = D + HEADS * VW
UC = 64
NUC = T // UC
NB = -(-NP // 512)
EPS = 1e-5
SCALE = HD ** -0.5
MASKED, FLOOR, RESTART, KEEP = -1e30, -1e29, -2e30, 1e30
assert EP * EJ == E and T % U == 0 and T == TRIPS * U and G == GTRIPS * GU and NWP > NW and T % P == 0


class Count:

    def __init__(self, sem):
        self.sem, self.n = sem, 0

    def inc(self, instruction, by=1):
        instruction.then_inc(self.sem, by)
        self.n += by
        return self.n


def live(trip, u, lag):
    return not isinstance(trip, int) or 0 <= trip * U + u - lag < T


def run_steps(eng, lag, step):
    for u in range(U):
        step(0, u)
    with eng.Fori(1, TRIPS) as trip:
        for u in range(U):
            step(trip, u)
    for u in range(lag):
        step(TRIPS, u)


def tile_of(trip, u, lag):
    return trip * U + (u - lag), (u - lag) % U, trip if u >= lag else trip - 1


def wait_freed(eng, sem, value):
    if not isinstance(value, int) or value > 0:
        eng.wait_ge(sem, value)


def build(nc, a, out):
    ctx = ExitStack()
    with ctx:
        def sb(name, shape, dt):
            return ctx.enter_context(nc.sbuf_tensor(name, shape, dt))

        def sem(name):
            return ctx.enter_context(nc.semaphore(name))

        def dram(name, shape, dt=F32):
            return nc.dram_tensor(name, shape, dt, kind="Internal").ap()

        rec_d = dram("edge_records", (P * T, REC))
        eat_d = dram("edge_attr_T", (TRIPS, P, U // 4 * P))
        dlt_d = dram("node_in_window_T", (T, P), BF16)
        kv_d = [dram(f"kv_rows{l}", (NP, KVW)) for l in range(2)]
        h_d = [dram(f"h_rows{l}", (NP, D)) for l in range(3)]

        ident = sb("ident", [P, P], F32)
        before = sb("before", [EP, EP], BF16)
        ones_b = sb("ones_b", [P, P], BF16)
        ones_f = sb("ones_f", [P, 1], F32)
        zeros_b = sb("zeros_b", [EP, CG * NW], BF16)
        iota_w = sb("iota_w", [P, NW], F32)
        ones_w = sb("ones_w", [P, NW], F32)
        iota_seg = sb("iota_seg", [P, SEG], F32)
        part_i = sb("part_i", [P, 1], I32)
        part_m = sb("part_m", [P, 1], I32)
        part_dl = sb("part_dl", [P, 1], F32)

        src_i = sb("src_i", [P, T], I32)
        seg_f = sb("seg_f", [P, T], F32)
        dl_f = sb("dl_f", [P, T], F32)
        restart = sb("restart", [P, T], F32)
        win_i = sb("win_i", [1, T], I32)

        wts = sb("wts", [P, 2, 4, 2, D], F32)
        bias_q = sb("bias_q", [P, 2, 2], F32)
        bias_s = sb("bias_s", [P, 2, 2], F32)
        gamma = sb("gamma", [P, 2, 2], F32)
        beta = sb("beta", [P, 2, 2], F32)
        bias_kv = sb("bias_kv", [P, 2, 2, D], F32)
        bias_r = sb("bias_r", [P, 3, D], F32)
        nnw = sb("nnw", [P, 2, ND], F32)
        nnwt = sb("nnwt", [ND + 1, D], F32)

        ht = sb("ht", [P, 2, NP], F32)
        REGION = 2 * NP + NWP * P + NWP * VW
        region = sb("region", [P, REGION], F32)
        at = 0
        st = region[:, 0:2 * NP].rearrange("p (c n) -> p c n", c=2)
        qblk = region[:, 2 * NP:2 * NP + NWP * P].rearrange("p (w c m) -> p w c m", c=2, m=2 * W)
        at = 2 * NP + NWP * P
        acc = region[:, at:at + NWP * VW].rearrange("p (w v) -> p w v", v=VW)
        chunk = region[:, at:at + 2 * UC * REC].rearrange("p (b t r) -> p b t r", b=2, r=REC)
        x1 = region[:, at:at + NT * D].rearrange("p (i f) -> p i f", f=D)
        racc = region[:, 0:2 * NREL * NP].rearrange("p (s n) -> p s n", n=NP)
        assert 2 * NREL * NP <= at and 2 * UC * REC <= NWP * VW and NT * D <= NWP * VW
        gring = sb("gring", [P, U, KVW], F32)
        xr = sb("xr", [P, 3, D], F32)
        rows = sb("rows", [P, 2 * KVW], F32)
        kvrow = rows[:, :].rearrange("p (s k) -> p s k", s=2)
        orow = rows[:, 0:4 * D].rearrange("p (s f) -> p s f", s=4)
        assert 4 * D <= 2 * KVW
        gidx = sb("gidx", [P, 2, HALF], I32)

        sort_at = [at]

        def sort_space(n, dt=F32):
            space = region[0:EP, sort_at[0]:sort_at[0] + n]
            sort_at[0] += n
            return space if dt == F32 else space.bitcast(dt)

        dst_e, typ_e, src_e, int_e = (sort_space(EJ, I32) for _ in range(4))
        row_e = sort_space(EJ, I32)
        win_f = sort_space(EJ)
        meta = sort_space(EJ * (REC - ND)).rearrange("p (j r) -> p j r", r=REC - ND)
        onehot_w = sort_space(GU * CG * NW // 2, BF16).rearrange("p (g c w) -> p g c w", g=GU, c=CG)
        rank = sort_space(CG * NW).rearrange("p (c w) -> p c w", c=CG)
        assert sort_at[0] <= REGION
        run_tot = sb("run_tot", [P, NW], F32)
        cnt_w = sb("cnt_w", [P, NW], F32)
        tiles_i = sb("tiles_i", [P, NW], I32)
        tiles_f = sb("tiles_f", [P, NW], F32)
        tend = sb("tend", [P, NW], F32)
        tend_c = sb("tend_c", [NW, 1], F32)
        pos_f = sb("pos_f", [EP, CG], F32)
        pos_i = sb("pos_i", [EP, CG], I32)
        pos_lo = sb("pos_lo", [EP, CG], I32)
        pos_hi = sb("pos_hi", [EP, CG], I32)
        blank = gring[:, 0:5, :].rearrange("p u k -> p (u k)")[:, 0:UC * REC].rearrange("p (t r) -> p t r", r=REC)
        iota_t = gring[0:NW, 5, 0:T]
        tile_w = ht[:, 0, 0:T]
        ended = ht[0:NW, 1, 0:T // 2].bitcast(BF16)
        eat_out = ht[:, 0, 0:8 * P].rearrange("p (s m) -> p s m", s=2)
        attrs = ht[:, :, 8 * P:8 * P + UC * ND]
        dlt_out = ht[:, 1, 0:T // 2].bitcast(BF16).rearrange("p (q e) -> p q e", e=P)

        rings = sb("rings", [P, 2 * 2 * P + U * 4 * W + HALF * P + 2 * HALF * P], F32)
        ring_at = [0]

        def ring_space(n):
            space = rings[:, ring_at[0]:ring_at[0] + n]
            ring_at[0] += n
            return space

        kt = ring_space(4 * P).rearrange("p (s m) -> p s m", s=2)
        qs = ring_space(U * 4 * W).rearrange("p (s c m) -> p s c m", s=U, c=2)
        dlb = ring_space(HALF * P).bitcast(BF16).rearrange("p (h m) -> p h m", h=2)
        mask = ring_space(2 * HALF * P).rearrange("p (h t e) -> p h t e", h=2, t=HALF)
        stage = rings[0:EP, 0:GU * CG * REC].rearrange("p (g c r) -> p g c r", g=GU, c=CG)
        stage_row = rings[0:EP, GU * CG * REC:GU * CG * (REC + 1)].bitcast(I32).rearrange("p (g c) -> p g c", g=GU)
        ring_at = [0]
        eat = ring_space(2 * 4 * P)[0:ND + 1, :].rearrange("p (h t e) -> p h t e", h=2, t=4)
        oh = ring_space(2 * HALF * SEG).rearrange("p (h t s) -> p h t s", h=2, t=HALF)
        prod = ring_space(2 * D).rearrange("p (s f) -> p s f", s=2)
        msg = ring_space(2 * D).rearrange("p (s f) -> p s f", s=2)
        xs = sb("xs", [P, 2, P + 1], F32)
        top = sb("top", [P, U], F32)
        ntop = sb("ntop", [P, 4], F32)
        et = sb("et", [P, 4, P + 1], F32)
        es = sb("es", [P, 2, P], F32)
        rden = sb("rden", [P, NWP], F32)
        stats = sb("stats", [P, 2, NB, 6], F32)
        mv = sb("mv", [P, 2, 2], F32)
        bn_t = sb("bn_t", [P, 2, 4], F32)
        ln_st = sb("ln_st", [P, NT, 6], F32)
        ln_mv = sb("ln_mv", [P, NT, 2], F32)
        ln_sd = sb("ln_sd", [P, NT, 2], F32)

        cnt_t = sb("cnt_t", [SEG, NWP], F32)
        inv_t = sb("inv_t", [P, NREL, NT], F32)

        bank = [ctx.enter_context(nc.psum_tensor(f"bank{i}", [P, 512], F32)) for i in range(8)]

        s_edges = sem("s_edges")
        s_small = sem("s_small")
        s_wr = [sem(f"s_wr{l}") for l in range(3)]
        s_pool = sem("s_pool")
        s_vec = sem("s_vec")
        s_blank = sem("s_blank")
        s_ohw = sem("s_ohw")
        s_cntw = sem("s_cntw")
        s_rank = sem("s_rank")
        s_row = sem("s_row")
        s_stage = sem("s_stage")
        s_sea = [sem(f"s_sea{i}") for i in range(GU)]
        s_scat = [sem(f"s_scat{i}") for i in range(GU)]
        s_chunk = [sem(f"s_chunk{i}") for i in range(2)]
        s_unv = sem("s_unv")
        s_attrs = sem("s_attrs")
        s_unp = sem("s_unp")
        s_eato = [sem(f"s_eato{i}") for i in range(2)]
        s_eatc = sem("s_eatc")
        s_dlt = sem("s_dlt")
        s_xr = [sem(f"s_xr{i}") for i in range(3)]
        s_proj = sem("s_proj")
        s_pev = sem("s_pev")
        s_kvo = [sem(f"s_kvo{i}") for i in range(2)]
        s_idx = sem("s_idx")
        s_g = [sem(f"s_g{i}") for i in range(U)]
        s_gate = sem("s_gate")
        s_gatev = sem("s_gatev")
        s_q = [sem(f"s_q{i}") for i in range(U)]
        s_dlb = [sem(f"s_dlb{i}") for i in range(2)]
        s_mask = sem("s_mask")
        s_ktp, s_kt, s_sc, s_old, s_top, s_x = (sem(n) for n in ("s_ktp", "s_kt", "s_sc", "s_old", "s_top", "s_x"))
        s_e, s_ep, s_es, s_o, s_acc = (sem(n) for n in ("s_e", "s_ep", "s_es", "s_o", "s_acc"))
        s_tr = sem("s_tr")
        s_add = sem("s_add")
        s_h = sem("s_h")
        s_eat = [sem(f"s_eat{i}") for i in range(2)]
        s_oh, s_ew, s_prod, s_msg, s_sp, s_racc, s_rc = (sem(n) for n in ("s_oh", "s_ew", "s_prod", "s_msg", "s_sp", "s_racc", "s_rc"))
        s_clr = sem("s_clr")
        s_dn = sem("s_dn")
        s_dv = sem("s_dv")
        s_htp = sem("s_htp")
        s_ht = sem("s_ht")
        s_ho = [[sem(f"s_ho{l}_{i}") for i in range(4)] for l in range(2)]
        s_ln = sem("s_ln")
        s_out = sem("s_out")
        pool_n, vec_n = Count(s_pool), Count(s_vec)
        events = {}

        def event(name):
            if name not in events:
                events[name] = sem("e_" + name)
            return events[name]


        ROWSTEPS = 8
        NPROJ = [NT + 2 * 2 * NB + NT, 2 * 2 * NB + NT]
        STEPD = 4

        def gpsimd_program(g):
            def step(ins):
                return pool_n.inc(ins)

            step(g.memset(ident[:, :], 0.0))
            step(g.memset(before[:, :], 1.0))
            step(g.memset(ones_b[:, :], 1.0))
            step(g.memset(ones_f[:, :], 1.0))
            step(g.memset(ones_w[:, :], 1.0))
            step(g.memset(zeros_b[:, :], 0.0))
            step(g.iota(iota_w[:, :], pattern=[[1, NW]], base=0, channel_multiplier=0,
                        allow_small_or_imprecise_dtypes=True))
            step(g.iota(iota_seg[:, :], pattern=[[1, SEG]], base=0, channel_multiplier=0,
                        allow_small_or_imprecise_dtypes=True))
            step(g.iota(iota_t, pattern=[[1, T]], base=0, channel_multiplier=0,
                        allow_small_or_imprecise_dtypes=True))
            step(g.iota(part_i[:, :], pattern=[[0, 1]], base=0, channel_multiplier=1))
            step(g.memset(meta[:, :, REC - ND - 1:REC - ND], 0.0))
            step(g.memset(blank, 0.0))
            g.wait_ge(s_pool, pool_n.n)
            step(g.affine_select(out=ident[:, :], in_=ident[:, :], compare_op=ALU.not_equal, fill=1.0,
                                 base=0, pattern=[[-1, P]], channel_multiplier=1))
            step(g.affine_select(out=before[:, :], in_=before[:, :], compare_op=ALU.is_gt, fill=0.0,
                                 base=0, pattern=[[1, EP]], channel_multiplier=-1))
            step(g.memset(blank[:, :, C_DL:C_DL + 1], float(W)))
            g.wait_ge(s_pool, pool_n.n)
            g.memset(blank[:, :, C_SEG:C_SEG + 1], float(SEG)).then_inc(event("consts"), 1)
            step(g.memset(xr[:, 2, :], 0.0))
            step(g.memset(kvrow, 1.0))
            g.wait_ge(s_pool, pool_n.n)
            g.memset(qblk, 0.0).then_inc(event("cleared"), 1)

            g.wait_ge(s_blank, 16 * NUC)

            def scatter(trip, slot):
                g.wait_ge(s_sea[slot], 16 * (trip + 1))
                g.wait_ge(s_stage, 2 * (trip * GU + slot) + 2)
                g.sem_inc(s_gate)
                for c in range(CG):
                    g.indirect_dma_start(
                        out=rec_d, out_offset=bass.IndirectOffsetOnAxis(ap=stage_row[:, slot, c:c + 1], axis=0),
                        in_=stage[:, slot, c, :], in_offset=None).then_inc(s_scat[slot], 16)

            for slot in range(GU):
                scatter(0, slot)
            with g.Fori(1, GTRIPS) as trip:
                for slot in range(GU):
                    scatter(trip, slot)

            def gather_layer(seq, rows, width, used, used_base):
                def step(trip, u):
                    half = u // HALF
                    if u % HALF == 0:
                        if seq or not isinstance(trip, int):
                            for k in range(u, u + HALF):
                                g.wait_ge(s_g[k], 16 * (seq * TRIPS + trip))
                        g.tensor_copy(gidx[:, half, :], src_i[:, bass.ds(trip * U + u, HALF)]).then_inc(s_idx, 1)
                        g.wait_ge(s_idx, seq * 2 * TRIPS + trip * 2 + half + 1)
                        g.sem_inc(s_gate)
                    if not isinstance(trip, int):
                        g.wait_ge(used, used_base + trip * U + u - U + 1)
                        g.sem_inc(s_gate)
                    g.indirect_dma_start(
                        out=gring[:, u, 0:width], out_offset=None, in_=rows,
                        in_offset=bass.IndirectOffsetOnAxis(ap=gidx[:, half, u % HALF:u % HALF + 1], axis=0)).then_inc(s_g[u], 16)

                run_steps(g, 0, step)

            for l in range(2):
                g.wait_ge(event("tables"), l + 1)
                for slot in range(2):
                    g.wait_ge(s_kvo[slot], 16 * ((NT + 1 - slot) // 2) * (l + 1))
                if l:
                    g.wait_ge(s_o, l * T)
                g.sem_inc(s_gate)
                gather_layer(l, kv_d[l], KVW, s_o, l * T)

            g.wait_ge(event("normed"), 2)
            g.wait_ge(s_tr, 2 * NT)
            g.memset(racc, 0.0).then_inc(s_clr, 1)
            g.memset(cnt_t[:, :], 0.0).then_inc(s_clr, 1)
            g.wait_ge(s_clr, 2)
            g.memset(eat[ND:ND + 1, :, :, :], 1.0).then_inc(s_clr, 1)
            g.wait_ge(s_clr, 3)
            for l in range(3):
                if l == 0:
                    g.wait_ge(s_h, 16 * NT)
                else:
                    for i in range(4):
                        g.wait_ge(s_ho[l - 1][i], 16 * len(range(i, NT, 4)))
                g.wait_ge(s_o, 2 * T)
                if l:
                    g.wait_ge(s_prod, l * T)
                g.sem_inc(s_gate)
                gather_layer(2 + l, h_d[l], D, s_prod, l * T)
                if l < 2:
                    for i in range(NT):
                        g.wait_ge(s_dn, l * NT + i + 1)
                        g.memset(racc[:, :, i * P:(i + 1) * P], 0.0).then_inc(s_clr, 1)

        def sync_program(sp):
            for t, n in ((dst_e, "dst"), (typ_e, "edge_type_3"), (src_e, "src")):
                sp.dma_start(t[:, :], a[n].rearrange("(p j) -> p j", p=EP)).then_inc(s_edges, 16)
            sp.wait_ge(event("consts"), 1)
            rec_v = rec_d.rearrange("(p t) r -> p t r", p=P)
            for k in range(NUC):
                sp.dma_start(rec_v[:, k * UC:(k + 1) * UC, :], blank).then_inc(s_blank, 16)

            def weights(slot, k, w, done):
                sp.dma_start(wts[:, slot, k, :, :], w.rearrange("(c p) n -> p c n", p=P)).then_inc(done, 16)

            for l in range(2):
                for k, n in enumerate("qkvs"):
                    weights(l, k, a[f"L0_gnn_w{l + 1}{n}"], s_small)
                for t, n in ((bias_q, "b{}q"), (bias_s, "b{}s"), (gamma, "g{}"), (beta, "be{}")):
                    sp.dma_start(t[:, l, :], a["L0_gnn_" + n.format(l + 1)].rearrange("(c p) -> p c", p=P),
                                 allow_slow_non_contiguous=True).then_inc(s_small, 16)
                for k, n in enumerate("kv"):
                    sp.dma_start(bias_kv[:, l, k, :], a[f"L0_gnn_b{l + 1}{n}"].partition_broadcast(P)).then_inc(s_small, 16)
            for l in range(3):
                sp.dma_start(bias_r[:, l, :], a["L1_gnn_bias"][l, :].partition_broadcast(P)).then_inc(s_small, 16)
            sp.dma_start(nnw[:, :, :], a["L1_gnn_nn_w"].rearrange("(c p) j -> p c j", p=P)).then_inc(s_small, 16)
            sp.dma_start(nnwt[ND:ND + 1, :], a["L1_gnn_nn_b"].rearrange("(o f) -> o f", o=1)).then_inc(s_small, 16)

            def load_rows(i, use, sem_used, used):
                tail = i == NT - 1
                slot = 2 if tail else i % 2
                if used is not None:
                    sp.wait_ge(sem_used, used)
                n = NTAIL if tail else P
                sp.dma_start(xr[0:n, slot, :], a["x"][i * P:i * P + n, :]).then_inc(s_xr[slot], 16)

            sp.wait_ge(event("cleared"), 1)
            for i in range(NT):
                load_rows(i, 0, s_proj, i - 1 if 2 <= i < NT - 1 else None)
            for l in range(2):
                if l == 0:
                    kv_base = NT + 4 * NB
                else:
                    kv_base = NPROJ[0] + 4 * NB
                for i in range(NT):
                    sp.wait_ge(s_pev, kv_base + i + 1)
                    sp.dma_start(kv_d[l][i * P:(i + 1) * P, :], kvrow[:, i % 2, :]).then_inc(s_kvo[i % 2], 16)
                if l == 0:
                    for slot in range(GU):
                        sp.wait_ge(s_scat[slot], 16 * CG * GTRIPS)
                    for k in range(NUC):
                        if k >= 2:
                            sp.wait_ge(s_unv, 3 * (k - 1))
                            sp.wait_ge(s_attrs, k - 1)
                        sp.dma_start(chunk[:, k % 2, :, :], rec_v[:, k * UC:(k + 1) * UC, :]).then_inc(s_chunk[k % 2], 16)
                    sp.wait_ge(event("dlt"), 1)
                    sp.dma_start(dlt_d.rearrange("(q t) p -> t q p", t=P), dlt_out[:, :, :]).then_inc(s_dlt, 16)
                    sp.wait_ge(s_dlt, 16)
                sp.wait_ge(s_pev, sum(NPROJ[:l + 1]))

                def step(trip, u):
                    t = trip * U + u
                    if u % HALF == 0:
                        half = u // HALF
                        if l or not isinstance(trip, int):
                            sp.wait_ge(s_mask, l * 2 * TRIPS + trip * 2 + half - 1)
                        sp.dma_start(dlb[:, half, :], dlt_d[bass.ds(t, HALF), :].rearrange("t p -> (t p)")
                                     .partition_broadcast(P)).then_inc(s_dlb[half], 16)
                    w = sp.value_load(win_i[0:1, bass.ds(t, 1)], min_val=0, max_val=NW)
                    if l or not isinstance(trip, int):
                        sp.wait_ge(s_sc, l * T + t - U + 1)
                    sp.dma_start(qs[:, u, :, :], qblk[:, bass.ds(w, 1), :, :].rearrange("p o c m -> p (o c) m"))\
                        .then_inc(s_q[u], 16)

                run_steps(sp, 0, step)
            for i in range(NT):
                load_rows(i, 1, s_add, 4 * 2 * NT + i - 1 if 2 <= i < NT - 1 else (4 * 2 * NT if i < 2 else None))
            for l in range(2):
                load_relational(sp, l)
            for i in range(NT):
                sp.wait_ge(s_ln, i + 1)
                sp.dma_start(h_d[0][i * P:(i + 1) * P, :], x1[:, i, :]).then_inc(s_h, 16)
            for l in range(3):
                def step(trip, u):
                    if u % HALF:
                        return
                    half = u // HALF
                    if l or not isinstance(trip, int):
                        sp.wait_ge(s_ew, l * T + trip * U + u - HALF)
                    sp.dma_start(eat[0:ND, half, :, :],
                                 eat_d[bass.ds(trip, 1), :, half * P:(half + 1) * P]
                                 .rearrange("o (q j) e -> (o j) q e", q=4)).then_inc(s_eat[half], 16)

                if l == 0:
                    for i in range(2):
                        sp.wait_ge(s_eato[i], 16 * NUC * 2)
                run_steps(sp, 0, step)
                if l < 2:
                    for i in range(NT):
                        sp.wait_ge(s_dv, STEPD * (l * NT + i + 1))
                        sp.dma_start(h_d[l + 1][i * P:(i + 1) * P, :], orow[:, i % 4, :]).then_inc(s_ho[l][i % 4], 16)
                    if l == 0:
                        load_relational(sp, 2)
            for i in range(NT):
                n = NTAIL if i == NT - 1 else P
                sp.wait_ge(s_ln, NT + i + 1)
                sp.dma_start(out[i * P:i * P + n, :], x1[0:n, i, :]).then_inc(s_out, 16)
            sp.wait_ge(s_out, 16 * NT)

        def load_relational(sp, l):
            if l == 0:
                sp.wait_ge(s_proj, sum(NPROJ))
            if l == 2:
                sp.wait_ge(s_dn, NT)
            for r in range(NREL):
                sp.dma_start(wts[:, l % 2, r, :, :], a["L1_gnn_W"][l, r, :, :].rearrange("(c p) n -> p c n", p=P))\
                    .then_inc(s_wr[l], 16)
            sp.dma_start(wts[:, l % 2, NREL, :, :], a["L1_gnn_root"][l, :, :].rearrange("(c p) n -> p c n", p=P))\
                .then_inc(s_wr[l], 16)

        def tensor_program(pe):
            pe.wait_ge(event("consts"), 1)
            pe.wait_ge(s_small, 16 * 25)
            for c in range(2):
                ins = pe.transpose(bank[7][0:ND, c * P:(c + 1) * P], nnw[:, c, :], ident[:, :])
            ins.then_inc(event("nnw"), 1)

            cnt = bank[6][:, 0:CG * NW]
            pe.matmul(cnt, ones_b[0:EP, :], zeros_b[:, :], start=True, stop=False)

            def count(trip, slot):
                pe.wait_ge(s_ohw, trip * GU + slot + 1)
                pe.matmul(cnt, ones_b[0:EP, :], onehot_w[:, slot, :, :].rearrange("p c w -> p (c w)"),
                          start=False, stop=False).then_inc(s_cntw, 1)

            for slot in range(GU):
                count(0, slot)
            with pe.Fori(1, GTRIPS) as trip:
                for slot in range(GU):
                    count(trip, slot)
            pe.matmul(cnt, ones_b[0:EP, :], zeros_b[:, :], start=False, stop=True)\
                .then_inc(event("counted"), 1)
            pe.wait_ge(event("tend"), 1)
            pe.transpose(bank[5][0:NW, 0:P], tend[:, :], ident[:, :]).then_inc(event("tend_c"), 1)
            pe.wait_ge(event("ended"), 1)
            pe.matmul(bank[7][:, 0:T], ones_b[0:NW, :], ended, start=True, stop=True).then_inc(event("tile_w"), 1)
            pe.wait_ge(event("tend_copied"), 1)

            def ranks(trip, slot):
                g = trip * GU + slot
                pe.wait_ge(s_ohw, G + g + 1)
                if not isinstance(trip, int):
                    pe.wait_ge(s_row, ROWSTEPS * (g - GU + 1))
                r = bank[slot][0:EP, 0:CG * NW]
                pe.matmul(r, before[:, :], onehot_w[:, slot, :, :].rearrange("p c w -> p (c w)"), start=True, stop=False)
                for c in range(CG - 1):
                    left = CG - 1 - c
                    pe.matmul(r[:, (c + 1) * NW:].rearrange("p (c w) -> p c w", w=NW), ones_b[0:EP, 0:EP],
                              onehot_w[:, slot, c:c + 1, :].to_broadcast([EP, left, NW]), start=False, stop=left == 1)
                wait_freed(pe, s_row, ROWSTEPS * (g - 1))
                for c in range(CG):
                    ins = pe.matmul(bank[5 + slot % 3][0:EP, 0:NW], ones_b[0:EP, 0:EP], onehot_w[:, slot, c, :],
                                    start=c == 0, stop=c == CG - 1)
                ins.then_inc(s_rank, 1)

            for slot in range(GU):
                ranks(0, slot)
            with pe.Fori(1, GTRIPS) as trip:
                for slot in range(GU):
                    ranks(trip, slot)
            pe.wait_ge(s_row, ROWSTEPS * G)

            for l in range(2):
                project(pe, l)
                if l == 0:
                    pe.wait_ge(s_pev, NPROJ[0])
                    for k in range(NUC):
                        pe.wait_ge(s_attrs, k + 1)
                        for b in range(4):
                            if k:
                                pe.wait_ge(s_eatc, 4 * (k - 1) + b + 1)
                            for q in range(4):
                                t = 16 * b + 4 * q
                                ins = pe.transpose(bank[b][:, q * P:(q + 1) * P],
                                                   attrs[:, k % 2, t * ND:(t + 4) * ND], ident[:, :])
                            ins.then_inc(s_unp, 1)
                    pe.wait_ge(s_unv, 3 * NUC)
                    for q in range(T // P):
                        ins = pe.transpose(bank[4][:, q * P:(q + 1) * P], dl_f[:, q * P:(q + 1) * P], ident[:, :])
                    ins.then_inc(event("dl_t"), 1)
                    pe.wait_ge(s_eatc, 4 * NUC)
                    pe.wait_ge(event("dlt"), 1)
                else:
                    pe.wait_ge(s_pev, sum(NPROJ))
                attention_tiles(pe, l)
                pe.wait_ge(event("divided"), l + 1)
                for j in range(NT):
                    if j >= 2:
                        pe.wait_ge(s_add, 4 * (l * NT + j - 1))
                    for k in range(WPT):
                        ins = pe.transpose(bank[j % 2][0:HD, k * P:(k + 1) * P], acc[:, WPT * j + k, 0:HD], ident[:, :])
                    ins.then_inc(s_tr, 1)

            pe.wait_ge(event("leaky"), 2)
            pe.wait_ge(s_add, 4 * 2 * NT)
            for i in range(NT):
                if i >= 2:
                    pe.wait_ge(s_add, 4 * 2 * NT + i - 1)
                for c in range(2):
                    ins = pe.transpose(bank[i % 2][:, c * P:(c + 1) * P], ht[:, c, i * P:(i + 1) * P], ident[:, :])
                ins.then_inc(s_tr, 1)
            for i in range(NT):
                pe.wait_ge(s_ln, i + 1)
                features(pe, i, x1[:, i, :], i)

            for l in range(3):
                pe.wait_ge(s_ht, NT * (l + 1))
                if l == 0:
                    pe.wait_ge(event("nnwt"), 1)
                    pe.wait_ge(s_clr, 3)
                else:
                    pe.wait_ge(s_dv, STEPD * l * NT)
                relation_tiles(pe, l)
                pe.wait_ge(s_wr[l], 16 * (NREL + 1))
                pe.wait_ge(s_racc, (l + 1) * T)
                if l == 0:
                    pe.wait_ge(s_rc, T)
                    for k in range(WPT):
                        for r in range(NREL):
                            ins = pe.matmul(bank[7][k * W:(k + 1) * W, r * NT:(r + 1) * NT],
                                            ident[0:SEG, r * W:(r + 1) * W], cnt_t[:, k:NWP:WPT], start=True, stop=True)
                    ins.then_inc(event("cnt"), 1)
                for i in range(NT):
                    n = l * NT + i
                    if n >= 2:
                        pe.wait_ge(s_dv, STEPD * (n - 1))
                    b = 2 * (n % 2)
                    for r in range(-1, NREL):
                        o = bank[b + (r + 1) // 2][:, (r + 1) % 2 * D:((r + 1) % 2 + 1) * D]
                        for c in range(2):
                            lhs = ht[:, c, i * P:(i + 1) * P] if r < 0 else \
                                racc[:, c * NREL + r, i * P:(i + 1) * P]
                            ins = pe.matmul(o, lhs, wts[:, l % 2, r if r >= 0 else NREL, c, :], start=c == 0, stop=c == 1)
                    ins.then_inc(s_dn, 1)
                    if l < 2 and i:
                        pe.wait_ge(s_dv, STEPD * n)
                        features(pe, i - 1, orow[:, (i - 1) % 4, :], (l + 1) * NT + i - 1)
                if l < 2:
                    pe.wait_ge(s_dv, STEPD * (l + 1) * NT)
                    features(pe, NT - 1, orow[:, (NT - 1) % 4, :], (l + 1) * NT + NT - 1)

        def features(pe, i, rows, n):
            if n >= 2:
                pe.wait_ge(s_ht, n - 1)
            for c in range(2):
                ins = pe.transpose(bank[4 + n % 2][:, c * P:(c + 1) * P], rows[:, c * P:(c + 1) * P], ident[:, :])
            ins.then_inc(s_htp, 1)

        def project(pe, l):
            job = sum(NPROJ[:l])

            def free(job):
                if job >= 4:
                    pe.wait_ge(s_pev, job - 3)
                return bank[job % 4]

            if l == 0:
                for i in range(NT):
                    slot = 2 if i == NT - 1 else i % 2
                    pe.wait_ge(s_xr[slot], 16 * (1 if slot == 2 else i // 2 + 1))
                    b = free(job)
                    for c in range(2):
                        ins = pe.transpose(b[:, c * P:(c + 1) * P], xr[:, slot, c * P:(c + 1) * P], ident[:, :])
                    ins.then_inc(s_proj, 1)
                    job += 1
                pe.wait_ge(s_pev, NT)
            else:
                pe.wait_ge(event("leaky"), 1)
                pe.wait_ge(s_add, 4 * NT)
            for k in (0, 3):
                for c in range(2):
                    for nb in range(NB):
                        n = min(512, NP - nb * 512)
                        b = free(job)
                        for kc in range(2):
                            ins = pe.matmul(b[:, 0:n], wts[:, l, k, kc, c * P:(c + 1) * P],
                                            ht[:, kc, nb * 512:nb * 512 + n], start=kc == 0, stop=kc == 1)
                        ins.then_inc(s_proj, 1)
                        job += 1
            for i in range(NT):
                b = free(job)
                for kc in range(2):
                    ins = pe.matmul(b[:, :].rearrange("p (k n) -> p k n", k=2), ht[:, kc, i * P:(i + 1) * P],
                                    wts[:, l, 1:3, kc, :], start=kc == 0, stop=kc == 1)
                ins.then_inc(s_proj, 1)
                job += 1

        def attention_tiles(pe, l):
            at = l * T

            def step(trip, u):
                if live(trip, u, 0):
                    t, slot, r = tile_of(trip, u, 0)
                    pe.wait_ge(s_g[slot], 16 * (l * TRIPS + r + 1))
                    wait_freed(pe, s_kt, at + t - 1)
                    for c in range(2):
                        ins = pe.transpose(bank[u % 2][:, c * P:(c + 1) * P], gring[:, slot, c * P:(c + 1) * P], ident[:, :])
                    ins.then_inc(s_ktp, 1)
                if live(trip, u, 1):
                    t, slot, r = tile_of(trip, u, 1)
                    pe.wait_ge(s_q[slot], 16 * (l * TRIPS + r + 1))
                    pe.wait_ge(s_kt, at + t + 1)
                    wait_freed(pe, s_x, at + t - 1)
                    for c in range(2):
                        ins = pe.matmul(bank[2 + slot % 2][c * 2 * W:(c + 1) * 2 * W, 0:P], qs[:, slot, c, :],
                                        kt[:, slot % 2, c * P:(c + 1) * P], start=True, stop=True)
                    ins.then_inc(s_sc, 1)
                if live(trip, u, 2):
                    t, slot, r = tile_of(trip, u, 2)
                    pe.wait_ge(s_e, at + t + 1)
                    wait_freed(pe, s_es, at + t - 1)
                    pe.transpose(bank[4 + slot % 2][:, 0:P], et[:, slot % 4, 0:P], ident[:, :]).then_inc(s_ep, 1)
                if live(trip, u, 3):
                    t, slot, r = tile_of(trip, u, 3)
                    pe.wait_ge(s_es, at + t + 1)
                    wait_freed(pe, s_acc, at + t - 1)
                    for h in range(HEADS):
                        ins = pe.matmul(bank[6 + slot % 2][h * W:(h + 1) * W, 0:VW], es[:, slot % 2, h * W:(h + 1) * W],
                                        gring[:, slot, D + h * VW:D + (h + 1) * VW], start=True, stop=True)
                    ins.then_inc(s_o, 1)

            run_steps(pe, 3, step)

        def relation_tiles(pe, l):
            at = l * T

            def step(trip, u):
                if live(trip, u, 0):
                    t, slot, r = tile_of(trip, u, 0)
                    if slot % HALF == 0:
                        pe.wait_ge(s_eat[slot // HALF], 16 * (l * TRIPS + r + 1))
                    wait_freed(pe, s_prod, at + t - 1)
                    pe.matmul(bank[slot % 2][:, 0:D], eat[:, slot // HALF, slot % HALF, :], nnwt[:, :],
                              start=True, stop=True).then_inc(s_ew, 1)
                if live(trip, u, 2):
                    t, slot, r = tile_of(trip, u, 2)
                    if slot % HALF == 0:
                        pe.wait_ge(s_oh, 2 * (l * TRIPS + r) + slot // HALF + 1)
                    pe.wait_ge(s_msg, at + t + 1)
                    wait_freed(pe, s_racc, at + t - 1)
                    if l == 0:
                        wait_freed(pe, s_rc, at + t - 1)
                    b = bank[2 + slot % 2]
                    one = oh[:, slot // HALF, slot % HALF, :]
                    if l == 0:
                        pe.matmul(b[0:SEG, 2 * SEG:2 * SEG + 1], one, ones_f[:, :], start=True, stop=True)
                    for c in range(2):
                        ins = pe.matmul(b[:, c * SEG:(c + 1) * SEG], msg[:, slot % 2, c * P:(c + 1) * P], one,
                                        start=True, stop=True)
                    ins.then_inc(s_sp, 1)

            run_steps(pe, 2, step)

        def scalar_program(act):
            ea_v = a["edge_attr_32"].rearrange("(p j) c -> p j c", p=EP)

            def staging(trip, slot):
                g = trip * GU + slot
                if not isinstance(trip, int):
                    act.wait_ge(s_scat[slot], 16 * CG * trip)
                act.dma_start(stage[:, slot, :, 0:ND], ea_v[:, bass.ds(g * CG, CG), :]).then_inc(s_sea[slot], 16)
                act.wait_ge(s_row, ROWSTEPS * (g + 1))
                act.copy(stage[:, slot, :, ND:REC], meta[:, bass.ds(g * CG, CG), :]).then_inc(s_stage, 1)
                act.copy(stage_row[:, slot, :], row_e[:, bass.ds(g * CG, CG)]).then_inc(s_stage, 1)

            for slot in range(GU):
                staging(0, slot)
            with act.Fori(1, GTRIPS) as trip:
                for slot in range(GU):
                    staging(trip, slot)

            for b in range(4 * NUC):
                if b % 4 == 0:
                    k = b // 4
                    act.wait_ge(s_chunk[k % 2], 16 * (k // 2 + 1))
                    if k == 0:
                        act.wait_ge(s_pev, NPROJ[0])
                    act.copy(attrs[:, k % 2, :].rearrange("p (t c) -> p t c", c=ND), chunk[:, k % 2, :, 0:ND])\
                        .then_inc(s_attrs, 1)
                act.wait_ge(s_unp, b + 1)
                if b >= 2:
                    act.wait_ge(s_eato[b % 2], 16 * (b // 2))
                act.copy(eat_out[:, b % 2, :], bank[b % 4][:, :]).then_inc(s_eatc, 1)
                act.wait_ge(s_eatc, b + 1)
                act.dma_start(eat_d[2 * b:2 * b + 2, :, :].rearrange("b q f -> q b f"),
                              eat_out[:, b % 2, :].rearrange("q (b f) -> q b f", b=2)).then_inc(s_eato[b % 2], 16)

            for i in range(2):
                act.wait_ge(s_eato[i], 16 * 2 * NUC)
            for l in range(2):
                attention_acts(act, l)
                act.wait_ge(event("var"), l + 1)
                act.activation(bn_t[:, :, 1], bn_t[:, :, 0], ACT.Sqrt).then_inc(event("std"), 1)
                act.wait_ge(event("affine"), l + 1)
                act.wait_ge(s_proj, sum(NPROJ[:l + 1]))
                for c in range(2):
                    ins = act.activation(ht[:, c, :], st[:, c, :], ACT.Identity, bias=bn_t[:, c, 3:4], scale=bn_t[:, c, 2:3])
                ins.then_inc(event("normed"), 1)
            act.wait_ge(event("ln_var"), 1)
            act.activation(ln_sd[:, :, 1], ln_sd[:, :, 0], ACT.Sqrt).then_inc(event("ln_std"), 1)

            def copy_features(i, n):
                act.wait_ge(s_htp, n + 1)
                act.copy(ht[:, :, i * P:(i + 1) * P], bank[4 + n % 2][:, 0:2 * P].rearrange("p (c n) -> p c n", c=2))\
                    .then_inc(s_ht, 1)

            for i in range(NT):
                copy_features(i, i)
            for l in range(3):
                def relation_step(trip, u):
                    t, slot, r = tile_of(trip, u, 0)
                    act.wait_ge(s_prod, l * T + t + 1)
                    wait_freed(act, s_sp, l * T + t - 1)
                    act.activation(msg[:, slot % 2, :], prod[:, slot % 2, :], ACT.Relu).then_inc(s_msg, 1)

                run_steps(act, 0, relation_step)
                if l < 2:
                    for i in range(NT):
                        copy_features(i, (l + 1) * NT + i)
            act.wait_ge(event("ln_var"), 2)
            act.activation(ln_sd[:, :, 1], ln_sd[:, :, 0], ACT.Sqrt).then_inc(event("ln_std"), 1)

        def attention_acts(act, l):
            at = l * T

            def step(trip, u):
                if live(trip, u, 0):
                    t, slot, r = tile_of(trip, u, 0)
                    act.wait_ge(s_ktp, at + t + 1)
                    wait_freed(act, s_sc, at + t - 1)
                    act.copy(kt[:, slot % 2, :], bank[slot % 2][:, 0:2 * P]).then_inc(s_kt, 1)
                if live(trip, u, 1):
                    t, slot, r = tile_of(trip, u, 1)
                    act.wait_ge(s_x, at + t + 1)
                    wait_freed(act, s_acc, at + t - 3)
                    act.activation(et[:, slot % 4, :], xs[:, slot % 2, :], ACT.Exp, bias=ntop[:, slot % 4:slot % 4 + 1],
                                   scale=SCALE).then_inc(s_e, 1)

            run_steps(act, 1, step)

        def vector_program(v):
            def step(ins):
                return vec_n.inc(ins)

            def after():
                v.wait_ge(s_vec, vec_n.n)

            def tell(name, ins):
                ins.then_inc(event(name), 1)
                told[name] = told.get(name, 0) + 1
                v.wait_ge(event(name), told[name])

            told = {}

            v.wait_ge(s_edges, 48)
            v.wait_ge(event("consts"), 1)
            step(v.tensor_scalar(int_e[:, :], dst_e[:, :], W - 1, None, ALU.bitwise_and))
            step(v.tensor_scalar(part_m[:, :], part_i[:, :], W - 1, None, ALU.bitwise_and))
            step(v.tensor_copy(meta[:, :, 0], src_e[:, :]))
            after()
            step(v.tensor_copy(part_dl[:, :], part_m[:, :]))
            step(v.tensor_copy(meta[:, :, 1], int_e[:, :]))
            after()
            step(v.scalar_tensor_tensor(meta[:, :, 2], typ_e[:, :], float(W), meta[:, :, 1], ALU.mult, ALU.add))
            step(v.tensor_scalar(int_e[:, :], dst_e[:, :], W.bit_length() - 1, None, ALU.logical_shift_right))
            after()
            step(v.tensor_copy(win_f[:, :], int_e[:, :]))
            v.wait_ge(event("nnw"), 1)
            v.wait_ge(s_small, 16 * 25)
            tell("nnwt", v.tensor_copy(nnwt[0:ND, :], bank[7][0:ND, 0:D]))
            after()

            def one_hot(trip, slot):
                g = trip * GU + slot
                v.tensor_tensor(onehot_w[:, slot, :, :],
                                win_f[:, bass.ds(g * CG, CG)].unsqueeze(2).to_broadcast([EP, CG, NW]),
                                iota_w[0:EP, :].unsqueeze(1).to_broadcast([EP, CG, NW]), ALU.is_equal).then_inc(s_ohw, 1)

            def count_step(trip, slot):
                if not isinstance(trip, int):
                    v.wait_ge(s_cntw, trip * GU + slot - GU + 1)
                one_hot(trip, slot)

            for slot in range(GU):
                count_step(0, slot)
            with v.Fori(1, GTRIPS) as trip:
                for slot in range(GU):
                    count_step(trip, slot)

            v.wait_ge(event("counted"), 1)
            step(v.tensor_reduce(cnt_w[:, :], bank[6][:, 0:CG * NW].rearrange("p (c w) -> p w c", c=CG), AX.X, ALU.add))
            after()
            step(v.tensor_scalar(tiles_i[:, :], cnt_w[:, :], float(P - 1), None, ALU.add))
            after()
            step(v.tensor_scalar(tiles_i[:, :], tiles_i[:, :], P.bit_length() - 1, None, ALU.logical_shift_right))
            after()
            step(v.tensor_copy(tiles_f[:, :], tiles_i[:, :]))
            after()
            tell("tend", v.tensor_tensor_scan(tend[:, :], ones_w[:, :], tiles_f[:, :], 0.0, ALU.mult, ALU.add))
            after()
            step(v.tensor_tensor(run_tot[:, :], tend[:, :], tiles_f[:, :], ALU.subtract))
            after()
            step(v.tensor_scalar(run_tot[:, :], run_tot[:, :], float(P), None, ALU.mult))
            v.wait_ge(event("tend_c"), 1)
            tell("tend_copied", v.tensor_copy(tend_c[:, :], bank[5][0:NW, 0:1]))
            after()
            tell("ended", v.tensor_scalar(ended, iota_t, tend_c[:, 0:1], None, ALU.is_ge))
            v.wait_ge(event("tile_w"), 1)
            step(v.tensor_copy(tile_w, bank[7][:, 0:T]))
            after()
            step(v.tensor_copy(win_i[:, :], tile_w[0:1, :]))
            step(v.memset(restart[:, 0:1], 1.0))
            step(v.tensor_tensor(restart[:, 1:T], tile_w[:, 1:T], tile_w[:, 0:T - 1], ALU.not_equal))
            after()
            step(v.tensor_scalar(restart[:, :], restart[:, :], RESTART - KEEP, KEEP, ALU.mult, ALU.add))
            after()

            def rows_of(trip, slot):
                g = trip * GU + slot
                n = ROWSTEPS * g
                v.wait_ge(s_rank, g + 1)
                if not isinstance(g, int) or g:
                    v.wait_ge(s_row, n)
                r = bank[slot][0:EP, 0:CG * NW].rearrange("p (c w) -> p c w", c=CG)
                v.tensor_tensor(rank[:, :, :], r, run_tot[0:EP, :].unsqueeze(1).to_broadcast([EP, CG, NW]), ALU.add)\
                    .then_inc(s_row, 1)
                v.wait_ge(s_row, n + 1)
                v.tensor_tensor(rank[:, :, :], rank[:, :, :], onehot_w[:, slot, :, :], ALU.mult).then_inc(s_row, 1)
                v.tensor_tensor(run_tot[0:EP, :], run_tot[0:EP, :], bank[5 + slot % 3][0:EP, 0:NW], ALU.add)\
                    .then_inc(s_row, 1)
                v.wait_ge(s_row, n + 2)
                v.tensor_reduce(pos_f[:, :], rank[:, :, :], AX.X, ALU.add).then_inc(s_row, 1)
                v.wait_ge(s_row, n + 4)
                v.tensor_copy(pos_i[:, :], pos_f[:, :]).then_inc(s_row, 1)
                v.wait_ge(s_row, n + 5)
                v.tensor_scalar(pos_lo[:, :], pos_i[:, :], P - 1, T.bit_length() - 1, ALU.bitwise_and,
                                ALU.logical_shift_left).then_inc(s_row, 1)
                v.tensor_scalar(pos_hi[:, :], pos_i[:, :], P.bit_length() - 1, None, ALU.logical_shift_right).then_inc(s_row, 1)
                v.wait_ge(s_row, n + 7)
                v.tensor_tensor(row_e[:, bass.ds(g * CG, CG)], pos_lo[:, :], pos_hi[:, :], ALU.bitwise_or).then_inc(s_row, 1)

            v.wait_ge(s_cntw, G)
            for slot in range(GU):
                one_hot(0, slot)
            for slot in range(GU):
                rows_of(0, slot)
            with v.Fori(1, GTRIPS) as trip:
                for slot in range(GU):
                    one_hot(trip, slot)
                for slot in range(GU):
                    rows_of(trip, slot)

            for l in range(2):
                projected(v, l)
                if l == 0:
                    for k in range(NUC):
                        v.wait_ge(s_chunk[k % 2], 16 * (k // 2 + 1))
                        for t, c in ((src_i, C_SRC), (dl_f, C_DL), (seg_f, C_SEG)):
                            v.tensor_copy(t[:, k * UC:(k + 1) * UC], chunk[:, k % 2, :, c]).then_inc(s_unv, 1)
                    v.wait_ge(event("dl_t"), 1)
                    tell("dlt", v.tensor_copy(dlt_out[:, :, :].rearrange("t q p -> t (q p)"), bank[4][:, 0:T]))
                    v.wait_ge(s_unp, 4 * NUC)
                    v.wait_ge(s_unv, 3 * NUC)
                step(v.memset(top[:, :], 0.0))
                tell("tables", v.memset(acc, 0.0))
                after()
                attended(v, l)
                v.wait_ge(s_acc, (l + 1) * T)
                step(v.tensor_scalar(rden[:, :], acc[:, :, HD], 1e-30, None, ALU.max))
                after()
                step(v.reciprocal(rden[:, :], rden[:, :]))
                after()
                tell("divided", v.tensor_tensor(acc[:, :, 0:HD], acc[:, :, 0:HD],
                                                rden[:, :].unsqueeze(2).to_broadcast([P, NWP, HD]), ALU.mult))
                for j in range(NT):
                    v.wait_ge(s_tr, l * NT + j + 1)
                    for h in range(HEADS):
                        o = st[h % 2 * HD:(h % 2 + 1) * HD, h // 2, j * P:(j + 1) * P].rearrange("p (w d) -> p w d", d=W)
                        v.tensor_tensor(o, bank[j % 2][0:HD, :].rearrange("p (w h d) -> p w h d", h=HEADS, d=W)[:, :, h, :],
                                        o, ALU.add).then_inc(s_add, 1)
                v.wait_ge(s_add, 4 * (l + 1) * NT)
                for c in range(2):
                    for nb in range(NB):
                        n = min(512, N - nb * 512)
                        step(v.bn_stats(stats[:, c, nb, :], st[:, c, nb * 512:nb * 512 + n]))
                after()
                for c in range(2):
                    step(v.bn_aggr(mv[:, c, :], stats[:, c, :, :].rearrange("p b s -> p (b s)")))
                after()
                tell("var", v.tensor_scalar(bn_t[:, :, 0], mv[:, :, 1], EPS, None, ALU.add))
                v.wait_ge(event("std"), l + 1)
                step(v.reciprocal(bn_t[:, :, 1], bn_t[:, :, 1]))
                after()
                step(v.tensor_tensor(bn_t[:, :, 2], bn_t[:, :, 1], gamma[:, l, :], ALU.mult))
                after()
                step(v.tensor_tensor(bn_t[:, :, 3], mv[:, :, 0], bn_t[:, :, 2], ALU.mult))
                after()
                tell("affine", v.tensor_tensor(bn_t[:, :, 3], beta[:, l, :], bn_t[:, :, 3], ALU.subtract))
                v.wait_ge(event("normed"), l + 1)
                step(v.scalar_tensor_tensor(ht[:, 0, :], ht[:, 0, :], 0.1, ht[:, 0, :], ALU.mult, ALU.max))
                tell("leaky", v.scalar_tensor_tensor(ht[:, 1, :], ht[:, 1, :], 0.1, ht[:, 1, :], ALU.mult, ALU.max))

            for i in range(NT):
                slot = 2 if i == NT - 1 else i % 2
                v.wait_ge(s_tr, 2 * NT + i + 1)
                v.wait_ge(s_xr[slot], 16 * (2 if slot == 2 else NT // 2 + i // 2 + 1))
                v.tensor_tensor(x1[:, i, :], bank[i % 2][:, 0:D], xr[:, slot, :], ALU.add).then_inc(s_add, 1)
            v.wait_ge(s_add, 4 * 2 * NT + NT)
            layer_norm(v, step, after, tell, 0)

            v.wait_ge(s_clr, 3)
            for l in range(3):
                related(v, l)
                if l == 0:
                    v.wait_ge(event("cnt"), 1)
                    step(v.tensor_scalar(inv_t[:, :, :].rearrange("p r i -> p (r i)"), bank[7][:, 0:NREL * NT], 1.0, None, ALU.max))
                    after()
                    step(v.reciprocal(inv_t[:, :, :], inv_t[:, :, :]))
                    after()
                for i in range(NT):
                    n = l * NT + i
                    b = 2 * (n % 2)
                    v.wait_ge(s_dn, n + 1)
                    if l < 2 and i >= 4:
                        v.wait_ge(s_ho[l][i % 4], 16 * (i // 4))
                        v.wait_ge(s_htp, (l + 1) * NT + i - 3)
                    o = orow[:, i % 4, :]
                    v.tensor_tensor(o, bank[b][:, 0:D], bias_r[:, l, :], ALU.add).then_inc(s_dv, 1)
                    for r in range(NREL):
                        p = bank[b + (r + 1) // 2][:, (r + 1) % 2 * D:((r + 1) % 2 + 1) * D]
                        v.wait_ge(s_dv, STEPD * n + r + 1)
                        v.scalar_tensor_tensor(o, p, inv_t[:, r, i:i + 1], o, ALU.mult, ALU.add).then_inc(s_dv, 1)
                    if l == 2:
                        v.wait_ge(s_dv, STEPD * (n + 1))
                        step(v.tensor_tensor(x1[:, i, :], x1[:, i, :], o, ALU.add))
            after()
            layer_norm(v, step, after, tell, 1)

        def layer_norm(v, step, after, tell, n):
            for i in range(NT):
                step(v.bn_stats(ln_st[:, i, :], x1[:, i, :]))
            after()
            for i in range(NT):
                step(v.bn_aggr(ln_mv[:, i, :], ln_st[:, i, :]))
            after()
            tell("ln_var", v.tensor_scalar(ln_sd[:, :, 0], ln_mv[:, :, 1], EPS, None, ALU.add))
            v.wait_ge(event("ln_std"), n + 1)
            step(v.reciprocal(ln_sd[:, :, 1], ln_sd[:, :, 1]))
            after()
            for i in range(NT):
                v.tensor_scalar(x1[:, i, :], x1[:, i, :], ln_mv[:, i, 0:1], ln_sd[:, i, 1:2], ALU.subtract, ALU.mult)\
                    .then_inc(s_ln, 1)

        def projected(v, l):
            job = sum(NPROJ[:l])
            if l == 0:
                v.wait_ge(event("cleared"), 1)
                for i in range(NT):
                    v.wait_ge(s_proj, job + 1)
                    v.tensor_copy(ht[:, :, i * P:(i + 1) * P], bank[job % 4][:, 0:2 * P].rearrange("p (c n) -> p c n", c=2))\
                        .then_inc(s_pev, 1)
                    job += 1
            for c in range(2):
                for nb in range(NB):
                    n = min(512, NP - nb * 512)
                    v.wait_ge(s_proj, job + 1)
                    for k in range(2):
                        ins = v.tensor_scalar(qblk[k * HD:(k + 1) * HD, nb * 512 // W:(nb * 512 + n) // W, c, k * W:(k + 1) * W],
                                              bank[job % 4][k * HD:(k + 1) * HD, 0:n].rearrange("p (w d) -> p w d", d=W),
                                              bias_q[k * HD:(k + 1) * HD, l, c:c + 1], None, ALU.add)
                        if k == 0:
                            vec_n.inc(ins)
                    ins.then_inc(s_pev, 1)
                    job += 1
            v.wait_ge(s_vec, vec_n.n)
            for c in range(2):
                for nb in range(NB):
                    n = min(512, NP - nb * 512)
                    v.wait_ge(s_proj, job + 1)
                    v.tensor_scalar(st[:, c, nb * 512:nb * 512 + n], bank[job % 4][:, 0:n], bias_s[:, l, c:c + 1], None, ALU.add)\
                        .then_inc(s_pev, 1)
                    job += 1
            for i in range(NT):
                v.wait_ge(s_proj, job + 1)
                done = 16 * (l * ((NT + 1 - i % 2) // 2) + i // 2)
                if done:
                    v.wait_ge(s_kvo[i % 2], done)
                vec_n.inc(v.tensor_tensor(kvrow[:, i % 2, 0:D], bank[job % 4][:, 0:D], bias_kv[:, l, 0, :], ALU.add))
                v.wait_ge(s_vec, vec_n.n)
                v.tensor_tensor(kvrow[:, i % 2, D:].rearrange("p (h v) -> p h v", v=VW)[:, :, 0:HD],
                                bank[job % 4][:, D:2 * D].rearrange("p (h v) -> p h v", v=HD),
                                bias_kv[:, l, 1, :].rearrange("p (h v) -> p h v", v=HD), ALU.add).then_inc(s_pev, 1)
                job += 1

        def attended(v, l):
            at = l * T

            def step(trip, u):
                if u % HALF == 0 and live(trip, u, 0):
                    half = u // HALF
                    v.wait_ge(s_dlb[half], 16 * (l * TRIPS + trip + 1))
                    v.tensor_scalar(mask[:, half, :, :].rearrange("p t e -> p (t e)"), dlb[:, half, :], part_dl[:, 0:1], MASKED,
                                    ALU.not_equal, ALU.mult).then_inc(s_mask, 1)
                if live(trip, u, 1):
                    t, slot, r = tile_of(trip, u, 1)
                    wait_freed(v, s_e, at + t - 1)
                    wait_freed(v, s_top, at + t)
                    v.tensor_tensor(xs[:, slot % 2, P:P + 1], top[:, (slot - 1) % U:(slot - 1) % U + 1],
                                    restart[:, bass.ds(t, 1)], ALU.min).then_inc(s_old, 1)
                if live(trip, u, 2):
                    t, slot, r = tile_of(trip, u, 2)
                    v.wait_ge(s_ep, at + t + 1)
                    wait_freed(v, s_o, at + t - 1)
                    v.tensor_copy(es[:, slot % 2, :], bank[4 + slot % 2][:, 0:P]).then_inc(s_es, 1)
                if live(trip, u, 1):
                    t, slot, r = tile_of(trip, u, 1)
                    v.wait_ge(s_mask, 2 * (l * TRIPS + r) + slot // HALF + 1)
                    v.wait_ge(s_old, at + t + 1)
                    v.wait_ge(s_sc, at + t + 1)
                    v.sem_inc(s_gatev)
                    v.tensor_tensor_reduce(xs[:, slot % 2, 0:P], bank[2 + slot % 2][:, 0:P], mask[:, slot // HALF, slot % HALF, :],
                                           1.0, xs[:, slot % 2, P:P + 1], ALU.add, ALU.max, top[:, slot:slot + 1]).then_inc(s_top, 1)
                    v.wait_ge(s_top, at + t + 1)
                    v.tensor_scalar(ntop[:, slot % 4:slot % 4 + 1], top[:, slot:slot + 1], FLOOR, -SCALE, ALU.max, ALU.mult)\
                        .then_inc(s_x, 1)
                if live(trip, u, 3):
                    t, slot, r = tile_of(trip, u, 3)
                    w = v.value_load(win_i[0:1, bass.ds(t, 1)], min_val=0, max_val=NW)
                    wait_freed(v, s_acc, at + t)
                    v.wait_ge(s_o, at + t + 1)
                    o = acc[:, bass.ds(w, 1), :].rearrange("p o v -> p (o v)")
                    v.scalar_tensor_tensor(o, o, et[:, slot % 4, P:P + 1], bank[6 + slot % 2][:, 0:VW], ALU.mult, ALU.add)\
                        .then_inc(s_acc, 1)

            run_steps(v, 3, step)

        def related(v, l):
            at = l * T

            def step(trip, u):
                if u % HALF == 0 and live(trip, u, 0):
                    half = u // HALF
                    if l or not isinstance(trip, int):
                        v.wait_ge(s_sp, at + trip * U + u - HALF)
                    v.tensor_tensor(oh[:, half, :, :],
                                    seg_f[:, bass.ds(trip * U + u, HALF)].unsqueeze(2).to_broadcast([P, HALF, SEG]),
                                    iota_seg[:, :].unsqueeze(1).to_broadcast([P, HALF, SEG]), ALU.is_equal).then_inc(s_oh, 1)
                if live(trip, u, 0):
                    t, slot, r = tile_of(trip, u, 0)
                    v.wait_ge(s_g[slot], 16 * ((2 + l) * TRIPS + r + 1))
                    v.wait_ge(s_ew, at + t + 1)
                    wait_freed(v, s_msg, at + t - 1)
                    v.tensor_tensor(prod[:, slot % 2, :], bank[slot % 2][:, 0:D], gring[:, slot, 0:D], ALU.mult)\
                        .then_inc(s_prod, 1)
                if live(trip, u, 3):
                    t, slot, r = tile_of(trip, u, 3)
                    w = v.value_load(win_i[0:1, bass.ds(t, 1)], min_val=0, max_val=NW)
                    if l == 0:
                        v.wait_ge(s_sp, at + t + 1)
                        wait_freed(v, s_rc, at + t)
                        c = cnt_t[:, bass.ds(w, 1)]
                        v.tensor_tensor(c, c, bank[2 + slot % 2][0:SEG, 2 * SEG:2 * SEG + 1], ALU.add).then_inc(s_rc, 1)
                    wait_freed(v, s_racc, at + t)
                    v.wait_ge(s_sp, at + t + 1)
                    if isinstance(trip, int) and t == 0 and l:
                        v.wait_ge(s_clr, 3 + l * NT)
                    o = racc[:, :, bass.ds(w * W, W)]
                    v.tensor_tensor(o, o, bank[2 + slot % 2][:, 0:2 * SEG].rearrange("p (s d) -> p s d", d=W), ALU.add).then_inc(s_racc, 1)

            run_steps(v, 3, step)

        block = ctx.enter_context(nc.Block())

        @block.gpsimd
        def _(g):
            gpsimd_program(g)

        @block.sync
        def _(sp):
            sync_program(sp)

        @block.tensor
        def _(pe):
            tensor_program(pe)

        @block.scalar
        def _(act):
            scalar_program(act)

        @block.vector
        def _(v):
            vector_program(v)


def kernel(**inputs):
    import numpy as np
    import concourse.bacc as bacc
    from concourse.bass_utils import run_bass_kernel_spmd

    nc = bacc.Bacc("TRN2", target_bir_lowering=False, num_devices=1)
    arrays, aps = {}, {}
    for name, value in inputs.items():
        array = np.ascontiguousarray(value)
        arrays["in_" + name] = array
        aps[name] = nc.dram_tensor("in_" + name, array.shape, mybir.dt.from_np(array.dtype), kind="ExternalInput").ap()
    out = nc.dram_tensor("out", (N, D), F32, kind="ExternalOutput").ap()
    build(nc, aps, out)
    return run_bass_kernel_spmd(nc, [arrays], core_ids=[0]).results[0]["out"]
```

```python
from contextlib import ExitStack

import concourse.bass as bass
from concourse import mybir

ALU = mybir.AluOpType
ACT = mybir.ActivationFunctionType
AX = mybir.AxisListType
F32 = mybir.dt.float32
BF16 = mybir.dt.bfloat16
I32 = mybir.dt.int32

P = 128
N, D = 3125, 256
E = 53125
HEADS, HD = 4, 64
VW = HD + 1
ND = 32
NREL = 3
W = 32
NW = -(-N // W)
NT = -(-N // P)
WPT = P // W
NWP = NT * WPT
NP = NT * P
NTAIL = N - (NT - 1) * P
T = (E + NW * (P - 1)) // P
U = 16
Q = 4
QUADS = U // Q
RL = 4
TRIPS = T // U
EP, EJ = 125, 425
CG = 5
G = EJ // CG
GU = 5
GTRIPS = G // GU
REC = 36
C_SRC, C_DL, C_SEG = ND, ND + 1, ND + 2
SEG = NREL * W
KVW = D + HEADS * VW
UC = 64
NUC = T // UC
NB = -(-NP // 512)
EPS = 1e-5
SCALE = HD ** -0.5
MASKED, RESTART, KEEP = 1e30, 1e29, -1e30
assert EP * EJ == E and T % U == 0 and T == TRIPS * U and G == GTRIPS * GU and NWP > NW and T % P == 0


class Count:

    def __init__(self, sem):
        self.sem, self.n = sem, 0

    def inc(self, instruction, by=1):
        instruction.then_inc(self.sem, by)
        self.n += by
        return self.n


def live(trip, u, lag):
    return not isinstance(trip, int) or 0 <= trip * U + u - lag < T


def run_steps(eng, lag, step):
    for u in range(U):
        step(0, u)
    with eng.Fori(1, TRIPS) as trip:
        for u in range(U):
            step(trip, u)
    for u in range(lag):
        step(TRIPS, u)


def tile_of(trip, u, lag):
    return trip * U + (u - lag), (u - lag) % U, trip if u >= lag else trip - 1


def quads_before(trip, u):
    return trip * (QUADS // 2) + u // Q // 2


def wait_freed(eng, sem, value):
    if not isinstance(value, int) or value > 0:
        eng.wait_ge(sem, value)


def build(nc, a, out):
    ctx = ExitStack()
    with ctx:
        def sb(name, shape, dt):
            return ctx.enter_context(nc.sbuf_tensor(name, shape, dt))

        def sem(name):
            return ctx.enter_context(nc.semaphore(name))

        def dram(name, shape, dt=F32):
            return nc.dram_tensor(name, shape, dt, kind="Internal").ap()

        rec_d = dram("edge_records", (P * T, REC))
        eat_d = dram("edge_attr_T", (TRIPS, P, QUADS * P))
        dlt_d = dram("node_in_window_T", (T, P), BF16)
        kv_d = [dram(f"kv_rows{l}", (NP, KVW)) for l in range(2)]
        h_d = [dram(f"h_rows{l}", (NP, D)) for l in range(3)]

        ident = sb("ident", [P, P], F32)
        before = sb("before", [EP, EP], BF16)
        ones_b = sb("ones_b", [P, P], BF16)
        ones_f = sb("ones_f", [P, 1], F32)
        zeros_b = sb("zeros_b", [EP, CG * NW], BF16)
        iota_w = sb("iota_w", [P, NW], F32)
        ones_w = sb("ones_w", [P, NW], F32)
        iota_seg = sb("iota_seg", [P, SEG], F32)
        part_i = sb("part_i", [P, 1], I32)
        part_m = sb("part_m", [P, 1], I32)
        part_dl = sb("part_dl", [P, 1], F32)

        src_i = sb("src_i", [P, T], I32)
        seg_f = sb("seg_f", [P, T], F32)
        dl_f = sb("dl_f", [P, T], F32)
        restart = sb("restart", [P, T], F32)
        win_i = sb("win_i", [1, T], I32)

        wts = sb("wts", [P, 2, 4, 2, D], F32)
        bias_q = sb("bias_q", [P, 2, 2], F32)
        bias_s = sb("bias_s", [P, 2, 2], F32)
        gamma = sb("gamma", [P, 2, 2], F32)
        beta = sb("beta", [P, 2, 2], F32)
        bias_kv = sb("bias_kv", [P, 2, 2, D], F32)
        bias_r = sb("bias_r", [P, 3, D], F32)
        nnw = sb("nnw", [P, 2, ND], F32)
        nnwt = sb("nnwt", [P, D], F32)

        ht_flat = sb("ht", [P, 2 * NP], F32)
        ht = ht_flat[:, :].rearrange("p (c n) -> p c n", c=2)
        REGION = 2 * NP + NWP * P + NWP * VW
        region = sb("region", [P, REGION], F32)
        at = 0
        st = region[:, 0:2 * NP].rearrange("p (c n) -> p c n", c=2)
        qblk = region[:, 2 * NP:2 * NP + NWP * P].rearrange("p (w c m) -> p w c m", c=2, m=2 * W)
        at = 2 * NP + NWP * P
        acc = region[:, at:at + NWP * VW].rearrange("p (w v) -> p w v", v=VW)
        chunk = region[:, at:at + 2 * UC * REC].rearrange("p (b t r) -> p b t r", b=2, r=REC)
        x1 = region[:, at:at + NT * D].rearrange("p (i f) -> p i f", f=D)
        racc = region[:, 0:2 * NREL * NP].rearrange("p (s n) -> p s n", n=NP)
        assert 2 * NREL * NP <= at and 2 * UC * REC <= NWP * VW and NT * D <= NWP * VW
        gring = sb("gring", [P, U // 2, KVW], F32)
        gring_ht = ht_flat[:, 0:U // 2 * KVW].rearrange("p (u k) -> p u k", k=KVW)
        gring_r = gring[:, :, :].rearrange("p u k -> p (u k)")[:, 0:U * D].rearrange("p (u f) -> p u f", f=D)

        def kv_slot(u):
            return gring[:, u, :] if u < U // 2 else gring_ht[:, u - U // 2, :]

        xr = sb("xr", [P, 3, D], F32)
        rows = sb("rows", [P, 2 * KVW], F32)
        kvrow = rows[:, :].rearrange("p (s k) -> p s k", s=2)
        orow = rows[:, 0:4 * D].rearrange("p (s f) -> p s f", s=4)
        assert 4 * D <= 2 * KVW
        gidx = sb("gidx", [P, QUADS, Q], I32)

        sort_at = [at]

        def sort_space(n, dt=F32):
            space = region[0:EP, sort_at[0]:sort_at[0] + n]
            sort_at[0] += n
            return space if dt == F32 else space.bitcast(dt)

        dst_e, typ_e, src_e, int_e = (sort_space(EJ, I32) for _ in range(4))
        row_e = sort_space(EJ, I32)
        win_f = sort_space(EJ)
        meta = sort_space(EJ * (REC - ND)).rearrange("p (j r) -> p j r", r=REC - ND)
        onehot_w = sort_space(GU * CG * NW // 2, BF16).rearrange("p (g c w) -> p g c w", g=GU, c=CG)
        rank = sort_space(CG * NW).rearrange("p (c w) -> p c w", c=CG)
        assert sort_at[0] <= REGION
        run_tot = sb("run_tot", [P, NW], F32)
        cnt_w = sb("cnt_w", [P, NW], F32)
        tiles_i = sb("tiles_i", [P, NW], I32)
        tiles_f = sb("tiles_f", [P, NW], F32)
        tend = sb("tend", [P, NW], F32)
        tend_c = sb("tend_c", [NW, 1], F32)
        pos_f = sb("pos_f", [EP, CG], F32)
        pos_i = sb("pos_i", [EP, CG], I32)
        pos_lo = sb("pos_lo", [EP, CG], I32)
        pos_hi = sb("pos_hi", [EP, CG], I32)
        blank = gring[:, 0:5, :].rearrange("p u k -> p (u k)")[:, 0:UC * REC].rearrange("p (t r) -> p t r", r=REC)
        iota_t = gring[0:NW, 5, 0:T]
        tile_w = ht[:, 0, 0:T]
        ended = ht[0:NW, 1, 0:T // 2].bitcast(BF16)
        attrs = ht_flat[:, 0:2 * UC * ND].rearrange("p (s m) -> p s m", s=2)
        behind = U // 2 * KVW
        eat_out = ht_flat[:, behind:behind + 8 * P].rearrange("p (s m) -> p s m", s=2)
        et = ht_flat[:, behind:behind + 2 * RL * (P + 1)].rearrange("p (s e) -> p s e", e=P + 1)
        assert 2 * UC * ND <= behind and 2 * RL * (P + 1) >= 8 * P
        behind += 2 * RL * (P + 1)
        dlt_out = ht_flat[:, behind:behind + T // 2].bitcast(BF16).rearrange("p (q e) -> p q e", e=P)
        behind += T // 2
        xs = ht_flat[:, behind:behind + RL * (P + 1)].rearrange("p (s e) -> p s e", e=P + 1)
        behind += RL * (P + 1)
        es = ht_flat[:, behind:behind + 2 * P].rearrange("p (s m) -> p s m", s=2)
        assert behind + 2 * P <= 2 * NP

        rings = sb("rings", [P, 2 * 2 * P + U * 4 * W + Q * P + 2 * Q * P], F32)
        ring_at = [0]

        def ring_space(n):
            space = rings[:, ring_at[0]:ring_at[0] + n]
            ring_at[0] += n
            return space

        kt = ring_space(4 * P).rearrange("p (s m) -> p s m", s=2)
        qs = ring_space(U * 4 * W).rearrange("p (s c m) -> p s c m", s=U, c=2)
        dlb = ring_space(Q * P).bitcast(BF16).rearrange("p (h m) -> p h m", h=2)
        mask = ring_space(2 * Q * P).rearrange("p (h t e) -> p h t e", h=2, t=Q)
        stage = rings[0:EP, 0:GU * CG * REC].rearrange("p (g c r) -> p g c r", g=GU, c=CG)
        stage_row = rings[0:EP, GU * CG * REC:GU * CG * (REC + 1)].bitcast(I32).rearrange("p (g c) -> p g c", g=GU)
        ring_at = [0]
        eat = ring_space(2 * Q * P).rearrange("p (h t e) -> p h t e", h=2, t=Q)
        oh = ring_space(2 * Q * SEG).rearrange("p (h t s) -> p h t s", h=2, t=Q)
        prod = ring_space(RL * D).rearrange("p (s f) -> p s f", s=RL)
        msg = ring_space(RL * D).rearrange("p (s f) -> p s f", s=RL)
        ntop = sb("ntop", [P, U], F32)
        rden = sb("rden", [P, NWP], F32)
        stats = sb("stats", [P, 2, NB, 6], F32)
        mv = sb("mv", [P, 2, 2], F32)
        bn_t = sb("bn_t", [P, 2, 4], F32)
        ln_st = sb("ln_st", [P, NT, 6], F32)
        ln_mv = sb("ln_mv", [P, NT, 2], F32)
        ln_sd = sb("ln_sd", [P, NT, 2], F32)

        cnt_t = sb("cnt_t", [SEG, NWP], F32)
        inv_t = sb("inv_t", [P, NREL, NT], F32)

        bank = [ctx.enter_context(nc.psum_tensor(f"bank{i}", [P, 512], F32)) for i in range(8)]

        s_edges = sem("s_edges")
        s_small = sem("s_small")
        s_wr = [sem(f"s_wr{l}") for l in range(3)]
        s_pool = sem("s_pool")
        s_vec = sem("s_vec")
        s_blank = sem("s_blank")
        s_ohw = sem("s_ohw")
        s_cntw = sem("s_cntw")
        s_rank = sem("s_rank")
        s_row = sem("s_row")
        s_stage = sem("s_stage")
        s_sea = [sem(f"s_sea{i}") for i in range(GU)]
        s_scat = [sem(f"s_scat{i}") for i in range(GU)]
        s_chunk = [sem(f"s_chunk{i}") for i in range(2)]
        s_unv = sem("s_unv")
        s_attrs = sem("s_attrs")
        s_unp = sem("s_unp")
        s_eato = [sem(f"s_eato{i}") for i in range(2)]
        s_eatc = sem("s_eatc")
        s_dlt = sem("s_dlt")
        s_xr = [sem(f"s_xr{i}") for i in range(3)]
        s_proj = sem("s_proj")
        s_pev = sem("s_pev")
        s_kvo = [sem(f"s_kvo{i}") for i in range(2)]
        s_idx = sem("s_idx")
        s_g = [sem(f"s_g{i}") for i in range(U)]
        s_gate = sem("s_gate")
        s_gatev = sem("s_gatev")
        s_q = [sem(f"s_q{i}") for i in range(U)]
        s_dlb = [sem(f"s_dlb{i}") for i in range(2)]
        s_mask = sem("s_mask")
        s_ktp, s_kt, s_sc, s_old, s_top = (sem(n) for n in ("s_ktp", "s_kt", "s_sc", "s_old", "s_top"))
        s_e, s_ep, s_es, s_o, s_acc = (sem(n) for n in ("s_e", "s_ep", "s_es", "s_o", "s_acc"))
        s_tr = sem("s_tr")
        s_add = sem("s_add")
        s_h = sem("s_h")
        s_eat = [sem(f"s_eat{i}") for i in range(2)]
        s_oh, s_ew, s_prod, s_msg, s_sp, s_racc, s_rc = (sem(n) for n in ("s_oh", "s_ew", "s_prod", "s_msg", "s_sp", "s_racc", "s_rc"))
        s_clr = sem("s_clr")
        s_dn = sem("s_dn")
        s_dv = sem("s_dv")
        s_htp = sem("s_htp")
        s_ht = sem("s_ht")
        s_ho = [[sem(f"s_ho{l}_{i}") for i in range(4)] for l in range(2)]
        s_ln = sem("s_ln")
        s_out = sem("s_out")
        pool_n, vec_n = Count(s_pool), Count(s_vec)
        events = {}

        def event(name):
            if name not in events:
                events[name] = sem("e_" + name)
            return events[name]


        ROWSTEPS = 8
        NPROJ = [NT + 2 * 2 * NB + NT, 2 * 2 * NB + NT]
        LAG_EXP, LAG_WT, LAG_O, LAG_ACC = 2, 3, 4, 5
        LAG_SUM, LAG_RACC = 2, 3
        STEPD = 4

        def gpsimd_program(g):
            def step(ins):
                return pool_n.inc(ins)

            step(g.memset(ident[:, :], 0.0))
            step(g.memset(before[:, :], 1.0))
            step(g.memset(ones_b[:, :], 1.0))
            step(g.memset(ones_f[:, :], 1.0))
            step(g.memset(ones_w[:, :], 1.0))
            step(g.memset(zeros_b[:, :], 0.0))
            step(g.memset(nnwt[:, :], 0.0))
            step(g.iota(iota_w[:, :], pattern=[[1, NW]], base=0, channel_multiplier=0,
                        allow_small_or_imprecise_dtypes=True))
            step(g.iota(iota_seg[:, :], pattern=[[1, SEG]], base=0, channel_multiplier=0,
                        allow_small_or_imprecise_dtypes=True))
            step(g.iota(iota_t, pattern=[[1, T]], base=0, channel_multiplier=0,
                        allow_small_or_imprecise_dtypes=True))
            step(g.iota(part_i[:, :], pattern=[[0, 1]], base=0, channel_multiplier=1))
            step(g.memset(meta[:, :, REC - ND - 1:REC - ND], 0.0))
            step(g.memset(blank, 0.0))
            g.wait_ge(s_pool, pool_n.n)
            step(g.affine_select(out=ident[:, :], in_=ident[:, :], compare_op=ALU.not_equal, fill=1.0,
                                 base=0, pattern=[[-1, P]], channel_multiplier=1))
            step(g.affine_select(out=before[:, :], in_=before[:, :], compare_op=ALU.is_gt, fill=0.0,
                                 base=0, pattern=[[1, EP]], channel_multiplier=-1))
            step(g.memset(blank[:, :, C_DL:C_DL + 1], float(W)))
            g.wait_ge(s_pool, pool_n.n)
            g.memset(blank[:, :, C_SEG:C_SEG + 1], float(SEG)).then_inc(event("consts"), 1)
            step(g.memset(xr[:, 2, :], 0.0))
            step(g.memset(kvrow, 1.0))
            g.wait_ge(s_pool, pool_n.n)
            g.memset(qblk, 0.0).then_inc(event("cleared"), 1)

            g.wait_ge(s_blank, 16 * NUC)

            def scatter(trip, slot):
                g.wait_ge(s_sea[slot], 16 * (trip + 1))
                g.wait_ge(s_stage, 2 * (trip * GU + slot) + 2)
                g.sem_inc(s_gate)
                for c in range(CG):
                    g.indirect_dma_start(
                        out=rec_d, out_offset=bass.IndirectOffsetOnAxis(ap=stage_row[:, slot, c:c + 1], axis=0),
                        in_=stage[:, slot, c, :], in_offset=None).then_inc(s_scat[slot], 16)

            for slot in range(GU):
                scatter(0, slot)
            with g.Fori(1, GTRIPS) as trip:
                for slot in range(GU):
                    scatter(trip, slot)

            def gather_layer(seq, rows, slot_rows, used, used_base):
                def step(trip, u):
                    quad = u // Q
                    if u % Q == 0:
                        if seq or not isinstance(trip, int):
                            for k in range(u, u + Q):
                                g.wait_ge(s_g[k], 16 * (seq * TRIPS + trip))
                        g.tensor_copy(gidx[:, quad, :], src_i[:, bass.ds(trip * U + u, Q)]).then_inc(s_idx, 1)
                        g.wait_ge(s_idx, (seq * TRIPS + trip) * QUADS + quad + 1)
                        g.sem_inc(s_gate)
                    if not isinstance(trip, int):
                        g.wait_ge(used, used_base + trip * U + u - U + 1)
                        g.sem_inc(s_gate)
                    g.indirect_dma_start(
                        out=slot_rows(u), out_offset=None, in_=rows,
                        in_offset=bass.IndirectOffsetOnAxis(ap=gidx[:, quad, u % Q:u % Q + 1], axis=0)).then_inc(s_g[u], 16)

                run_steps(g, 0, step)

            for l in range(2):
                g.wait_ge(event("tables"), l + 1)
                for slot in range(2):
                    g.wait_ge(s_kvo[slot], 16 * ((NT + 1 - slot) // 2) * (l + 1))
                if l:
                    g.wait_ge(s_o, l * T)
                g.sem_inc(s_gate)
                gather_layer(l, kv_d[l], kv_slot, s_o, l * T)

            g.wait_ge(event("normed"), 2)
            g.wait_ge(s_tr, 2 * NT)
            g.memset(racc, 0.0).then_inc(s_clr, 1)
            g.memset(cnt_t[:, :], 0.0).then_inc(s_clr, 1)
            g.wait_ge(s_clr, 2)
            g.memset(eat, 1.0).then_inc(s_clr, 1)
            g.wait_ge(s_clr, 3)
            for l in range(3):
                if l == 0:
                    g.wait_ge(s_h, 16 * NT)
                else:
                    for i in range(4):
                        g.wait_ge(s_ho[l - 1][i], 16 * len(range(i, NT, 4)))
                g.wait_ge(s_o, 2 * T)
                if l:
                    g.wait_ge(s_prod, l * T)
                g.sem_inc(s_gate)
                gather_layer(2 + l, h_d[l], lambda u: gring_r[:, u, :], s_prod, l * T)
                if l < 2:
                    for i in range(NT):
                        g.wait_ge(s_dn, l * NT + i + 1)
                        g.memset(racc[:, :, i * P:(i + 1) * P], 0.0).then_inc(s_clr, 1)

        def sync_program(sp):
            for t, n in ((dst_e, "dst"), (typ_e, "edge_type_3"), (src_e, "src")):
                sp.dma_start(t[:, :], a[n].rearrange("(p j) -> p j", p=EP)).then_inc(s_edges, 16)
            sp.wait_ge(event("consts"), 1)
            rec_v = rec_d.rearrange("(p t) r -> p t r", p=P)
            for k in range(NUC):
                sp.dma_start(rec_v[:, k * UC:(k + 1) * UC, :], blank).then_inc(s_blank, 16)

            def weights(slot, k, w, done):
                sp.dma_start(wts[:, slot, k, :, :], w.rearrange("(c p) n -> p c n", p=P)).then_inc(done, 16)

            for l in range(2):
                for k, n in enumerate("qkvs"):
                    weights(l, k, a[f"L0_gnn_w{l + 1}{n}"], s_small)
                for t, n in ((bias_q, "b{}q"), (bias_s, "b{}s"), (gamma, "g{}"), (beta, "be{}")):
                    sp.dma_start(t[:, l, :], a["L0_gnn_" + n.format(l + 1)].rearrange("(c p) -> p c", p=P),
                                 allow_slow_non_contiguous=True).then_inc(s_small, 16)
                for k, n in enumerate("kv"):
                    sp.dma_start(bias_kv[:, l, k, :], a[f"L0_gnn_b{l + 1}{n}"].partition_broadcast(P)).then_inc(s_small, 16)
            for l in range(3):
                sp.dma_start(bias_r[:, l, :], a["L1_gnn_bias"][l, :].partition_broadcast(P)).then_inc(s_small, 16)
            sp.dma_start(nnw[:, :, :], a["L1_gnn_nn_w"].rearrange("(c p) j -> p c j", p=P)).then_inc(s_small, 16)
            sp.dma_start(nnwt[ND:ND + 1, :], a["L1_gnn_nn_b"].rearrange("(o f) -> o f", o=1)).then_inc(s_small, 16)

            def load_rows(i, use, sem_used, used):
                tail = i == NT - 1
                slot = 2 if tail else i % 2
                if used is not None:
                    sp.wait_ge(sem_used, used)
                n = NTAIL if tail else P
                sp.dma_start(xr[0:n, slot, :], a["x"][i * P:i * P + n, :]).then_inc(s_xr[slot], 16)

            sp.wait_ge(event("cleared"), 1)
            for i in range(NT):
                load_rows(i, 0, s_proj, i - 1 if 2 <= i < NT - 1 else None)
            for l in range(2):
                if l == 0:
                    kv_base = NT + 4 * NB
                else:
                    kv_base = NPROJ[0] + 4 * NB
                for i in range(NT):
                    sp.wait_ge(s_pev, kv_base + i + 1)
                    sp.dma_start(kv_d[l][i * P:(i + 1) * P, :], kvrow[:, i % 2, :]).then_inc(s_kvo[i % 2], 16)
                if l == 0:
                    for slot in range(GU):
                        sp.wait_ge(s_scat[slot], 16 * CG * GTRIPS)
                    for k in range(NUC):
                        if k >= 2:
                            sp.wait_ge(s_unv, 3 * (k - 1))
                            sp.wait_ge(s_attrs, k - 1)
                        sp.dma_start(chunk[:, k % 2, :, :], rec_v[:, k * UC:(k + 1) * UC, :]).then_inc(s_chunk[k % 2], 16)
                    sp.wait_ge(event("dlt"), 1)
                    sp.dma_start(dlt_d.rearrange("(q t) p -> t q p", t=P), dlt_out[:, :, :]).then_inc(s_dlt, 16)
                    sp.wait_ge(s_dlt, 16)
                sp.wait_ge(s_pev, sum(NPROJ[:l + 1]))

                def step(trip, u):
                    t = trip * U + u
                    if u % Q == 0:
                        quad = (l * TRIPS + trip) * QUADS + u // Q
                        wait_freed(sp, s_mask, quad - 1)
                        sp.dma_start(dlb[:, u // Q % 2, :], dlt_d[bass.ds(t, Q), :].rearrange("t p -> (t p)")
                                     .partition_broadcast(P)).then_inc(s_dlb[u // Q % 2], 16)
                    w = sp.value_load(win_i[0:1, bass.ds(t, 1)], min_val=0, max_val=NW)
                    if l or not isinstance(trip, int):
                        sp.wait_ge(s_sc, l * T + t - U + 1)
                    sp.dma_start(qs[:, u, :, :], qblk[:, bass.ds(w, 1), :, :].rearrange("p o c m -> p (o c) m"))\
                        .then_inc(s_q[u], 16)

                run_steps(sp, 0, step)
            for i in range(NT):
                load_rows(i, 1, s_add, 4 * 2 * NT + i - 1 if 2 <= i < NT - 1 else (4 * 2 * NT if i < 2 else None))
            for l in range(2):
                load_relational(sp, l)
            for i in range(NT):
                sp.wait_ge(s_ln, i + 1)
                sp.dma_start(h_d[0][i * P:(i + 1) * P, :], x1[:, i, :]).then_inc(s_h, 16)
            for l in range(3):
                def step(trip, u):
                    if u % Q:
                        return
                    quad = u // Q
                    wait_freed(sp, s_ew, l * T + trip * U + u - Q)
                    sp.dma_start(eat[0:ND, quad % 2, :, :],
                                 eat_d[bass.ds(trip, 1), :, quad * P:(quad + 1) * P]
                                 .rearrange("o (q j) e -> (o j) q e", q=Q)).then_inc(s_eat[quad % 2], 16)

                if l == 0:
                    sp.wait_ge(s_clr, 3)
                    for i in range(2):
                        sp.wait_ge(s_eato[i], 16 * NUC * 2)
                run_steps(sp, 0, step)
                if l < 2:
                    for i in range(NT):
                        sp.wait_ge(s_dv, STEPD * (l * NT + i + 1))
                        sp.dma_start(h_d[l + 1][i * P:(i + 1) * P, :], orow[:, i % 4, :]).then_inc(s_ho[l][i % 4], 16)
                    if l == 0:
                        load_relational(sp, 2)
            for i in range(NT):
                n = NTAIL if i == NT - 1 else P
                sp.wait_ge(s_ln, NT + i + 1)
                sp.dma_start(out[i * P:i * P + n, :], x1[0:n, i, :]).then_inc(s_out, 16)
            sp.wait_ge(s_out, 16 * NT)

        def load_relational(sp, l):
            if l == 0:
                sp.wait_ge(s_proj, sum(NPROJ))
            if l == 2:
                sp.wait_ge(s_dn, NT)
            for r in range(NREL):
                sp.dma_start(wts[:, l % 2, r, :, :], a["L1_gnn_W"][l, r, :, :].rearrange("(c p) n -> p c n", p=P))\
                    .then_inc(s_wr[l], 16)
            sp.dma_start(wts[:, l % 2, NREL, :, :], a["L1_gnn_root"][l, :, :].rearrange("(c p) n -> p c n", p=P))\
                .then_inc(s_wr[l], 16)

        def tensor_program(pe):
            pe.wait_ge(event("consts"), 1)
            pe.wait_ge(s_small, 16 * 25)
            for c in range(2):
                ins = pe.transpose(bank[7][0:ND, c * P:(c + 1) * P], nnw[:, c, :], ident[:, :])
            ins.then_inc(event("nnw"), 1)

            cnt = bank[6][:, 0:CG * NW]
            pe.matmul(cnt, ones_b[0:EP, :], zeros_b[:, :], start=True, stop=False)

            def count(trip, slot):
                pe.wait_ge(s_ohw, trip * GU + slot + 1)
                pe.matmul(cnt, ones_b[0:EP, :], onehot_w[:, slot, :, :].rearrange("p c w -> p (c w)"),
                          start=False, stop=False).then_inc(s_cntw, 1)

            for slot in range(GU):
                count(0, slot)
            with pe.Fori(1, GTRIPS) as trip:
                for slot in range(GU):
                    count(trip, slot)
            pe.matmul(cnt, ones_b[0:EP, :], zeros_b[:, :], start=False, stop=True)\
                .then_inc(event("counted"), 1)
            pe.wait_ge(event("tend"), 1)
            pe.transpose(bank[5][0:NW, 0:P], tend[:, :], ident[:, :]).then_inc(event("tend_c"), 1)
            pe.wait_ge(event("ended"), 1)
            pe.matmul(bank[7][:, 0:T], ones_b[0:NW, :], ended, start=True, stop=True).then_inc(event("tile_w"), 1)
            pe.wait_ge(event("tend_copied"), 1)

            def ranks(trip, slot):
                g = trip * GU + slot
                pe.wait_ge(s_ohw, G + g + 1)
                if not isinstance(trip, int):
                    pe.wait_ge(s_row, ROWSTEPS * (g - GU + 1))
                r = bank[slot][0:EP, 0:CG * NW]
                pe.matmul(r, before[:, :], onehot_w[:, slot, :, :].rearrange("p c w -> p (c w)"), start=True, stop=False)
                for c in range(CG - 1):
                    left = CG - 1 - c
                    pe.matmul(r[:, (c + 1) * NW:].rearrange("p (c w) -> p c w", w=NW), ones_b[0:EP, 0:EP],
                              onehot_w[:, slot, c:c + 1, :].to_broadcast([EP, left, NW]), start=False, stop=left == 1)
                wait_freed(pe, s_row, ROWSTEPS * (g - 1))
                for c in range(CG):
                    ins = pe.matmul(bank[5 + slot % 3][0:EP, 0:NW], ones_b[0:EP, 0:EP], onehot_w[:, slot, c, :],
                                    start=c == 0, stop=c == CG - 1)
                ins.then_inc(s_rank, 1)

            for slot in range(GU):
                ranks(0, slot)
            with pe.Fori(1, GTRIPS) as trip:
                for slot in range(GU):
                    ranks(trip, slot)
            pe.wait_ge(s_row, ROWSTEPS * G)

            for l in range(2):
                project(pe, l)
                if l == 0:
                    pe.wait_ge(s_pev, NPROJ[0])
                    for k in range(NUC):
                        pe.wait_ge(s_attrs, k + 1)
                        for b in range(4):
                            if k:
                                pe.wait_ge(s_eatc, 4 * (k - 1) + b + 1)
                            for q in range(4):
                                t = 16 * b + 4 * q
                                ins = pe.transpose(bank[b][:, q * P:(q + 1) * P],
                                                   attrs[:, k % 2, t * ND:(t + 4) * ND], ident[:, :])
                            ins.then_inc(s_unp, 1)
                    pe.wait_ge(s_unv, 3 * NUC)
                    for q in range(T // P):
                        ins = pe.transpose(bank[4][:, q * P:(q + 1) * P], dl_f[:, q * P:(q + 1) * P], ident[:, :])
                    ins.then_inc(event("dl_t"), 1)
                    pe.wait_ge(s_eatc, 4 * NUC)
                    pe.wait_ge(event("dlt"), 1)
                else:
                    pe.wait_ge(s_pev, sum(NPROJ))
                attention_tiles(pe, l)
                pe.wait_ge(event("divided"), l + 1)
                for j in range(NT):
                    if j >= 2:
                        pe.wait_ge(s_add, 4 * (l * NT + j - 1))
                    for k in range(WPT):
                        ins = pe.transpose(bank[j % 2][0:HD, k * P:(k + 1) * P], acc[:, WPT * j + k, 0:HD], ident[:, :])
                    ins.then_inc(s_tr, 1)

            pe.wait_ge(event("leaky"), 2)
            pe.wait_ge(s_add, 4 * 2 * NT)
            for i in range(NT):
                if i >= 2:
                    pe.wait_ge(s_add, 4 * 2 * NT + i - 1)
                for c in range(2):
                    ins = pe.transpose(bank[i % 2][:, c * P:(c + 1) * P], ht[:, c, i * P:(i + 1) * P], ident[:, :])
                ins.then_inc(s_tr, 1)
            for i in range(NT):
                pe.wait_ge(s_ln, i + 1)
                features(pe, i, x1[:, i, :], i)

            for l in range(3):
                pe.wait_ge(s_ht, NT * (l + 1))
                if l == 0:
                    pe.wait_ge(event("nnwt"), 1)
                    pe.wait_ge(s_clr, 3)
                else:
                    pe.wait_ge(s_dv, STEPD * l * NT)
                relation_tiles(pe, l)
                pe.wait_ge(s_wr[l], 16 * (NREL + 1))
                pe.wait_ge(s_racc, (l + 1) * T)
                if l == 0:
                    pe.wait_ge(s_rc, T)
                    for k in range(WPT):
                        for r in range(NREL):
                            ins = pe.matmul(bank[7][k * W:(k + 1) * W, r * NT:(r + 1) * NT],
                                            ident[0:SEG, r * W:(r + 1) * W], cnt_t[:, k:NWP:WPT], start=True, stop=True)
                    ins.then_inc(event("cnt"), 1)
                for i in range(NT):
                    n = l * NT + i
                    if n >= 2:
                        pe.wait_ge(s_dv, STEPD * (n - 1))
                    b = 2 * (n % 2)
                    for r in range(-1, NREL):
                        o = bank[b + (r + 1) // 2][:, (r + 1) % 2 * D:((r + 1) % 2 + 1) * D]
                        for c in range(2):
                            lhs = ht[:, c, i * P:(i + 1) * P] if r < 0 else \
                                racc[:, c * NREL + r, i * P:(i + 1) * P]
                            ins = pe.matmul(o, lhs, wts[:, l % 2, r if r >= 0 else NREL, c, :], start=c == 0, stop=c == 1)
                    ins.then_inc(s_dn, 1)
                    if l < 2 and i:
                        pe.wait_ge(s_dv, STEPD * n)
                        features(pe, i - 1, orow[:, (i - 1) % 4, :], (l + 1) * NT + i - 1)
                if l < 2:
                    pe.wait_ge(s_dv, STEPD * (l + 1) * NT)
                    features(pe, NT - 1, orow[:, (NT - 1) % 4, :], (l + 1) * NT + NT - 1)

        def features(pe, i, rows, n):
            if n >= 2:
                pe.wait_ge(s_ht, n - 1)
            for c in range(2):
                ins = pe.transpose(bank[4 + n % 2][:, c * P:(c + 1) * P], rows[:, c * P:(c + 1) * P], ident[:, :])
            ins.then_inc(s_htp, 1)

        def project(pe, l):
            job = sum(NPROJ[:l])

            def free(job):
                if job >= 4:
                    pe.wait_ge(s_pev, job - 3)
                return bank[job % 4]

            if l == 0:
                for i in range(NT):
                    slot = 2 if i == NT - 1 else i % 2
                    pe.wait_ge(s_xr[slot], 16 * (1 if slot == 2 else i // 2 + 1))
                    b = free(job)
                    for c in range(2):
                        ins = pe.transpose(b[:, c * P:(c + 1) * P], xr[:, slot, c * P:(c + 1) * P], ident[:, :])
                    ins.then_inc(s_proj, 1)
                    job += 1
                pe.wait_ge(s_pev, NT)
            else:
                pe.wait_ge(event("leaky"), 1)
                pe.wait_ge(s_add, 4 * NT)
            for k in (0, 3):
                for c in range(2):
                    for nb in range(NB):
                        n = min(512, NP - nb * 512)
                        b = free(job)
                        for kc in range(2):
                            ins = pe.matmul(b[:, 0:n], wts[:, l, k, kc, c * P:(c + 1) * P],
                                            ht[:, kc, nb * 512:nb * 512 + n], start=kc == 0, stop=kc == 1)
                        ins.then_inc(s_proj, 1)
                        job += 1
            for i in range(NT):
                b = free(job)
                for kc in range(2):
                    ins = pe.matmul(b[:, :].rearrange("p (k n) -> p k n", k=2), ht[:, kc, i * P:(i + 1) * P],
                                    wts[:, l, 1:3, kc, :], start=kc == 0, stop=kc == 1)
                ins.then_inc(s_proj, 1)
                job += 1

        def attention_tiles(pe, l):
            at = l * T

            def step(trip, u):
                if live(trip, u, 0):
                    t, slot, r = tile_of(trip, u, 0)
                    pe.wait_ge(s_g[slot], 16 * (l * TRIPS + r + 1))
                    wait_freed(pe, s_kt, at + t - 1)
                    for c in range(2):
                        ins = pe.transpose(bank[slot % 2][:, c * P:(c + 1) * P], kv_slot(slot)[:, c * P:(c + 1) * P], ident[:, :])
                    ins.then_inc(s_ktp, 1)
                if live(trip, u, 1):
                    t, slot, r = tile_of(trip, u, 1)
                    pe.wait_ge(s_q[slot], 16 * (l * TRIPS + r + 1))
                    pe.wait_ge(s_kt, at + t + 1)
                    wait_freed(pe, s_top, at + t - 1)
                    for c in range(2):
                        ins = pe.matmul(bank[2 + slot % 2][c * 2 * W:(c + 1) * 2 * W, 0:P], qs[:, slot, c, :],
                                        kt[:, slot % 2, c * P:(c + 1) * P], start=True, stop=True)
                    ins.then_inc(s_sc, 1)
                if live(trip, u, LAG_WT):
                    t, slot, r = tile_of(trip, u, LAG_WT)
                    pe.wait_ge(s_e, at + t + 1)
                    wait_freed(pe, s_es, at + t - 1)
                    pe.transpose(bank[4 + slot % 2][:, 0:P], et[:, slot % (2 * RL), 0:P], ident[:, :]).then_inc(s_ep, 1)
                if live(trip, u, LAG_O):
                    t, slot, r = tile_of(trip, u, LAG_O)
                    pe.wait_ge(s_es, at + t + 1)
                    wait_freed(pe, s_acc, at + t - 1)
                    for h in range(HEADS):
                        ins = pe.matmul(bank[6 + slot % 2][h * W:(h + 1) * W, 0:VW], es[:, slot % 2, h * W:(h + 1) * W],
                                        kv_slot(slot)[:, D + h * VW:D + (h + 1) * VW], start=True, stop=True)
                    ins.then_inc(s_o, 1)

            run_steps(pe, LAG_O, step)

        def relation_tiles(pe, l):
            at = l * T

            def step(trip, u):
                if live(trip, u, 0):
                    t, slot, r = tile_of(trip, u, 0)
                    if slot % Q == 0:
                        pe.wait_ge(s_eat[slot // Q % 2], 16 * (quads_before(l * TRIPS + r, slot) + 1))
                    wait_freed(pe, s_prod, at + t - RL + 1)
                    pe.matmul(bank[slot % RL][:, 0:D], eat[:, slot // Q % 2, slot % Q, :], nnwt[:, :],
                              start=True, stop=True).then_inc(s_ew, 1)
                if live(trip, u, LAG_SUM):
                    t, slot, r = tile_of(trip, u, LAG_SUM)
                    if slot % Q == 0:
                        pe.wait_ge(s_oh, QUADS * (l * TRIPS + r) + slot // Q + 1)
                    pe.wait_ge(s_msg, at + t + 1)
                    wait_freed(pe, s_racc, at + t - RL + 1)
                    if l == 0:
                        wait_freed(pe, s_rc, at + t - RL + 1)
                    b = bank[RL + slot % RL]
                    one = oh[:, slot // Q % 2, slot % Q, :]
                    if l == 0:
                        pe.matmul(b[0:SEG, 2 * SEG:2 * SEG + 1], one, ones_f[:, :], start=True, stop=True)
                    for c in range(2):
                        ins = pe.matmul(b[:, c * SEG:(c + 1) * SEG], msg[:, slot % RL, c * P:(c + 1) * P], one,
                                        start=True, stop=True)
                    ins.then_inc(s_sp, 1)

            run_steps(pe, LAG_SUM, step)

        def scalar_program(act):
            ea_v = a["edge_attr_32"].rearrange("(p j) c -> p j c", p=EP)

            def staging(trip, slot):
                g = trip * GU + slot
                if not isinstance(trip, int):
                    act.wait_ge(s_scat[slot], 16 * CG * trip)
                act.dma_start(stage[:, slot, :, 0:ND], ea_v[:, bass.ds(g * CG, CG), :]).then_inc(s_sea[slot], 16)
                act.wait_ge(s_row, ROWSTEPS * (g + 1))
                act.copy(stage[:, slot, :, ND:REC], meta[:, bass.ds(g * CG, CG), :]).then_inc(s_stage, 1)
                act.copy(stage_row[:, slot, :], row_e[:, bass.ds(g * CG, CG)]).then_inc(s_stage, 1)

            for slot in range(GU):
                staging(0, slot)
            with act.Fori(1, GTRIPS) as trip:
                for slot in range(GU):
                    staging(trip, slot)

            for b in range(4 * NUC):
                if b % 4 == 0:
                    k = b // 4
                    act.wait_ge(s_chunk[k % 2], 16 * (k // 2 + 1))
                    if k == 0:
                        act.wait_ge(s_pev, NPROJ[0])
                    act.copy(attrs[:, k % 2, :].rearrange("p (t c) -> p t c", c=ND), chunk[:, k % 2, :, 0:ND])\
                        .then_inc(s_attrs, 1)
                act.wait_ge(s_unp, b + 1)
                if b >= 2:
                    act.wait_ge(s_eato[b % 2], 16 * (b // 2))
                act.copy(eat_out[:, b % 2, :], bank[b % 4][:, :]).then_inc(s_eatc, 1)
                act.wait_ge(s_eatc, b + 1)
                act.dma_start(eat_d[b, :, :], eat_out[:, b % 2, :]).then_inc(s_eato[b % 2], 16)

            for i in range(2):
                act.wait_ge(s_eato[i], 16 * 2 * NUC)
            for l in range(2):
                attention_acts(act, l)
                act.wait_ge(event("var"), l + 1)
                act.activation(bn_t[:, :, 1], bn_t[:, :, 0], ACT.Sqrt).then_inc(event("std"), 1)
                act.wait_ge(event("affine"), l + 1)
                act.wait_ge(s_proj, sum(NPROJ[:l + 1]))
                for c in range(2):
                    ins = act.activation(ht[:, c, :], st[:, c, :], ACT.Identity, bias=bn_t[:, c, 3:4], scale=bn_t[:, c, 2:3])
                ins.then_inc(event("normed"), 1)
            act.wait_ge(event("ln_var"), 1)
            act.activation(ln_sd[:, :, 1], ln_sd[:, :, 0], ACT.Sqrt).then_inc(event("ln_std"), 1)

            def copy_features(i, n):
                act.wait_ge(s_htp, n + 1)
                act.copy(ht[:, :, i * P:(i + 1) * P], bank[4 + n % 2][:, 0:2 * P].rearrange("p (c n) -> p c n", c=2))\
                    .then_inc(s_ht, 1)

            for i in range(NT):
                copy_features(i, i)
            for l in range(3):
                def relation_step(trip, u):
                    t, slot, r = tile_of(trip, u, 0)
                    act.wait_ge(s_prod, l * T + t + 1)
                    wait_freed(act, s_sp, l * T + t - RL + 1)
                    act.activation(msg[:, slot % RL, :], prod[:, slot % RL, :], ACT.Relu).then_inc(s_msg, 1)

                run_steps(act, 0, relation_step)
                if l < 2:
                    for i in range(NT):
                        copy_features(i, (l + 1) * NT + i)
            act.wait_ge(event("ln_var"), 2)
            act.activation(ln_sd[:, :, 1], ln_sd[:, :, 0], ACT.Sqrt).then_inc(event("ln_std"), 1)

        def attention_acts(act, l):
            at = l * T

            def step(trip, u):
                if live(trip, u, 0):
                    t, slot, r = tile_of(trip, u, 0)
                    act.wait_ge(s_ktp, at + t + 1)
                    wait_freed(act, s_sc, at + t - 1)
                    act.copy(kt[:, slot % 2, :], bank[slot % 2][:, 0:2 * P]).then_inc(s_kt, 1)
                if live(trip, u, LAG_EXP):
                    t, slot, r = tile_of(trip, u, LAG_EXP)
                    act.wait_ge(s_top, at + t + 1)
                    wait_freed(act, s_acc, at + t - 2 * RL + 1)
                    act.activation(et[:, slot % (2 * RL), :], xs[:, slot % RL, :], ACT.Exp, bias=ntop[:, slot:slot + 1],
                                   scale=-1.0).then_inc(s_e, 1)
                if live(trip, u, LAG_WT):
                    t, slot, r = tile_of(trip, u, LAG_WT)
                    act.wait_ge(s_ep, at + t + 1)
                    wait_freed(act, s_o, at + t - 1)
                    act.copy(es[:, slot % 2, :], bank[4 + slot % 2][:, 0:P]).then_inc(s_es, 1)

            run_steps(act, LAG_WT, step)

        def vector_program(v):
            def step(ins):
                return vec_n.inc(ins)

            def after():
                v.wait_ge(s_vec, vec_n.n)

            def tell(name, ins):
                ins.then_inc(event(name), 1)
                told[name] = told.get(name, 0) + 1
                v.wait_ge(event(name), told[name])

            told = {}

            v.wait_ge(s_edges, 48)
            v.wait_ge(event("consts"), 1)
            step(v.tensor_scalar(int_e[:, :], dst_e[:, :], W - 1, None, ALU.bitwise_and))
            step(v.tensor_scalar(part_m[:, :], part_i[:, :], W - 1, None, ALU.bitwise_and))
            step(v.tensor_copy(meta[:, :, 0], src_e[:, :]))
            after()
            step(v.tensor_copy(part_dl[:, :], part_m[:, :]))
            step(v.tensor_copy(meta[:, :, 1], int_e[:, :]))
            after()
            step(v.scalar_tensor_tensor(meta[:, :, 2], typ_e[:, :], float(W), meta[:, :, 1], ALU.mult, ALU.add))
            step(v.tensor_scalar(int_e[:, :], dst_e[:, :], W.bit_length() - 1, None, ALU.logical_shift_right))
            after()
            step(v.tensor_copy(win_f[:, :], int_e[:, :]))
            v.wait_ge(event("nnw"), 1)
            v.wait_ge(s_small, 16 * 25)
            tell("nnwt", v.tensor_copy(nnwt[0:ND, :], bank[7][0:ND, 0:D]))
            after()

            def one_hot(trip, slot):
                g = trip * GU + slot
                v.tensor_tensor(onehot_w[:, slot, :, :],
                                win_f[:, bass.ds(g * CG, CG)].unsqueeze(2).to_broadcast([EP, CG, NW]),
                                iota_w[0:EP, :].unsqueeze(1).to_broadcast([EP, CG, NW]), ALU.is_equal).then_inc(s_ohw, 1)

            def count_step(trip, slot):
                if not isinstance(trip, int):
                    v.wait_ge(s_cntw, trip * GU + slot - GU + 1)
                one_hot(trip, slot)

            for slot in range(GU):
                count_step(0, slot)
            with v.Fori(1, GTRIPS) as trip:
                for slot in range(GU):
                    count_step(trip, slot)

            v.wait_ge(event("counted"), 1)
            step(v.tensor_reduce(cnt_w[:, :], bank[6][:, 0:CG * NW].rearrange("p (c w) -> p w c", c=CG), AX.X, ALU.add))
            after()
            step(v.tensor_scalar(tiles_i[:, :], cnt_w[:, :], float(P - 1), None, ALU.add))
            after()
            step(v.tensor_scalar(tiles_i[:, :], tiles_i[:, :], P.bit_length() - 1, None, ALU.logical_shift_right))
            after()
            step(v.tensor_copy(tiles_f[:, :], tiles_i[:, :]))
            after()
            tell("tend", v.tensor_tensor_scan(tend[:, :], ones_w[:, :], tiles_f[:, :], 0.0, ALU.mult, ALU.add))
            after()
            step(v.tensor_tensor(run_tot[:, :], tend[:, :], tiles_f[:, :], ALU.subtract))
            after()
            step(v.tensor_scalar(run_tot[:, :], run_tot[:, :], float(P), None, ALU.mult))
            v.wait_ge(event("tend_c"), 1)
            tell("tend_copied", v.tensor_copy(tend_c[:, :], bank[5][0:NW, 0:1]))
            after()
            tell("ended", v.tensor_scalar(ended, iota_t, tend_c[:, 0:1], None, ALU.is_ge))
            v.wait_ge(event("tile_w"), 1)
            step(v.tensor_copy(tile_w, bank[7][:, 0:T]))
            after()
            step(v.tensor_copy(win_i[:, :], tile_w[0:1, :]))
            step(v.memset(restart[:, 0:1], 1.0))
            step(v.tensor_tensor(restart[:, 1:T], tile_w[:, 1:T], tile_w[:, 0:T - 1], ALU.not_equal))
            after()
            step(v.tensor_scalar(restart[:, :], restart[:, :], RESTART - KEEP, KEEP, ALU.mult, ALU.add))
            after()

            def rows_of(trip, slot):
                g = trip * GU + slot
                n = ROWSTEPS * g
                v.wait_ge(s_rank, g + 1)
                if not isinstance(g, int) or g:
                    v.wait_ge(s_row, n)
                r = bank[slot][0:EP, 0:CG * NW].rearrange("p (c w) -> p c w", c=CG)
                v.tensor_tensor(rank[:, :, :], r, run_tot[0:EP, :].unsqueeze(1).to_broadcast([EP, CG, NW]), ALU.add)\
                    .then_inc(s_row, 1)
                v.wait_ge(s_row, n + 1)
                v.tensor_tensor(rank[:, :, :], rank[:, :, :], onehot_w[:, slot, :, :], ALU.mult).then_inc(s_row, 1)
                v.tensor_tensor(run_tot[0:EP, :], run_tot[0:EP, :], bank[5 + slot % 3][0:EP, 0:NW], ALU.add)\
                    .then_inc(s_row, 1)
                v.wait_ge(s_row, n + 2)
                v.tensor_reduce(pos_f[:, :], rank[:, :, :], AX.X, ALU.add).then_inc(s_row, 1)
                v.wait_ge(s_row, n + 4)
                v.tensor_copy(pos_i[:, :], pos_f[:, :]).then_inc(s_row, 1)
                v.wait_ge(s_row, n + 5)
                v.tensor_scalar(pos_lo[:, :], pos_i[:, :], P - 1, T.bit_length() - 1, ALU.bitwise_and,
                                ALU.logical_shift_left).then_inc(s_row, 1)
                v.tensor_scalar(pos_hi[:, :], pos_i[:, :], P.bit_length() - 1, None, ALU.logical_shift_right).then_inc(s_row, 1)
                v.wait_ge(s_row, n + 7)
                v.tensor_tensor(row_e[:, bass.ds(g * CG, CG)], pos_lo[:, :], pos_hi[:, :], ALU.bitwise_or).then_inc(s_row, 1)

            v.wait_ge(s_cntw, G)
            for slot in range(GU):
                one_hot(0, slot)
            for slot in range(GU):
                rows_of(0, slot)
            with v.Fori(1, GTRIPS) as trip:
                for slot in range(GU):
                    one_hot(trip, slot)
                for slot in range(GU):
                    rows_of(trip, slot)

            for l in range(2):
                projected(v, l)
                if l == 0:
                    for k in range(NUC):
                        v.wait_ge(s_chunk[k % 2], 16 * (k // 2 + 1))
                        for t, c in ((src_i, C_SRC), (dl_f, C_DL), (seg_f, C_SEG)):
                            v.tensor_copy(t[:, k * UC:(k + 1) * UC], chunk[:, k % 2, :, c]).then_inc(s_unv, 1)
                    v.wait_ge(event("dl_t"), 1)
                    tell("dlt", v.tensor_copy(dlt_out[:, :, :].rearrange("t q p -> t (q p)"), bank[4][:, 0:T]))
                    v.wait_ge(s_unp, 4 * NUC)
                    v.wait_ge(s_unv, 3 * NUC)
                step(v.memset(ntop[:, :], 0.0))
                tell("tables", v.memset(acc, 0.0))
                after()
                attended(v, l)
                v.wait_ge(s_acc, (l + 1) * T)
                step(v.tensor_scalar(rden[:, :], acc[:, :, HD], 1e-30, None, ALU.max))
                after()
                step(v.reciprocal(rden[:, :], rden[:, :]))
                after()
                tell("divided", v.tensor_tensor(acc[:, :, 0:HD], acc[:, :, 0:HD],
                                                rden[:, :].unsqueeze(2).to_broadcast([P, NWP, HD]), ALU.mult))
                for j in range(NT):
                    v.wait_ge(s_tr, l * NT + j + 1)
                    for h in range(HEADS):
                        o = st[h % 2 * HD:(h % 2 + 1) * HD, h // 2, j * P:(j + 1) * P].rearrange("p (w d) -> p w d", d=W)
                        v.tensor_tensor(o, bank[j % 2][0:HD, :].rearrange("p (w h d) -> p w h d", h=HEADS, d=W)[:, :, h, :],
                                        o, ALU.add).then_inc(s_add, 1)
                v.wait_ge(s_add, 4 * (l + 1) * NT)
                for c in range(2):
                    for nb in range(NB):
                        n = min(512, N - nb * 512)
                        step(v.bn_stats(stats[:, c, nb, :], st[:, c, nb * 512:nb * 512 + n]))
                after()
                for c in range(2):
                    step(v.bn_aggr(mv[:, c, :], stats[:, c, :, :].rearrange("p b s -> p (b s)")))
                after()
                tell("var", v.tensor_scalar(bn_t[:, :, 0], mv[:, :, 1], EPS, None, ALU.add))
                v.wait_ge(event("std"), l + 1)
                step(v.reciprocal(bn_t[:, :, 1], bn_t[:, :, 1]))
                after()
                step(v.tensor_tensor(bn_t[:, :, 2], bn_t[:, :, 1], gamma[:, l, :], ALU.mult))
                after()
                step(v.tensor_tensor(bn_t[:, :, 3], mv[:, :, 0], bn_t[:, :, 2], ALU.mult))
                after()
                tell("affine", v.tensor_tensor(bn_t[:, :, 3], beta[:, l, :], bn_t[:, :, 3], ALU.subtract))
                v.wait_ge(event("normed"), l + 1)
                step(v.scalar_tensor_tensor(ht[:, 0, :], ht[:, 0, :], 0.1, ht[:, 0, :], ALU.mult, ALU.max))
                tell("leaky", v.scalar_tensor_tensor(ht[:, 1, :], ht[:, 1, :], 0.1, ht[:, 1, :], ALU.mult, ALU.max))

            for i in range(NT):
                slot = 2 if i == NT - 1 else i % 2
                v.wait_ge(s_tr, 2 * NT + i + 1)
                v.wait_ge(s_xr[slot], 16 * (2 if slot == 2 else NT // 2 + i // 2 + 1))
                v.tensor_tensor(x1[:, i, :], bank[i % 2][:, 0:D], xr[:, slot, :], ALU.add).then_inc(s_add, 1)
            v.wait_ge(s_add, 4 * 2 * NT + NT)
            layer_norm(v, step, after, tell, 0)

            v.wait_ge(s_clr, 3)
            for l in range(3):
                related(v, l)
                if l == 0:
                    v.wait_ge(event("cnt"), 1)
                    step(v.tensor_scalar(inv_t[:, :, :].rearrange("p r i -> p (r i)"), bank[7][:, 0:NREL * NT], 1.0, None, ALU.max))
                    after()
                    step(v.reciprocal(inv_t[:, :, :], inv_t[:, :, :]))
                    after()
                for i in range(NT):
                    n = l * NT + i
                    b = 2 * (n % 2)
                    v.wait_ge(s_dn, n + 1)
                    if l < 2 and i >= 4:
                        v.wait_ge(s_ho[l][i % 4], 16 * (i // 4))
                        v.wait_ge(s_htp, (l + 1) * NT + i - 3)
                    o = orow[:, i % 4, :]
                    v.tensor_tensor(o, bank[b][:, 0:D], bias_r[:, l, :], ALU.add).then_inc(s_dv, 1)
                    for r in range(NREL):
                        p = bank[b + (r + 1) // 2][:, (r + 1) % 2 * D:((r + 1) % 2 + 1) * D]
                        v.wait_ge(s_dv, STEPD * n + r + 1)
                        v.scalar_tensor_tensor(o, p, inv_t[:, r, i:i + 1], o, ALU.mult, ALU.add).then_inc(s_dv, 1)
                    if l == 2:
                        v.wait_ge(s_dv, STEPD * (n + 1))
                        step(v.tensor_tensor(x1[:, i, :], x1[:, i, :], o, ALU.add))
            after()
            layer_norm(v, step, after, tell, 1)

        def layer_norm(v, step, after, tell, n):
            for i in range(NT):
                step(v.bn_stats(ln_st[:, i, :], x1[:, i, :]))
            after()
            for i in range(NT):
                step(v.bn_aggr(ln_mv[:, i, :], ln_st[:, i, :]))
            after()
            tell("ln_var", v.tensor_scalar(ln_sd[:, :, 0], ln_mv[:, :, 1], EPS, None, ALU.add))
            v.wait_ge(event("ln_std"), n + 1)
            step(v.reciprocal(ln_sd[:, :, 1], ln_sd[:, :, 1]))
            after()
            for i in range(NT):
                v.tensor_scalar(x1[:, i, :], x1[:, i, :], ln_mv[:, i, 0:1], ln_sd[:, i, 1:2], ALU.subtract, ALU.mult)\
                    .then_inc(s_ln, 1)

        def projected(v, l):
            job = sum(NPROJ[:l])
            if l == 0:
                v.wait_ge(event("cleared"), 1)
                for i in range(NT):
                    v.wait_ge(s_proj, job + 1)
                    v.tensor_copy(ht[:, :, i * P:(i + 1) * P], bank[job % 4][:, 0:2 * P].rearrange("p (c n) -> p c n", c=2))\
                        .then_inc(s_pev, 1)
                    job += 1
            for c in range(2):
                for nb in range(NB):
                    n = min(512, NP - nb * 512)
                    v.wait_ge(s_proj, job + 1)
                    for k in range(2):
                        ins = v.tensor_scalar(qblk[k * HD:(k + 1) * HD, nb * 512 // W:(nb * 512 + n) // W, c, k * W:(k + 1) * W],
                                              bank[job % 4][k * HD:(k + 1) * HD, 0:n].rearrange("p (w d) -> p w d", d=W),
                                              bias_q[k * HD:(k + 1) * HD, l, c:c + 1], -SCALE, ALU.add, ALU.mult)
                        if k == 0:
                            vec_n.inc(ins)
                    ins.then_inc(s_pev, 1)
                    job += 1
            v.wait_ge(s_vec, vec_n.n)
            for c in range(2):
                for nb in range(NB):
                    n = min(512, NP - nb * 512)
                    v.wait_ge(s_proj, job + 1)
                    v.tensor_scalar(st[:, c, nb * 512:nb * 512 + n], bank[job % 4][:, 0:n], bias_s[:, l, c:c + 1], None, ALU.add)\
                        .then_inc(s_pev, 1)
                    job += 1
            for i in range(NT):
                v.wait_ge(s_proj, job + 1)
                done = 16 * (l * ((NT + 1 - i % 2) // 2) + i // 2)
                if done:
                    v.wait_ge(s_kvo[i % 2], done)
                vec_n.inc(v.tensor_tensor(kvrow[:, i % 2, 0:D], bank[job % 4][:, 0:D], bias_kv[:, l, 0, :], ALU.add))
                v.wait_ge(s_vec, vec_n.n)
                v.tensor_tensor(kvrow[:, i % 2, D:].rearrange("p (h v) -> p h v", v=VW)[:, :, 0:HD],
                                bank[job % 4][:, D:2 * D].rearrange("p (h v) -> p h v", v=HD),
                                bias_kv[:, l, 1, :].rearrange("p (h v) -> p h v", v=HD), ALU.add).then_inc(s_pev, 1)
                job += 1

        def attended(v, l):
            at = l * T

            def step(trip, u):
                if u % Q == 0 and live(trip, u, 0):
                    b = u // Q % 2
                    v.wait_ge(s_dlb[b], 16 * (quads_before(l * TRIPS + trip, u) + 1))
                    v.tensor_scalar(mask[:, b, :, :].rearrange("p t e -> p (t e)"), dlb[:, b, :], part_dl[:, 0:1], MASKED,
                                    ALU.not_equal, ALU.mult).then_inc(s_mask, 1)
                if live(trip, u, 1):
                    t, slot, r = tile_of(trip, u, 1)
                    wait_freed(v, s_e, at + t - RL + 1)
                    wait_freed(v, s_top, at + t)
                    v.tensor_tensor(xs[:, slot % RL, P:P + 1], ntop[:, (slot - 1) % U:(slot - 1) % U + 1],
                                    restart[:, bass.ds(t, 1)], ALU.max).then_inc(s_old, 1)
                if live(trip, u, LAG_ACC):
                    t, slot, r = tile_of(trip, u, LAG_ACC)
                    w = v.value_load(win_i[0:1, bass.ds(t, 1)], min_val=0, max_val=NW)
                    wait_freed(v, s_acc, at + t)
                    v.wait_ge(s_o, at + t + 1)
                    o = acc[:, bass.ds(w, 1), :].rearrange("p o v -> p (o v)")
                    v.scalar_tensor_tensor(o, o, et[:, slot % (2 * RL), P:P + 1], bank[6 + slot % 2][:, 0:VW], ALU.mult, ALU.add)\
                        .then_inc(s_acc, 1)
                if live(trip, u, 1):
                    t, slot, r = tile_of(trip, u, 1)
                    v.wait_ge(s_mask, QUADS * (l * TRIPS + r) + slot // Q + 1)
                    v.wait_ge(s_old, at + t + 1)
                    v.wait_ge(s_sc, at + t + 1)
                    v.sem_inc(s_gatev)
                    v.tensor_tensor_reduce(xs[:, slot % RL, 0:P], bank[2 + slot % 2][:, 0:P], mask[:, slot // Q % 2, slot % Q, :],
                                           1.0, xs[:, slot % RL, P:P + 1], ALU.add, ALU.min, ntop[:, slot:slot + 1]).then_inc(s_top, 1)

            run_steps(v, LAG_ACC, step)

        def related(v, l):
            at = l * T

            def step(trip, u):
                if u % Q == 0 and live(trip, u, 0):
                    b = u // Q % 2
                    wait_freed(v, s_sp, at + trip * U + u - Q)
                    v.tensor_tensor(oh[:, b, :, :],
                                    seg_f[:, bass.ds(trip * U + u, Q)].unsqueeze(2).to_broadcast([P, Q, SEG]),
                                    iota_seg[:, :].unsqueeze(1).to_broadcast([P, Q, SEG]), ALU.is_equal).then_inc(s_oh, 1)
                if live(trip, u, 0):
                    t, slot, r = tile_of(trip, u, 0)
                    v.wait_ge(s_g[slot], 16 * ((2 + l) * TRIPS + r + 1))
                    v.wait_ge(s_ew, at + t + 1)
                    wait_freed(v, s_msg, at + t - RL + 1)
                    v.tensor_tensor(prod[:, slot % RL, :], bank[slot % RL][:, 0:D], gring_r[:, slot, :], ALU.mult)\
                        .then_inc(s_prod, 1)
                if live(trip, u, LAG_RACC):
                    t, slot, r = tile_of(trip, u, LAG_RACC)
                    w = v.value_load(win_i[0:1, bass.ds(t, 1)], min_val=0, max_val=NW)
                    b = bank[RL + slot % RL]
                    if l == 0:
                        v.wait_ge(s_sp, at + t + 1)
                        wait_freed(v, s_rc, at + t)
                        c = cnt_t[:, bass.ds(w, 1)]
                        v.tensor_tensor(c, c, b[0:SEG, 2 * SEG:2 * SEG + 1], ALU.add).then_inc(s_rc, 1)
                    wait_freed(v, s_racc, at + t)
                    v.wait_ge(s_sp, at + t + 1)
                    if isinstance(trip, int) and t == 0 and l:
                        v.wait_ge(s_clr, 3 + l * NT)
                    o = racc[:, :, bass.ds(w * W, W)]
                    v.tensor_tensor(o, o, b[:, 0:2 * SEG].rearrange("p (s d) -> p s d", d=W), ALU.add).then_inc(s_racc, 1)

            run_steps(v, LAG_RACC, step)

        block = ctx.enter_context(nc.Block())

        @block.gpsimd
        def _(g):
            gpsimd_program(g)

        @block.sync
        def _(sp):
            sync_program(sp)

        @block.tensor
        def _(pe):
            tensor_program(pe)

        @block.scalar
        def _(act):
            scalar_program(act)

        @block.vector
        def _(v):
            vector_program(v)


def kernel(**inputs):
    import numpy as np
    import concourse.bacc as bacc
    from concourse.bass_utils import run_bass_kernel_spmd

    nc = bacc.Bacc("TRN2", target_bir_lowering=False, num_devices=1)
    arrays, aps = {}, {}
    for name, value in inputs.items():
        array = np.ascontiguousarray(value)
        arrays["in_" + name] = array
        aps[name] = nc.dram_tensor("in_" + name, array.shape, mybir.dt.from_np(array.dtype), kind="ExternalInput").ap()
    out = nc.dram_tensor("out", (N, D), F32, kind="ExternalOutput").ap()
    build(nc, aps, out)
    return run_bass_kernel_spmd(nc, [arrays], core_ids=[0]).results[0]["out"]
```

```python
from contextlib import ExitStack

import concourse.bass as bass
from concourse import mybir

ALU = mybir.AluOpType
ACT = mybir.ActivationFunctionType
AX = mybir.AxisListType
F32 = mybir.dt.float32
BF16 = mybir.dt.bfloat16
I32 = mybir.dt.int32

P = 128
N, D = 3125, 256
E = 53125
HEADS, HD = 4, 64
VW = HD + 1
ND = 32
NREL = 3
W = 32
NW = -(-N // W)
NT = -(-N // P)
WPT = P // W
NWP = NT * WPT
NP = NT * P
NTAIL = N - (NT - 1) * P
T = (E + NW * (P - 1)) // P
U = 8
TU = 2 * U
Q = 4
QUADS = TU // Q
RL = 4
TRIPS = T // TU
PAIRS = T // 2
EP, EJ = 125, 425
CG = 5
G = EJ // CG
GU = 5
GTRIPS = G // GU
REC = 36
C_SRC, C_DL, C_SEG = ND, ND + 1, ND + 2
SEG = NREL * W
KVW = D + HEADS * VW
UC = 64
NUC = T // UC
EO = 8
NB = -(-NP // 512)
DG = 5
HG, OG = 5, 4
EPS = 1e-5
SCALE = HD ** -0.5
MASKED, RESTART, KEEP = 1e30, 1e29, -1e30
assert NT % HG == 0 and NT % DG == 0 and (NT - 1) % OG == 0
assert EP * EJ == E and T == TRIPS * TU and G == GTRIPS * GU and NWP > NW and T % P == 0


class Count:

    def __init__(self, sem):
        self.sem, self.n = sem, 0

    def inc(self, instruction, by=1):
        instruction.then_inc(self.sem, by)
        self.n += by
        return self.n


def live(trip, u, lag):
    return not isinstance(trip, int) or 0 <= trip * U + u - lag < PAIRS


def run_steps(eng, lag, step):
    for u in range(U):
        step(0, u)
    with eng.Fori(1, TRIPS) as trip:
        for u in range(U):
            step(trip, u)
    for u in range(lag):
        step(TRIPS, u)


def tile_of(trip, u, lag):
    return trip * U + (u - lag), (u - lag) % U, trip if u >= lag else trip - 1


def quads_before(trip, u):
    return trip * (QUADS // 2) + u // 4


def wait_freed(eng, sem, value):
    if not isinstance(value, int) or value > 0:
        eng.wait_ge(sem, value)


def build(nc, a, out):
    ctx = ExitStack()
    with ctx:
        def sb(name, shape, dt):
            return ctx.enter_context(nc.sbuf_tensor(name, shape, dt))

        def sem(name):
            return ctx.enter_context(nc.semaphore(name))

        def dram(name, shape, dt=F32):
            return nc.dram_tensor(name, shape, dt, kind="Internal").ap()

        rec_d = dram("edge_records", (P * T, REC))
        eat_d = dram("edge_attr_T", (TRIPS, P, QUADS * P))
        dlt_d = dram("node_in_window_T", (T, P), BF16)
        kv_d = [dram(f"kv_rows{l}", (NP, KVW)) for l in range(2)]
        h_d = [dram(f"h_rows{l}", (NP, D)) for l in range(3)]

        ident = sb("ident", [P, P], F32)
        before = sb("before", [EP, EP], BF16)
        ones_b = sb("ones_b", [P, P], BF16)
        ones_f = sb("ones_f", [P, 1], F32)
        zeros_b = sb("zeros_b", [EP, CG * NW], BF16)
        ones_w = sb("ones_w", [P, NW], F32)
        iota_seg = sb("iota_seg", [P, SEG], F32)
        part_i = sb("part_i", [P, 1], I32)
        part_m = sb("part_m", [P, 1], I32)
        part_dl = sb("part_dl", [P, 1], F32)

        src_i = sb("src_i", [P, T + TU], I32)
        seg_f = sb("seg_f", [P, T], F32)
        dl_f = sb("dl_f", [P, T], F32)
        restart = sb("restart", [P, T], F32)
        win_i = sb("win_i", [1, T], I32)
        win_v = sb("win_v", [1, T], I32)

        wts = sb("wts", [P, 2, 4, 2, D], F32)
        bias_q = sb("bias_q", [P, 2, 2], F32)
        bias_s = sb("bias_s", [P, 2, 2], F32)
        gamma = sb("gamma", [P, 2, 2], F32)
        beta = sb("beta", [P, 2, 2], F32)
        bias_kv = sb("bias_kv", [P, 2, 2, D], F32)
        bias_r = sb("bias_r", [P, 3, D], F32)
        nnw = sb("nnw", [P, 2, ND], F32)
        nnwt = sb("nnwt", [P, D], F32)

        ht_flat = sb("ht", [P, 2 * NP], F32)
        ht = ht_flat[:, :].rearrange("p (c n) -> p c n", c=2)
        REGION = 2 * NP + NWP * P + NWP * VW
        region = sb("region", [P, REGION], F32)
        at = 0
        st = region[:, 0:2 * NP].rearrange("p (c n) -> p c n", c=2)
        qblk = region[:, 2 * NP:2 * NP + NWP * P].rearrange("p (w c m) -> p w c m", c=2, m=2 * W)
        at = 2 * NP + NWP * P
        acc_flat = region[:, at:at + NWP * VW]
        acc = acc_flat.rearrange("p (w v) -> p w v", v=VW)
        chunk = region[:, at:at + 2 * UC * REC].rearrange("p (b t r) -> p b t r", b=2, r=REC)
        x1 = region[:, at:at + NT * D].rearrange("p (i f) -> p i f", f=D)
        racc = region[:, 0:2 * NREL * NP].rearrange("p (s n) -> p s n", n=NP)
        assert 2 * NREL * NP <= at and 2 * UC * REC <= NWP * VW and NT * D <= NWP * VW
        gring = sb("gring", [P, TU // 2, KVW], F32)
        gring_ht = ht_flat[:, 0:TU // 2 * KVW].rearrange("p (u k) -> p u k", k=KVW)
        gring_r = gring[:, :, :].rearrange("p u k -> p (u k)")[:, 0:TU * D].rearrange("p (u f) -> p u f", f=D)

        def kv_slot(i):
            return gring[:, i, :] if i < TU // 2 else gring_ht[:, i - TU // 2, :]

        xr = sb("xr", [P, 3, D], F32)
        rows = sb("rows", [P, 2 * KVW], F32)
        kvrow = rows[:, :].rearrange("p (s k) -> p s k", s=2)
        orow = rows[:, 0:4 * D].rearrange("p (s f) -> p s f", s=4)
        assert 4 * D <= 2 * KVW
        gidx = sb("gidx", [P, QUADS, Q], I32)

        sort_at = [at]

        def sort_space(n, dt=F32):
            space = region[0:EP, sort_at[0]:sort_at[0] + n]
            sort_at[0] += n
            return space if dt == F32 else space.bitcast(dt)

        dst_e, typ_e, src_e, int_e = (sort_space(EJ, I32) for _ in range(4))
        row_e = sort_space(EJ, I32)
        win_f = sort_space(-(-EJ // 2), BF16)[:, 0:EJ]
        meta = sort_space(EJ * (REC - ND)).rearrange("p (j r) -> p j r", r=REC - ND)
        onehot_w = sort_space(GU * CG * NW // 2, BF16).rearrange("p (g w c) -> p g c w", g=GU, c=CG)
        onehot_packed = onehot_w.rearrange("p g c w -> p g w c")
        rank = sort_space(CG * NW).rearrange("p (c w) -> p c w", c=CG)
        assert sort_at[0] <= REGION
        run_tot = sb("run_tot", [P, NW], F32)
        cnt_w = sb("cnt_w", [P, NW], F32)
        tiles_i = sb("tiles_i", [P, NW], I32)
        tiles_f = sb("tiles_f", [P, NW], F32)
        tend = sb("tend", [P, NW], F32)
        tend_c = sb("tend_c", [NW, 1], F32)
        pos_f = sb("pos_f", [EP, CG], F32)
        pos_i = sb("pos_i", [EP, CG], I32)
        pos_lo = sb("pos_lo", [EP, CG], I32)
        pos_hi = sb("pos_hi", [EP, CG], I32)
        blank = gring[:, 0:5, :].rearrange("p u k -> p (u k)")[:, 0:UC * REC].rearrange("p (t r) -> p t r", r=REC)
        iota_t = gring[0:NW, 5, 0:T]
        iota_w = gring[0:EP, 6, 0:NW * CG // 2].bitcast(BF16).rearrange("p (w c) -> p w c", c=CG)
        tile_w = ht[:, 0, 0:T]
        ended = ht[0:NW, 1, 0:T // 2].bitcast(BF16)
        attrs = ht_flat[:, 0:2 * UC * ND].rearrange("p (s m) -> p s m", s=2)
        behind = TU // 2 * KVW
        eat_out = gring[:, :, :].rearrange("p u k -> p (u k)")[:, 0:EO * 4 * P].rearrange("p (s m) -> p s m", s=EO)
        et = ht_flat[:, behind:behind + 2 * RL * (P + 1)].rearrange("p (s e) -> p s e", e=P + 1)
        assert 2 * UC * ND <= behind
        behind += 2 * RL * (P + 1)
        dlt_out = ht_flat[:, behind:behind + T // 2].bitcast(BF16).rearrange("p (q e) -> p q e", e=P)
        behind += T // 2
        xs = ht_flat[:, behind:behind + 4 * (P + 1)].rearrange("p (s e) -> p s e", e=P + 1)
        behind += 4 * (P + 1)
        assert behind <= 2 * NP

        rings = sb("rings", [P, 2 * 4 * P + TU // 2 * 4 * W + Q * P + 2 * Q * P + 4 * P], F32)
        ring_at = [0]

        def ring_space(n):
            space = rings[:, ring_at[0]:ring_at[0] + n]
            ring_at[0] += n
            return space

        kt = ring_space(2 * 4 * P).rearrange("p (s k m) -> p s k m", s=2, k=2)
        qs = ring_space(TU // 2 * 4 * W).rearrange("p (s c m) -> p s c m", s=TU // 2, c=2)
        es = ring_space(2 * 2 * P).rearrange("p (s k m) -> p s k m", s=2, k=2)
        dlb = ring_space(Q * P).bitcast(BF16).rearrange("p (h m) -> p h m", h=2)
        mask = ring_space(2 * Q * P).rearrange("p (h t e) -> p h t e", h=2, t=Q)
        stage = rings[0:EP, 0:GU * CG * REC].rearrange("p (g c r) -> p g c r", g=GU, c=CG)
        stage_row = rings[0:EP, GU * CG * REC:GU * CG * (REC + 1)].bitcast(I32).rearrange("p (g c) -> p g c", g=GU)
        ring_at = [0]
        eat = ring_space(2 * Q * P).rearrange("p (h t e) -> p h t e", h=2, t=Q)
        oh = ring_space(2 * Q * SEG).rearrange("p (h t s) -> p h t s", h=2, t=Q)
        prod = ring_space(2 * 2 * D).rearrange("p (s f) -> p s f", s=2)
        msg = ring_space(2 * 2 * D).rearrange("p (s f) -> p s f", s=2)
        cnt_t = ring_space(NWP)[0:SEG, :]
        inv_t = ring_space(NREL * NT).rearrange("p (r i) -> p r i", i=NT)
        ln_at = [0]

        def ln_space(k):
            space = prod[:, :, :].rearrange("p s f -> p (s f)")[:, ln_at[0]:ln_at[0] + NT * k]
            ln_at[0] += NT * k
            return space.rearrange("p (i k) -> p i k", k=k)

        ln_st, ln_mv, ln_sd = ln_space(6), ln_space(2), ln_space(2)
        restart_t = sb("restart_t", [P, TU], F32)
        ntop = sb("ntop", [P, TU], F32)
        rden = sb("rden", [P, NWP], F32)
        stats = sb("stats", [P, 2, NB, 6], F32)
        mv = sb("mv", [P, 2, 2], F32)
        bn_t = sb("bn_t", [P, 2, 4], F32)


        bank = [ctx.enter_context(nc.psum_tensor(f"bank{i}", [P, 512], F32)) for i in range(8)]

        s_edges = sem("s_edges")
        s_small = sem("s_small")
        s_wr = [sem(f"s_wr{l}") for l in range(3)]
        s_pool = sem("s_pool")
        s_vec = sem("s_vec")
        s_blank = sem("s_blank")
        s_ohw = sem("s_ohw")
        s_cntw = sem("s_cntw")
        s_rank = sem("s_rank")
        s_row = sem("s_row")
        s_stage = sem("s_stage")
        s_sea = [sem(f"s_sea{i}") for i in range(GU)]
        s_scat = [sem(f"s_scat{i}") for i in range(GU)]
        s_chunk = [sem(f"s_chunk{i}") for i in range(2)]
        s_unv = sem("s_unv")
        s_attrs = sem("s_attrs")
        s_unp = sem("s_unp")
        s_eato = [sem(f"s_eato{i}") for i in range(EO)]
        s_eatc = sem("s_eatc")
        s_dlt = sem("s_dlt")
        s_xr = [sem(f"s_xr{i}") for i in range(3)]
        s_x2 = [sem(f"s_x2_{i}") for i in range(TU)]
        s_proj = sem("s_proj")
        s_pev = sem("s_pev")
        s_kvo = [sem(f"s_kvo{i}") for i in range(2)]
        s_idx = sem("s_idx")
        s_g = [sem(f"s_g{i}") for i in range(U)]
        s_gate = sem("s_gate")
        s_gatev = sem("s_gatev")
        s_q = [sem(f"s_q{i}") for i in range(RL)]
        s_dlb = [sem(f"s_dlb{i}") for i in range(2)]
        s_mask = sem("s_mask")
        s_rst = sem("s_rst")
        s_ktp, s_kt, s_sc, s_old, s_top = (sem(n) for n in ("s_ktp", "s_kt", "s_sc", "s_old", "s_top"))
        s_e, s_ep, s_es, s_o, s_acc = (sem(n) for n in ("s_e", "s_ep", "s_es", "s_o", "s_acc"))
        s_tr = sem("s_tr")
        s_add = sem("s_add")
        s_h = sem("s_h")
        s_eat = [sem(f"s_eat{i}") for i in range(2)]
        s_oh, s_ew, s_prod, s_msg, s_sp, s_racc, s_rc = (sem(n) for n in ("s_oh", "s_ew", "s_prod", "s_msg", "s_sp", "s_racc", "s_rc"))
        s_clr = sem("s_clr")
        s_dn = sem("s_dn")
        s_dv = sem("s_dv")
        s_htp = sem("s_htp")
        s_ht = sem("s_ht")
        s_ho = [[sem(f"s_ho{l}_{i}") for i in range(4)] for l in range(2)]
        s_ln = sem("s_ln")
        s_out = sem("s_out")
        pool_n, vec_n = Count(s_pool), Count(s_vec)
        events = {}

        def event(name):
            if name not in events:
                events[name] = sem("e_" + name)
            return events[name]


        ROWSTEPS = 8
        NPROJ = [NT + 2 * 2 * NB + NT, 2 * 2 * NB + NT]
        LAG_S, LAG_WT, LAG_O, LAG_ACC = 1, 2, 3, 4
        LAG_SUM, LAG_RACC = 1, 2
        ADDS = 2
        STEPD = 4

        def gpsimd_program(g):
            def step(ins):
                return pool_n.inc(ins)

            step(g.memset(ident[:, :], 0.0))
            step(g.memset(before[:, :], 1.0))
            step(g.memset(ones_b[:, :], 1.0))
            step(g.memset(ones_f[:, :], 1.0))
            step(g.memset(ones_w[:, :], 1.0))
            step(g.memset(zeros_b[:, :], 0.0))
            step(g.memset(src_i[:, T:T + TU], 0))
            step(g.memset(nnwt[:, :], 0.0))
            step(g.iota(iota_w[:, :, :], pattern=[[1, NW], [0, CG]], base=0, channel_multiplier=0,
                        allow_small_or_imprecise_dtypes=True))
            step(g.iota(iota_seg[:, :], pattern=[[1, SEG]], base=0, channel_multiplier=0,
                        allow_small_or_imprecise_dtypes=True))
            step(g.iota(iota_t, pattern=[[1, T]], base=0, channel_multiplier=0,
                        allow_small_or_imprecise_dtypes=True))
            step(g.iota(part_i[:, :], pattern=[[0, 1]], base=0, channel_multiplier=1))
            step(g.memset(meta[:, :, REC - ND - 1:REC - ND], 0.0))
            step(g.memset(blank, 0.0))
            g.wait_ge(s_pool, pool_n.n)
            step(g.affine_select(out=ident[:, :], in_=ident[:, :], compare_op=ALU.not_equal, fill=1.0,
                                 base=0, pattern=[[-1, P]], channel_multiplier=1))
            step(g.affine_select(out=before[:, :], in_=before[:, :], compare_op=ALU.is_gt, fill=0.0,
                                 base=0, pattern=[[1, EP]], channel_multiplier=-1))
            step(g.memset(blank[:, :, C_DL:C_DL + 1], float(W)))
            g.wait_ge(s_pool, pool_n.n)
            g.memset(blank[:, :, C_SEG:C_SEG + 1], float(SEG)).then_inc(event("consts"), 1)
            step(g.memset(xr[:, 2, :], 0.0))
            step(g.memset(kvrow, 1.0))
            g.wait_ge(s_pool, pool_n.n)
            g.memset(qblk, 0.0).then_inc(event("cleared"), 1)

            g.wait_ge(s_blank, 16 * NUC)

            def scatter(trip, slot):
                g.wait_ge(s_sea[slot], 16 * (trip + 1))
                g.wait_ge(s_stage, 2 * (trip * GU + slot) + 2)
                g.sem_inc(s_gate)
                for c in range(CG):
                    g.indirect_dma_start(
                        out=rec_d, out_offset=bass.IndirectOffsetOnAxis(ap=stage_row[:, slot, c:c + 1], axis=0),
                        in_=stage[:, slot, c, :], in_offset=None).then_inc(s_scat[slot], 16)

            for slot in range(GU):
                scatter(0, slot)
            with g.Fori(1, GTRIPS) as trip:
                for slot in range(GU):
                    scatter(trip, slot)

            def gather_layer(seq, rows, slot_rows, used, used_base):
                indices = seq * (1 + TRIPS * QUADS)

                def step(trip, u):
                    quad = u // 2
                    if u % 2 == 0:
                        g.wait_ge(s_idx, indices + 1 if isinstance(trip, int) else indices + 1 + (trip - 1) * QUADS + quad + 1)
                    if not isinstance(trip, int):
                        g.wait_ge(used, used_base + trip * U + u - U + 1)
                    elif seq == 1 and u == U // 2:
                        g.wait_ge(s_proj, sum(NPROJ))
                    g.sem_inc(s_gate)
                    for k in range(2):
                        i = 2 * u + k
                        g.indirect_dma_start(
                            out=slot_rows(i), out_offset=None, in_=rows,
                            in_offset=bass.IndirectOffsetOnAxis(ap=gidx[:, quad, i % Q:i % Q + 1], axis=0)).then_inc(s_g[u], 16)

                run_steps(g, 0, step)

            def divide(l):
                g.wait_ge(event("rden"), l + 1)
                for i in range(0, NWP, DG * WPT):
                    w = slice(i, i + DG * WPT)
                    g.tensor_tensor(acc[:, w, 0:HD], acc[:, w, 0:HD],
                                    rden[:, w].unsqueeze(2).to_broadcast([P, DG * WPT, HD]), ALU.mult).then_inc(event("divided"), 1)

            for l in range(2):
                if l:
                    g.wait_ge(s_tr, NT)
                    g.memset(acc, 0.0).then_inc(event("acc_cleared"), 1)
                g.wait_ge(event("tables"), l + 1)
                if l == 0:
                    for i in range(EO):
                        g.wait_ge(s_eato[i], 16 * 4 * NUC // EO)
                for slot in range(2):
                    g.wait_ge(s_kvo[slot], 16 * ((NT + 1 - slot) // 2) * (l + 1))
                if l:
                    g.wait_ge(s_o, l * PAIRS)
                g.sem_inc(s_gate)
                gather_layer(l, kv_d[l], kv_slot, s_o, l * PAIRS)
                divide(l)

            g.wait_ge(event("normed"), 2 * NB)
            g.wait_ge(s_tr, 2 * NT)
            g.memset(racc, 0.0).then_inc(s_clr, 1)
            g.memset(cnt_t[:, :], 0.0).then_inc(s_clr, 1)
            g.wait_ge(s_clr, 2)
            g.memset(eat, 1.0).then_inc(s_clr, 1)
            g.wait_ge(s_clr, 3)
            for l in range(3):
                if l == 0:
                    g.wait_ge(s_h, 16 * (NT // HG))
                else:
                    for i in range(4):
                        g.wait_ge(s_ho[l - 1][i], 16 * len(range(i, NT, 4)))
                g.wait_ge(s_o, 2 * PAIRS)
                if l:
                    g.wait_ge(s_prod, l * PAIRS)
                g.sem_inc(s_gate)
                gather_layer(2 + l, h_d[l], lambda i: gring_r[:, i, :], s_prod, l * PAIRS)
                if l < 2:
                    for i in range(NT):
                        g.wait_ge(s_dn, l * NT + i + 1)
                        g.memset(racc[:, :, i * P:(i + 1) * P], 0.0).then_inc(s_clr, 1)

        def windows(engine, pair, table, unit):
            w = nc.values_load_multi_w_load_instructions(
                table[0:1, bass.ds(2 * pair, Q)], engines=(engine,), min_val=0, max_val=NW * unit,
                skip_runtime_bounds_check_because="the table counts the windows that end before a tile, of which there are NW")[1]
            return {0: w[0:2], 1: w[2:4]}

        def next_indices(copy, slot, r):
            copy(gidx[:, slot // 2, :], src_i[:, bass.ds((r + 1) * TU + slot // 2 * Q, Q)]).then_inc(s_idx, 1)

        def sync_program(sp):
            for t, n in ((dst_e, "dst"), (typ_e, "edge_type_3"), (src_e, "src")):
                sp.dma_start(t[:, :], a[n].rearrange("(p j) -> p j", p=EP)).then_inc(s_edges, 16)
            sp.wait_ge(event("consts"), 1)
            rec_v = rec_d.rearrange("(p t) r -> p t r", p=P)
            for k in range(NUC):
                sp.dma_start(rec_v[:, k * UC:(k + 1) * UC, :], blank).then_inc(s_blank, 16)

            def weights(slot, k, w, done):
                sp.dma_start(wts[:, slot, k, :, :], w.rearrange("(c p) n -> p c n", p=P)).then_inc(done, 16)

            for l in range(2):
                for k, n in enumerate("qkvs"):
                    weights(l, k, a[f"L0_gnn_w{l + 1}{n}"], s_small)
                for t, n in ((bias_q, "b{}q"), (bias_s, "b{}s"), (gamma, "g{}"), (beta, "be{}")):
                    sp.dma_start(t[:, l, :], a["L0_gnn_" + n.format(l + 1)].rearrange("(c p) -> p c", p=P),
                                 allow_slow_non_contiguous=True).then_inc(s_small, 16)
                for k, n in enumerate("kv"):
                    sp.dma_start(bias_kv[:, l, k, :], a[f"L0_gnn_b{l + 1}{n}"].partition_broadcast(P)).then_inc(s_small, 16)
            for l in range(3):
                sp.dma_start(bias_r[:, l, :], a["L1_gnn_bias"][l, :].partition_broadcast(P)).then_inc(s_small, 16)
            sp.dma_start(nnw[:, :, :], a["L1_gnn_nn_w"].rearrange("(c p) j -> p c j", p=P)).then_inc(s_small, 16)
            sp.dma_start(nnwt[ND:ND + 1, :], a["L1_gnn_nn_b"].rearrange("(o f) -> o f", o=1)).then_inc(s_small, 16)

            def load_rows(i, sem_used, used):
                tail = i == NT - 1
                slot = 2 if tail else i % 2
                if used is not None:
                    sp.wait_ge(sem_used, used)
                n = NTAIL if tail else P
                sp.dma_start(xr[0:n, slot, :], a["x"][i * P:i * P + n, :]).then_inc(s_xr[slot], 16)

            sp.wait_ge(event("cleared"), 1)
            for i in range(NT):
                load_rows(i, s_proj, i - 1 if 2 <= i < NT - 1 else None)
            for l in range(2):
                kv_base = NT if l == 0 else NPROJ[0]
                for i in range(NT):
                    sp.wait_ge(s_pev, kv_base + i + 1)
                    sp.dma_start(kv_d[l][i * P:(i + 1) * P, :], kvrow[:, i % 2, :]).then_inc(s_kvo[i % 2], 16)
                if l == 0:
                    for slot in range(GU):
                        sp.wait_ge(s_scat[slot], 16 * CG * GTRIPS)
                    for k in range(NUC):
                        if k >= 2:
                            sp.wait_ge(s_unv, 3 * (k - 1))
                            sp.wait_ge(s_attrs, k - 1)
                        sp.dma_start(chunk[:, k % 2, :, :], rec_v[:, k * UC:(k + 1) * UC, :]).then_inc(s_chunk[k % 2], 16)
                    sp.wait_ge(event("dlt"), 1)
                    sp.dma_start(dlt_d.rearrange("(q t) p -> t q p", t=P), dlt_out[:, :, :]).then_inc(s_dlt, 16)
                    sp.wait_ge(s_dlt, 16)
                sp.wait_ge(s_pev, sum(NPROJ[:l + 1]))

                pair_w = {}

                def step(trip, u):
                    t = trip * TU + 2 * u
                    if u % 2 == 0:
                        b = u // 2 % 2
                        wait_freed(sp, s_mask, (l * TRIPS + trip) * QUADS + u // 2 - 1)
                        sp.dma_start(dlb[:, b, :], dlt_d[bass.ds(t, Q), :].rearrange("t p -> (t p)")
                                     .partition_broadcast(P)).then_inc(s_dlb[b], 16)
                        pair_w.update(windows(mybir.EngineType.SP, trip * U + u, win_i, 1))
                    wait_freed(sp, s_sc, l * PAIRS + trip * U + u - RL + 1)
                    for k, w in enumerate(pair_w[u % 2]):
                        sp.dma_start(qs[:, 2 * (u % RL) + k, :, :],
                                     qblk[:, bass.ds(w, 1), :, :].rearrange("p o c m -> p (o c) m")).then_inc(s_q[u % RL], 16)

                run_steps(sp, 0, step)
            sp.wait_ge(s_o, 2 * PAIRS)
            for i in range(NT):
                if i >= TU:
                    sp.wait_ge(s_add, ADDS * 2 * NT + i - TU + 1)
                n = NTAIL if i == NT - 1 else P
                sp.dma_start(gring_r[0:n, i % TU, :], a["x"][i * P:i * P + n, :]).then_inc(s_x2[i % TU], 16)
            for l in range(2):
                load_relational(sp, l)
            for i in range(0, NT, HG):
                sp.wait_ge(s_ln, i + HG)
                sp.dma_start(h_d[0][i * P:(i + HG) * P, :].rearrange("(i p) f -> p i f", p=P), x1[:, i:i + HG, :]).then_inc(s_h, 16)
            for l in range(3):
                def step(trip, u):
                    if u % 2:
                        return
                    quad = u // 2
                    wait_freed(sp, s_ew, l * PAIRS + trip * U + u - 2)
                    sp.dma_start(eat[0:ND, quad % 2, :, :],
                                 eat_d[bass.ds(trip, 1), :, quad * P:(quad + 1) * P]
                                 .rearrange("o (q j) e -> (o j) q e", q=Q)).then_inc(s_eat[quad % 2], 16)

                if l == 0:
                    sp.wait_ge(s_clr, 3)
                    for i in range(EO):
                        sp.wait_ge(s_eato[i], 16 * 4 * NUC // EO)
                run_steps(sp, 0, step)
                if l < 2:
                    for i in range(NT):
                        sp.wait_ge(s_dv, STEPD * (l * NT + i + 1))
                        sp.dma_start(h_d[l + 1][i * P:(i + 1) * P, :], orow[:, i % 4, :]).then_inc(s_ho[l][i % 4], 16)
                    if l == 0:
                        load_relational(sp, 2)
            for i in range(0, NT - 1, OG):
                sp.wait_ge(s_ln, NT + i + OG)
                sp.dma_start(out[i * P:(i + OG) * P, :].rearrange("(i p) f -> p i f", p=P), x1[:, i:i + OG, :]).then_inc(s_out, 16)
            sp.wait_ge(s_ln, 2 * NT)
            sp.dma_start(out[(NT - 1) * P:N, :], x1[0:NTAIL, NT - 1, :]).then_inc(s_out, 16)
            sp.wait_ge(s_out, 16 * ((NT - 1) // OG + 1))

        def load_relational(sp, l):
            if l == 0:
                sp.wait_ge(s_proj, sum(NPROJ))
            if l == 2:
                sp.wait_ge(s_dn, NT)
            for r in range(NREL):
                sp.dma_start(wts[:, l % 2, r, :, :], a["L1_gnn_W"][l, r, :, :].rearrange("(c p) n -> p c n", p=P))\
                    .then_inc(s_wr[l], 16)
            sp.dma_start(wts[:, l % 2, NREL, :, :], a["L1_gnn_root"][l, :, :].rearrange("(c p) n -> p c n", p=P))\
                .then_inc(s_wr[l], 16)

        def tensor_program(pe):
            pe.wait_ge(event("consts"), 1)
            cnt = bank[6][:, 0:CG * NW]
            pe.matmul(cnt, ones_b[0:EP, :], zeros_b[:, :], start=True, stop=False)

            def count(trip, slot):
                pe.wait_ge(s_ohw, trip * GU + slot + 1)
                pe.matmul(cnt.rearrange("p (c w) -> p c w", c=CG), ones_b[0:EP, :], onehot_w[:, slot, :, :],
                          start=False, stop=False).then_inc(s_cntw, 1)

            for slot in range(GU):
                count(0, slot)
            with pe.Fori(1, GTRIPS) as trip:
                for slot in range(GU):
                    count(trip, slot)
            pe.matmul(cnt, ones_b[0:EP, :], zeros_b[:, :], start=False, stop=True)\
                .then_inc(event("counted"), 1)
            pe.wait_ge(event("tend"), 1)
            pe.transpose(bank[5][0:NW, 0:P], tend[:, :], ident[:, :]).then_inc(event("tend_c"), 1)
            pe.wait_ge(event("ended"), 1)
            pe.matmul(bank[7][:, 0:T], ones_b[0:NW, :], ended, start=True, stop=True).then_inc(event("tile_w"), 1)
            pe.wait_ge(event("tend_copied"), 1)

            def ranks(trip, slot):
                g = trip * GU + slot
                pe.wait_ge(s_ohw, G + g + 1)
                if not isinstance(trip, int):
                    pe.wait_ge(s_row, ROWSTEPS * (g - GU + 1))
                r = bank[slot][0:EP, 0:CG * NW]
                pe.matmul(r.rearrange("p (c w) -> p c w", c=CG), before[:, :], onehot_w[:, slot, :, :], start=True, stop=False)
                for c in range(CG - 1):
                    left = CG - 1 - c
                    pe.matmul(r[:, (c + 1) * NW:].rearrange("p (c w) -> p c w", w=NW), ones_b[0:EP, 0:EP],
                              onehot_w[:, slot, c:c + 1, :].to_broadcast([EP, left, NW]), start=False, stop=left == 1)
                wait_freed(pe, s_row, ROWSTEPS * (g - 1))
                for c in range(CG):
                    ins = pe.matmul(bank[5 + slot % 3][0:EP, 0:NW], ones_b[0:EP, 0:EP], onehot_w[:, slot, c, :],
                                    start=c == 0, stop=c == CG - 1)
                ins.then_inc(s_rank, 1)

            for slot in range(GU):
                ranks(0, slot)
            with pe.Fori(1, GTRIPS) as trip:
                for slot in range(GU):
                    ranks(trip, slot)
            pe.wait_ge(s_row, ROWSTEPS * G)

            pe.wait_ge(s_small, 16 * 25)
            for c in range(2):
                ins = pe.transpose(bank[7][0:ND, c * P:(c + 1) * P], nnw[:, c, :], ident[:, :])
            ins.then_inc(event("nnw"), 1)

            for l in range(2):
                project(pe, l)
                if l == 0:
                    pe.wait_ge(s_pev, NPROJ[0])
                    for k in range(NUC):
                        pe.wait_ge(s_attrs, k + 1)
                        for b in range(4):
                            if k:
                                pe.wait_ge(s_eatc, 4 * (k - 1) + b + 1)
                            for q in range(4):
                                t = 16 * b + 4 * q
                                ins = pe.transpose(bank[b][:, q * P:(q + 1) * P],
                                                   attrs[:, k % 2, t * ND:(t + 4) * ND], ident[:, :])
                            ins.then_inc(s_unp, 1)
                    pe.wait_ge(s_unv, 3 * NUC)
                    for q in range(T // P):
                        ins = pe.transpose(bank[4][:, q * P:(q + 1) * P], dl_f[:, q * P:(q + 1) * P], ident[:, :])
                    ins.then_inc(event("dl_t"), 1)
                    pe.wait_ge(s_eatc, 4 * NUC)
                    pe.wait_ge(event("dlt"), 1)
                else:
                    pe.wait_ge(s_pev, sum(NPROJ))
                attention_tiles(pe, l)
                for j in range(NT):
                    pe.wait_ge(event("divided"), l * NT // DG + j // DG + 1)
                    if j >= 2:
                        pe.wait_ge(s_add, ADDS * (l * NT + j - 1))
                    for k in range(WPT):
                        ins = pe.transpose(bank[j % 2][0:HD, k * P:(k + 1) * P], acc[:, WPT * j + k, 0:HD], ident[:, :])
                    ins.then_inc(s_tr, 1)

            pe.wait_ge(event("leaky"), 2 * NB)
            pe.wait_ge(s_add, ADDS * 2 * NT)
            for i in range(NT):
                if i >= 2:
                    pe.wait_ge(s_add, ADDS * 2 * NT + i - 1)
                for c in range(2):
                    ins = pe.transpose(bank[i % 2][:, c * P:(c + 1) * P], ht[:, c, i * P:(i + 1) * P], ident[:, :])
                ins.then_inc(s_tr, 1)
            for i in range(NT):
                pe.wait_ge(s_ln, i + 1)
                features(pe, i, x1[:, i, :], i)

            for l in range(3):
                pe.wait_ge(s_ht, NT * (l + 1))
                if l == 0:
                    pe.wait_ge(event("nnwt"), 1)
                    pe.wait_ge(s_clr, 3)
                else:
                    pe.wait_ge(s_dv, STEPD * l * NT)
                relation_tiles(pe, l)
                pe.wait_ge(s_wr[l], 16 * (NREL + 1))
                pe.wait_ge(s_racc, (l + 1) * T)
                if l == 0:
                    pe.wait_ge(s_rc, T)
                    for k in range(WPT):
                        for r in range(NREL):
                            ins = pe.matmul(bank[7][k * W:(k + 1) * W, r * NT:(r + 1) * NT],
                                            ident[0:SEG, r * W:(r + 1) * W], cnt_t[:, k:NWP:WPT], start=True, stop=True)
                    ins.then_inc(event("cnt"), 1)
                for i in range(NT):
                    n = l * NT + i
                    if n >= 2:
                        pe.wait_ge(s_dv, STEPD * (n - 1))
                    b = 2 * (n % 2)
                    for r in range(-1, NREL):
                        o = bank[b + (r + 1) // 2][:, (r + 1) % 2 * D:((r + 1) % 2 + 1) * D]
                        for c in range(2):
                            lhs = ht[:, c, i * P:(i + 1) * P] if r < 0 else \
                                racc[:, c * NREL + r, i * P:(i + 1) * P]
                            ins = pe.matmul(o, lhs, wts[:, l % 2, r if r >= 0 else NREL, c, :], start=c == 0, stop=c == 1)
                    ins.then_inc(s_dn, 1)
                    if l < 2 and i:
                        pe.wait_ge(s_dv, STEPD * n)
                        features(pe, i - 1, orow[:, (i - 1) % 4, :], (l + 1) * NT + i - 1)
                if l < 2:
                    pe.wait_ge(s_dv, STEPD * (l + 1) * NT)
                    features(pe, NT - 1, orow[:, (NT - 1) % 4, :], (l + 1) * NT + NT - 1)

        def features(pe, i, rows, n):
            if n >= 2:
                pe.wait_ge(s_ht, n - 1)
            for c in range(2):
                ins = pe.transpose(bank[4 + n % 2][:, c * P:(c + 1) * P], rows[:, c * P:(c + 1) * P], ident[:, :])
            ins.then_inc(s_htp, 1)

        def project(pe, l):
            job = sum(NPROJ[:l])

            def free(job):
                if job >= 4:
                    pe.wait_ge(s_pev, job - 3)
                return bank[job % 4]

            if l == 0:
                for i in range(NT):
                    slot = 2 if i == NT - 1 else i % 2
                    pe.wait_ge(s_xr[slot], 16 * (1 if slot == 2 else i // 2 + 1))
                    b = free(job)
                    for c in range(2):
                        ins = pe.transpose(b[:, c * P:(c + 1) * P], xr[:, slot, c * P:(c + 1) * P], ident[:, :])
                    ins.then_inc(s_proj, 1)
                    job += 1
                pe.wait_ge(s_pev, NT)
            for i in range(NT):
                if l:
                    pe.wait_ge(event("leaky"), i * P // 512 + 1)
                b = free(job)
                for kc in range(2):
                    ins = pe.matmul(b[:, :].rearrange("p (k n) -> p k n", k=2), ht[:, kc, i * P:(i + 1) * P],
                                    wts[:, l, 1:3, kc, :], start=kc == 0, stop=kc == 1)
                ins.then_inc(s_proj, 1)
                job += 1
            for k in (0, 3):
                for c in range(2):
                    for nb in range(NB):
                        n = min(512, NP - nb * 512)
                        b = free(job)
                        for kc in range(2):
                            ins = pe.matmul(b[:, 0:n], wts[:, l, k, kc, c * P:(c + 1) * P],
                                            ht[:, kc, nb * 512:nb * 512 + n], start=kc == 0, stop=kc == 1)
                        ins.then_inc(s_proj, 1)
                        job += 1

        def attention_tiles(pe, l):
            at = l * PAIRS

            def step(trip, u):
                if live(trip, u, LAG_S):
                    p, slot, r = tile_of(trip, u, LAG_S)
                    pe.wait_ge(s_q[slot % RL], 32 * (2 * (l * TRIPS + r) + slot // RL + 1))
                    pe.wait_ge(s_kt, at + p + 1)
                    wait_freed(pe, s_top, 2 * (at + p - 1))
                    for k in range(2):
                        for c in range(2):
                            ins = pe.matmul(bank[2 + slot % 2][c * 2 * W:(c + 1) * 2 * W, k * P:(k + 1) * P],
                                            qs[:, 2 * (slot % RL) + k, c, :], kt[:, slot % 2, k, c * P:(c + 1) * P],
                                            start=True, stop=True)
                    ins.then_inc(s_sc, 1)
                if live(trip, u, 0):
                    p, slot, r = tile_of(trip, u, 0)
                    pe.wait_ge(s_g[slot], 32 * (l * TRIPS + r + 1))
                    wait_freed(pe, s_kt, at + p - 1)
                    for k in range(2):
                        for c in range(2):
                            ins = pe.transpose(bank[slot % 2][:, (2 * k + c) * P:(2 * k + c + 1) * P],
                                               kv_slot(2 * slot + k)[:, c * P:(c + 1) * P], ident[:, :])
                    ins.then_inc(s_ktp, 1)
                if live(trip, u, LAG_WT):
                    p, slot, r = tile_of(trip, u, LAG_WT)
                    pe.wait_ge(s_e, at + p + 1)
                    wait_freed(pe, s_es, at + p - 1)
                    for k in range(2):
                        ins = pe.transpose(bank[4 + slot % 2][:, k * P:(k + 1) * P], et[:, 2 * (slot % RL) + k, 0:P], ident[:, :])
                    ins.then_inc(s_ep, 1)
                if live(trip, u, LAG_O):
                    p, slot, r = tile_of(trip, u, LAG_O)
                    pe.wait_ge(s_es, at + p + 1)
                    wait_freed(pe, s_acc, 2 * (at + p - 1))
                    for k in range(2):
                        for h in range(HEADS):
                            ins = pe.matmul(bank[6 + slot % 2][h * W:(h + 1) * W, k * VW:(k + 1) * VW],
                                            es[:, slot % 2, k, h * W:(h + 1) * W],
                                            kv_slot(2 * slot + k)[:, D + h * VW:D + (h + 1) * VW], start=True, stop=True)
                    ins.then_inc(s_o, 1)

            run_steps(pe, LAG_O, step)

        def relation_tiles(pe, l):
            at = l * PAIRS

            def step(trip, u):
                if live(trip, u, 0):
                    p, slot, r = tile_of(trip, u, 0)
                    b = slot // 2 % 2
                    if slot % 2 == 0:
                        pe.wait_ge(s_eat[b], 16 * (quads_before(l * TRIPS + r, slot) + 1))
                    wait_freed(pe, s_prod, at + p - RL + 1)
                    for k in range(2):
                        ins = pe.matmul(bank[slot % RL][:, k * D:(k + 1) * D], eat[:, b, 2 * (slot % 2) + k, :], nnwt[:, :],
                                        start=True, stop=True)
                    ins.then_inc(s_ew, 1)
                if live(trip, u, LAG_SUM):
                    p, slot, r = tile_of(trip, u, LAG_SUM)
                    if slot % 2 == 0:
                        pe.wait_ge(s_oh, QUADS * (l * TRIPS + r) + slot // 2 + 1)
                    pe.wait_ge(s_msg, at + p + 1)
                    wait_freed(pe, s_racc, 2 * (at + p - RL + 1))
                    b = bank[RL + slot % RL]
                    for k in range(2):
                        one = oh[:, slot // 2 % 2, 2 * (slot % 2) + k, :]
                        if l == 0:
                            pe.matmul(b[0:SEG, 4 * SEG + k:4 * SEG + k + 1], one, ones_f[:, :], start=True, stop=True)
                        for c in range(2):
                            ins = pe.matmul(b[:, (2 * k + c) * SEG:(2 * k + c + 1) * SEG],
                                            msg[:, slot % 2, (2 * k + c) * P:(2 * k + c + 1) * P], one, start=True, stop=True)
                    ins.then_inc(s_sp, 1)

            run_steps(pe, LAG_SUM, step)

        def scalar_program(act):
            ea_v = a["edge_attr_32"].rearrange("(p j) c -> p j c", p=EP)

            def staging(trip, slot):
                g = trip * GU + slot
                if not isinstance(trip, int):
                    act.wait_ge(s_scat[slot], 16 * CG * trip)
                act.dma_start(stage[:, slot, :, 0:ND], ea_v[:, bass.ds(g * CG, CG), :]).then_inc(s_sea[slot], 16)
                act.wait_ge(s_row, ROWSTEPS * (g + 1))
                act.copy(stage[:, slot, :, ND:REC], meta[:, bass.ds(g * CG, CG), :]).then_inc(s_stage, 1)
                act.copy(stage_row[:, slot, :], row_e[:, bass.ds(g * CG, CG)]).then_inc(s_stage, 1)

            for slot in range(GU):
                staging(0, slot)
            with act.Fori(1, GTRIPS) as trip:
                for slot in range(GU):
                    staging(trip, slot)

            for b in range(4 * NUC):
                act.wait_ge(s_unp, b + 1)
                if b >= EO:
                    act.wait_ge(s_eato[b % EO], 16 * (b // EO))
                act.copy(eat_out[:, b % EO, :], bank[b % 4][:, :]).then_inc(s_eatc, 1)
                act.wait_ge(s_eatc, b + 1)
                act.dma_start(eat_d[b, :, :], eat_out[:, b % EO, :]).then_inc(s_eato[b % EO], 16)

            for l in range(2):
                attention_acts(act, l)
                act.wait_ge(event("var"), l + 1)
                act.activation(bn_t[:, :, 1], bn_t[:, :, 0], ACT.Sqrt).then_inc(event("std"), 1)
                act.wait_ge(event("affine"), l + 1)
                act.wait_ge(s_proj, sum(NPROJ[:l + 1]))
                for nb in range(NB):
                    block = slice(nb * 512, min(NP, (nb + 1) * 512))
                    for c in range(2):
                        ins = act.activation(ht[:, c, block], st[:, c, block], ACT.Identity, bias=bn_t[:, c, 3:4],
                                             scale=bn_t[:, c, 2:3])
                    ins.then_inc(event("normed"), 1)
            act.wait_ge(event("ln_var"), 1)
            act.activation(ln_sd[:, :, 1], ln_sd[:, :, 0], ACT.Sqrt).then_inc(event("ln_std"), 1)

            def copy_features(i, n):
                act.wait_ge(s_htp, n + 1)
                act.copy(ht[:, :, i * P:(i + 1) * P], bank[4 + n % 2][:, 0:2 * P].rearrange("p (c n) -> p c n", c=2))\
                    .then_inc(s_ht, 1)

            for i in range(NT):
                copy_features(i, i)
            for l in range(3):
                def relation_step(trip, u):
                    p, slot, r = tile_of(trip, u, 0)
                    act.wait_ge(s_prod, l * PAIRS + p + 1)
                    wait_freed(act, s_sp, l * PAIRS + p - 1)
                    act.activation(msg[:, slot % 2, :], prod[:, slot % 2, :], ACT.Relu).then_inc(s_msg, 1)

                run_steps(act, 0, relation_step)
                if l < 2:
                    for i in range(NT):
                        copy_features(i, (l + 1) * NT + i)
            act.wait_ge(event("ln_var"), 2)
            act.activation(ln_sd[:, :, 1], ln_sd[:, :, 0], ACT.Sqrt).then_inc(event("ln_std"), 1)

        def attention_acts(act, l):
            at = l * PAIRS

            def step(trip, u):
                if live(trip, u, 0):
                    p, slot, r = tile_of(trip, u, 0)
                    act.wait_ge(s_ktp, at + p + 1)
                    wait_freed(act, s_sc, at + p - 1)
                    act.copy(kt[:, slot % 2, :, :].rearrange("p k m -> p (k m)"), bank[slot % 2][:, :]).then_inc(s_kt, 1)
                if live(trip, u, LAG_S):
                    p, slot, r = tile_of(trip, u, LAG_S)
                    wait_freed(act, s_acc, 2 * (at + p - RL + 1))
                    for k in range(2):
                        act.wait_ge(s_top, 2 * (at + p) + k + 1)
                        ins = act.activation(et[:, 2 * (slot % RL) + k, :], xs[:, 2 * (slot % 2) + k, :], ACT.Exp,
                                             bias=ntop[:, 2 * slot + k:2 * slot + k + 1], scale=-1.0)
                    ins.then_inc(s_e, 1)
                if live(trip, u, LAG_WT):
                    p, slot, r = tile_of(trip, u, LAG_WT)
                    act.wait_ge(s_ep, at + p + 1)
                    wait_freed(act, s_o, at + p - 1)
                    act.copy(es[:, slot % 2, :, :].rearrange("p k m -> p (k m)"), bank[4 + slot % 2][:, 0:2 * P]).then_inc(s_es, 1)

                if live(trip, u, LAG_ACC):
                    p, slot, r = tile_of(trip, u, LAG_ACC)
                    if slot % 2:
                        act.wait_ge(s_o, at + p + 1)
                        next_indices(act.copy, slot, r)

            run_steps(act, LAG_ACC, step)

        def vector_program(v):
            def step(ins):
                return vec_n.inc(ins)

            def after():
                v.wait_ge(s_vec, vec_n.n)

            def tell(name, ins):
                ins.then_inc(event(name), 1)
                told[name] = told.get(name, 0) + 1
                v.wait_ge(event(name), told[name])

            told = {}

            v.wait_ge(s_edges, 48)
            v.wait_ge(event("consts"), 1)
            step(v.tensor_scalar(int_e[:, :], dst_e[:, :], W - 1, None, ALU.bitwise_and))
            step(v.tensor_scalar(part_m[:, :], part_i[:, :], W - 1, None, ALU.bitwise_and))
            step(v.tensor_copy(meta[:, :, 0], src_e[:, :]))
            after()
            step(v.tensor_copy(part_dl[:, :], part_m[:, :]))
            step(v.tensor_copy(meta[:, :, 1], int_e[:, :]))
            after()
            step(v.scalar_tensor_tensor(meta[:, :, 2], typ_e[:, :], float(W), meta[:, :, 1], ALU.mult, ALU.add))
            step(v.tensor_scalar(int_e[:, :], dst_e[:, :], W.bit_length() - 1, None, ALU.logical_shift_right))
            after()
            step(v.tensor_copy(win_f[:, :], int_e[:, :]))
            after()

            def one_hot(trip, slot):
                g = trip * GU + slot
                v.tensor_tensor(onehot_packed[:, slot, :, :],
                                win_f[:, bass.ds(g * CG, CG)].unsqueeze(1).to_broadcast([EP, NW, CG]),
                                iota_w[:, :, :], ALU.is_equal).then_inc(s_ohw, 1)

            def count_step(trip, slot):
                if not isinstance(trip, int):
                    v.wait_ge(s_cntw, trip * GU + slot - GU + 1)
                one_hot(trip, slot)

            for slot in range(GU):
                count_step(0, slot)
            with v.Fori(1, GTRIPS) as trip:
                for slot in range(GU):
                    count_step(trip, slot)

            v.wait_ge(event("counted"), 1)
            step(v.tensor_reduce(cnt_w[:, :], bank[6][:, 0:CG * NW].rearrange("p (c w) -> p w c", c=CG), AX.X, ALU.add))
            after()
            step(v.tensor_scalar(tiles_i[:, :], cnt_w[:, :], float(P - 1), None, ALU.add))
            after()
            step(v.tensor_scalar(tiles_i[:, :], tiles_i[:, :], P.bit_length() - 1, None, ALU.logical_shift_right))
            after()
            step(v.tensor_copy(tiles_f[:, :], tiles_i[:, :]))
            after()
            tell("tend", v.tensor_tensor_scan(tend[:, :], ones_w[:, :], tiles_f[:, :], 0.0, ALU.mult, ALU.add))
            after()
            step(v.tensor_tensor(run_tot[:, :], tend[:, :], tiles_f[:, :], ALU.subtract))
            after()
            step(v.tensor_scalar(run_tot[:, :], run_tot[:, :], float(P), None, ALU.mult))
            v.wait_ge(event("tend_c"), 1)
            tell("tend_copied", v.tensor_copy(tend_c[:, :], bank[5][0:NW, 0:1]))
            after()
            tell("ended", v.tensor_scalar(ended, iota_t, tend_c[:, 0:1], None, ALU.is_ge))
            v.wait_ge(event("tile_w"), 1)
            step(v.tensor_copy(tile_w, bank[7][:, 0:T]))
            after()
            step(v.tensor_copy(win_i[:, :], tile_w[0:1, :]))
            step(v.tensor_scalar(win_v[:, :], tile_w[0:1, :], float(VW), None, ALU.mult))
            step(v.memset(restart[:, 0:1], 1.0))
            step(v.tensor_tensor(restart[:, 1:T], tile_w[:, 1:T], tile_w[:, 0:T - 1], ALU.not_equal))
            after()
            step(v.tensor_scalar(restart[:, :], restart[:, :], RESTART - KEEP, KEEP, ALU.mult, ALU.add))
            after()

            def rows_of(trip, slot):
                g = trip * GU + slot
                n = ROWSTEPS * g
                v.wait_ge(s_rank, g + 1)
                if not isinstance(g, int) or g:
                    v.wait_ge(s_row, n)
                r = bank[slot][0:EP, 0:CG * NW].rearrange("p (c w) -> p c w", c=CG)
                v.tensor_tensor(rank[:, :, :], r, run_tot[0:EP, :].unsqueeze(1).to_broadcast([EP, CG, NW]), ALU.add)\
                    .then_inc(s_row, 1)
                v.wait_ge(s_row, n + 1)
                v.tensor_tensor(rank[:, :, :], rank[:, :, :], onehot_w[:, slot, :, :], ALU.mult).then_inc(s_row, 1)
                v.tensor_tensor(run_tot[0:EP, :], run_tot[0:EP, :], bank[5 + slot % 3][0:EP, 0:NW], ALU.add)\
                    .then_inc(s_row, 1)
                v.wait_ge(s_row, n + 2)
                v.tensor_reduce(pos_f[:, :], rank[:, :, :], AX.X, ALU.add).then_inc(s_row, 1)
                v.wait_ge(s_row, n + 4)
                v.tensor_copy(pos_i[:, :], pos_f[:, :]).then_inc(s_row, 1)
                v.wait_ge(s_row, n + 5)
                v.tensor_scalar(pos_lo[:, :], pos_i[:, :], P - 1, T.bit_length() - 1, ALU.bitwise_and,
                                ALU.logical_shift_left).then_inc(s_row, 1)
                v.tensor_scalar(pos_hi[:, :], pos_i[:, :], P.bit_length() - 1, None, ALU.logical_shift_right).then_inc(s_row, 1)
                v.wait_ge(s_row, n + 7)
                v.tensor_tensor(row_e[:, bass.ds(g * CG, CG)], pos_lo[:, :], pos_hi[:, :], ALU.bitwise_or).then_inc(s_row, 1)

            v.wait_ge(s_cntw, G)
            for slot in range(GU):
                one_hot(0, slot)
            for slot in range(GU):
                rows_of(0, slot)
            with v.Fori(1, GTRIPS) as trip:
                for slot in range(GU):
                    one_hot(trip, slot)
                for slot in range(GU):
                    rows_of(trip, slot)

            v.wait_ge(event("nnw"), 1)
            v.wait_ge(s_small, 16 * 25)
            tell("nnwt", v.tensor_copy(nnwt[0:ND, :], bank[7][0:ND, 0:D]))

            for l in range(2):
                projected(v, tell, l)
                if l == 0:
                    for k in range(NUC):
                        v.wait_ge(s_chunk[k % 2], 16 * (k // 2 + 1))
                        if k >= 2:
                            v.wait_ge(s_unp, 4 * (k - 1))
                        v.tensor_copy(attrs[:, k % 2, :].rearrange("p (t c) -> p t c", c=ND), chunk[:, k % 2, :, 0:ND])\
                            .then_inc(s_attrs, 1)
                        for t, c in ((src_i, C_SRC), (dl_f, C_DL), (seg_f, C_SEG)):
                            v.tensor_copy(t[:, k * UC:(k + 1) * UC], chunk[:, k % 2, :, c]).then_inc(s_unv, 1)
                    v.wait_ge(event("dl_t"), 1)
                    tell("dlt", v.tensor_copy(dlt_out[:, :, :].rearrange("t q p -> t (q p)"), bank[4][:, 0:T]))
                    v.wait_ge(s_unp, 4 * NUC)
                    v.wait_ge(s_unv, 3 * NUC)
                    first_indices(v)
                    v.wait_ge(s_idx, 1)
                    tell("tables", v.memset(ntop[:, :], 0.0))
                    step(v.memset(acc, 0.0))
                    after()
                else:
                    v.wait_ge(event("acc_cleared"), 1)
                attended(v, l)
                v.wait_ge(s_acc, (l + 1) * T)
                step(v.tensor_scalar(rden[:, :], acc[:, :, HD], 1e-30, None, ALU.max))
                after()
                v.reciprocal(rden[:, :], rden[:, :]).then_inc(event("rden"), 1)
                for j in range(NT):
                    v.wait_ge(s_tr, l * NT + j + 1)
                    for k in range(ADDS):
                        o = st[k * HD:(k + 1) * HD, :, j * P:(j + 1) * P].rearrange("p c (w d) -> p c w d", d=W)
                        v.tensor_tensor(o, bank[j % 2][0:HD, :].rearrange("p (w c k d) -> p c k w d", c=2, k=2, d=W)[:, :, k, :, :],
                                        o, ALU.add).then_inc(s_add, 1)
                v.wait_ge(s_add, ADDS * (l + 1) * NT)
                for c in range(2):
                    for nb in range(NB):
                        n = min(512, N - nb * 512)
                        step(v.bn_stats(stats[:, c, nb, :], st[:, c, nb * 512:nb * 512 + n]))
                after()
                for c in range(2):
                    step(v.bn_aggr(mv[:, c, :], stats[:, c, :, :].rearrange("p b s -> p (b s)")))
                after()
                tell("var", v.tensor_scalar(bn_t[:, :, 0], mv[:, :, 1], EPS, None, ALU.add))
                v.wait_ge(event("std"), l + 1)
                step(v.reciprocal(bn_t[:, :, 1], bn_t[:, :, 1]))
                after()
                step(v.tensor_tensor(bn_t[:, :, 2], bn_t[:, :, 1], gamma[:, l, :], ALU.mult))
                after()
                step(v.tensor_tensor(bn_t[:, :, 3], mv[:, :, 0], bn_t[:, :, 2], ALU.mult))
                after()
                tell("affine", v.tensor_tensor(bn_t[:, :, 3], beta[:, l, :], bn_t[:, :, 3], ALU.subtract))
                for nb in range(NB):
                    block = ht[:, :, nb * 512:min(NP, (nb + 1) * 512)]
                    v.wait_ge(event("normed"), l * NB + nb + 1)
                    v.scalar_tensor_tensor(block, block, 0.1, block, ALU.mult, ALU.max).then_inc(event("leaky"), 1)

            stats_of, aggregate_of = {}, {}

            def ln_stats(i):
                stats_of[i] = step(v.bn_stats(ln_st[:, i, :], x1[:, i, :]))

            def ln_aggregate(i):
                v.wait_ge(s_vec, stats_of[i])
                step(v.bn_aggr(ln_mv[:, i, :], ln_st[:, i, :]))

            for i in range(NT):
                v.wait_ge(s_tr, 2 * NT + i + 1)
                v.wait_ge(s_x2[i % TU], 16 * (i // TU + 1))
                v.tensor_tensor(x1[:, i, :], bank[i % 2][:, 0:D], gring_r[:, i % TU, :], ALU.add).then_inc(s_add, 1)
                if i:
                    v.wait_ge(s_add, ADDS * 2 * NT + i)
                    ln_stats(i - 1)
                if i > 1:
                    ln_aggregate(i - 2)
            v.wait_ge(s_add, ADDS * 2 * NT + NT)
            ln_stats(NT - 1)
            for i in (NT - 2, NT - 1):
                ln_aggregate(i)
            layer_norm(v, step, after, tell, 0)

            v.wait_ge(s_clr, 3)
            for l in range(3):
                related(v, l)
                if l == 0:
                    v.wait_ge(event("cnt"), 1)
                    step(v.tensor_scalar(inv_t[:, :, :].rearrange("p r i -> p (r i)"), bank[7][:, 0:NREL * NT], 1.0, None, ALU.max))
                    after()
                    step(v.reciprocal(inv_t[:, :, :], inv_t[:, :, :]))
                    after()
                for i in range(NT):
                    n = l * NT + i
                    b = 2 * (n % 2)
                    v.wait_ge(s_dn, n + 1)
                    if l < 2 and i >= 4:
                        v.wait_ge(s_ho[l][i % 4], 16 * (i // 4))
                        v.wait_ge(s_htp, (l + 1) * NT + i - 3)
                    o = orow[:, i % 4, :]
                    v.tensor_tensor(o, bank[b][:, 0:D], bias_r[:, l, :], ALU.add).then_inc(s_dv, 1)
                    for r in range(NREL):
                        p = bank[b + (r + 1) // 2][:, (r + 1) % 2 * D:((r + 1) % 2 + 1) * D]
                        v.wait_ge(s_dv, STEPD * n + r + 1)
                        v.scalar_tensor_tensor(o, p, inv_t[:, r, i:i + 1], o, ALU.mult, ALU.add).then_inc(s_dv, 1)
                    if l == 2:
                        if i:
                            v.wait_ge(s_vec, residual)
                            ln_stats(i - 1)
                        if i > 1:
                            ln_aggregate(i - 2)
                        v.wait_ge(s_dv, STEPD * (n + 1))
                        residual = step(v.tensor_tensor(x1[:, i, :], x1[:, i, :], o, ALU.add))
            after()
            ln_stats(NT - 1)
            for i in (NT - 2, NT - 1):
                ln_aggregate(i)
            layer_norm(v, step, after, tell, 1)

        def layer_norm(v, step, after, tell, n):
            after()
            tell("ln_var", v.tensor_scalar(ln_sd[:, :, 0], ln_mv[:, :, 1], EPS, None, ALU.add))
            v.wait_ge(event("ln_std"), n + 1)
            step(v.reciprocal(ln_sd[:, :, 1], ln_sd[:, :, 1]))
            after()
            for i in range(NT):
                v.tensor_scalar(x1[:, i, :], x1[:, i, :], ln_mv[:, i, 0:1], ln_sd[:, i, 1:2], ALU.subtract, ALU.mult)\
                    .then_inc(s_ln, 1)

        def projected(v, tell, l):
            job = sum(NPROJ[:l])
            if l == 0:
                v.wait_ge(event("cleared"), 1)
                for i in range(NT):
                    v.wait_ge(s_proj, job + 1)
                    v.tensor_copy(ht[:, :, i * P:(i + 1) * P], bank[job % 4][:, 0:2 * P].rearrange("p (c n) -> p c n", c=2))\
                        .then_inc(s_pev, 1)
                    job += 1
            for i in range(NT):
                v.wait_ge(s_proj, job + 1)
                done = 16 * (l * ((NT + 1 - i % 2) // 2) + i // 2)
                if done:
                    v.wait_ge(s_kvo[i % 2], done)
                vec_n.inc(v.tensor_tensor(kvrow[:, i % 2, 0:D], bank[job % 4][:, 0:D], bias_kv[:, l, 0, :], ALU.add))
                v.wait_ge(s_vec, vec_n.n)
                v.tensor_tensor(kvrow[:, i % 2, D:].rearrange("p (h v) -> p h v", v=VW)[:, :, 0:HD],
                                bank[job % 4][:, D:2 * D].rearrange("p (h v) -> p h v", v=HD),
                                bias_kv[:, l, 1, :].rearrange("p (h v) -> p h v", v=HD), ALU.add).then_inc(s_pev, 1)
                job += 1
            if l:
                first_indices(v)
                v.wait_ge(s_idx, 1 + TRIPS * QUADS + 1)
                tell("tables", v.memset(ntop[:, :], 0.0))
            for c in range(2):
                for nb in range(NB):
                    n = min(512, NP - nb * 512)
                    v.wait_ge(s_proj, job + 1)
                    for k in range(2):
                        ins = v.tensor_scalar(qblk[k * HD:(k + 1) * HD, nb * 512 // W:(nb * 512 + n) // W, c, k * W:(k + 1) * W],
                                              bank[job % 4][k * HD:(k + 1) * HD, 0:n].rearrange("p (w d) -> p w d", d=W),
                                              bias_q[k * HD:(k + 1) * HD, l, c:c + 1], -SCALE, ALU.add, ALU.mult)
                        if k == 0:
                            vec_n.inc(ins)
                    ins.then_inc(s_pev, 1)
                    job += 1
            v.wait_ge(s_vec, vec_n.n)
            for c in range(2):
                for nb in range(NB):
                    n = min(512, NP - nb * 512)
                    v.wait_ge(s_proj, job + 1)
                    v.tensor_scalar(st[:, c, nb * 512:nb * 512 + n], bank[job % 4][:, 0:n], bias_s[:, l, c:c + 1], None, ALU.add)\
                        .then_inc(s_pev, 1)
                    job += 1

        def first_indices(v):
            v.tensor_copy(gidx[:, :, :].rearrange("p q i -> p (q i)"), src_i[:, 0:TU]).then_inc(s_idx, 1)

        def attended(v, l):
            at = l * PAIRS
            pair_w = {}

            def old_top(p, slot, k):
                i = 2 * slot + k
                wait_freed(v, s_top, 2 * (at + p) + k)
                v.tensor_tensor(xs[:, 2 * (slot % 2) + k, P:P + 1], ntop[:, (i - 1) % TU:(i - 1) % TU + 1],
                                restart_t[:, i:i + 1], ALU.max).then_inc(s_old, 1)

            def new_top(p, slot, r, k):
                i = 2 * slot + k
                x = xs[:, 2 * (slot % 2) + k, :]
                if k == 0:
                    if slot % 2 == 0:
                        v.wait_ge(s_mask, QUADS * (l * TRIPS + r) + slot // 2 + 1)
                    v.wait_ge(s_sc, at + p + 1)
                v.wait_ge(s_old, 2 * (at + p) + k + 1)
                v.sem_inc(s_gatev)
                v.tensor_tensor_reduce(x[:, 0:P], bank[2 + slot % 2][:, k * P:(k + 1) * P],
                                       mask[:, slot // 2 % 2, 2 * (slot % 2) + k, :],
                                       1.0, x[:, P:P + 1], ALU.add, ALU.min, ntop[:, i:i + 1]).then_inc(s_top, 1)

            def add_sums(p, slot, k):
                if k == 0:
                    v.wait_ge(s_o, at + p + 1)
                wait_freed(v, s_acc, 2 * (at + p) + k)
                o = acc_flat[:, bass.ds(pair_w[slot % 2][k], VW)]
                v.scalar_tensor_tensor(o, o, et[:, 2 * (slot % RL) + k, P:P + 1],
                                       bank[6 + slot % 2][:, k * VW:(k + 1) * VW], ALU.mult, ALU.add).then_inc(s_acc, 1)

            def step(trip, u):
                scored, summed = live(trip, u, LAG_S), live(trip, u, LAG_ACC)
                ps, slot_s, rs = tile_of(trip, u, LAG_S)
                pa, slot_a, ra = tile_of(trip, u, LAG_ACC)
                if summed and slot_a % 2 == 0:
                    pair_w.update(windows(mybir.EngineType.DVE, pa, win_v, VW))
                if scored:
                    if slot_s == 0:
                        v.tensor_copy(restart_t[:, :], restart[:, bass.ds(rs * TU, TU)]).then_inc(s_rst, 1)
                        v.wait_ge(s_rst, l * TRIPS + rs + 1)
                    wait_freed(v, s_e, at + ps - 1)
                    old_top(ps, slot_s, 0)
                if summed:
                    add_sums(pa, slot_a, 0)
                if scored:
                    new_top(ps, slot_s, rs, 0)
                if summed:
                    add_sums(pa, slot_a, 1)
                if scored:
                    old_top(ps, slot_s, 1)
                if u % 2 == 0 and live(trip, u, 0):
                    b = u // 2 % 2
                    v.wait_ge(s_dlb[b], 16 * (quads_before(l * TRIPS + trip, u) + 1))
                    v.tensor_scalar(mask[:, b, :, :].rearrange("p t e -> p (t e)"), dlb[:, b, :], part_dl[:, 0:1], MASKED,
                                    ALU.not_equal, ALU.mult).then_inc(s_mask, 1)
                if scored:
                    new_top(ps, slot_s, rs, 1)

            run_steps(v, LAG_ACC, step)

        def related(v, l):
            at = l * PAIRS
            pair_w = {}

            def step(trip, u):
                if u % 2 == 0 and live(trip, u, 0):
                    b = u // 2 % 2
                    wait_freed(v, s_sp, at + trip * U + u - 2)
                    v.tensor_tensor(oh[:, b, :, :],
                                    seg_f[:, bass.ds(trip * TU + 2 * u, Q)].unsqueeze(2).to_broadcast([P, Q, SEG]),
                                    iota_seg[:, :].unsqueeze(1).to_broadcast([P, Q, SEG]), ALU.is_equal).then_inc(s_oh, 1)
                if live(trip, u, 0):
                    p, slot, r = tile_of(trip, u, 0)
                    v.wait_ge(s_g[slot], 32 * ((2 + l) * TRIPS + r + 1))
                    v.wait_ge(s_ew, at + p + 1)
                    wait_freed(v, s_msg, at + p - 1)
                    v.tensor_tensor(prod[:, slot % 2, :], bank[slot % RL][:, :],
                                    gring_r[:, 2 * slot:2 * slot + 2, :].rearrange("p k f -> p (k f)"), ALU.mult).then_inc(s_prod, 1)
                    if slot % 2:
                        next_indices(v.tensor_copy, slot, r)
                if live(trip, u, LAG_RACC):
                    p, slot, r = tile_of(trip, u, LAG_RACC)
                    b = bank[RL + slot % RL]
                    v.wait_ge(s_sp, at + p + 1)
                    if slot % 2 == 0:
                        pair_w.update(windows(mybir.EngineType.DVE, p, win_i, 1))
                    for k, w in enumerate(pair_w[slot % 2]):
                        if l == 0:
                            wait_freed(v, s_rc, 2 * (at + p) + k)
                            c = cnt_t[:, bass.ds(w, 1)]
                            v.tensor_tensor(c, c, b[0:SEG, 4 * SEG + k:4 * SEG + k + 1], ALU.add).then_inc(s_rc, 1)
                        wait_freed(v, s_racc, 2 * (at + p) + k)
                        if l and k == 0 and isinstance(trip, int) and p == 0:
                            v.wait_ge(s_clr, 3 + l * NT)
                        o = racc[:, :, bass.ds(w * W, W)]
                        v.tensor_tensor(o, o, b[:, 2 * k * SEG:2 * (k + 1) * SEG].rearrange("p (s d) -> p s d", d=W), ALU.add)\
                            .then_inc(s_racc, 1)

            first_indices(v)
            run_steps(v, LAG_RACC, step)

        block = ctx.enter_context(nc.Block())

        @block.gpsimd
        def _(g):
            gpsimd_program(g)

        @block.sync
        def _(sp):
            sync_program(sp)

        @block.tensor
        def _(pe):
            tensor_program(pe)

        @block.scalar
        def _(act):
            scalar_program(act)

        @block.vector
        def _(v):
            vector_program(v)


def kernel(**inputs):
    import numpy as np
    import concourse.bacc as bacc
    from concourse.bass_utils import run_bass_kernel_spmd

    nc = bacc.Bacc("TRN2", target_bir_lowering=False, num_devices=1)
    arrays, aps = {}, {}
    for name, value in inputs.items():
        array = np.ascontiguousarray(value)
        arrays["in_" + name] = array
        aps[name] = nc.dram_tensor("in_" + name, array.shape, mybir.dt.from_np(array.dtype), kind="ExternalInput").ap()
    out = nc.dram_tensor("out", (N, D), F32, kind="ExternalOutput").ap()
    build(nc, aps, out)
    return run_bass_kernel_spmd(nc, [arrays], core_ids=[0]).results[0]["out"]
```
